# Optimizing a Trainium2 kernel written in Bass

```python
import numpy as np
import jax
import jax.numpy as jnp

def _softmax(x, axis=-1):
    return jax.nn.softmax(x, axis=axis)

def _gelu(x):
    return jax.nn.gelu(x, approximate=True)

def _silu(x):
    return jax.nn.silu(x)

def _sigmoid(x):
    return jax.nn.sigmoid(x)

def _layernorm(x, axis=-1, eps=1e-05):
    m = jnp.mean(x, axis=axis, keepdims=True)
    v = jnp.var(x, axis=axis, keepdims=True)
    return (x - m) / jnp.sqrt(v + eps)

def _scatter_add(tgt, idx, src, axis=0):
    return tgt.at[idx].add(src)

def _segment_sum(src, seg, n):
    return jax.ops.segment_sum(src, seg, n)
kernel_name = 'mk_seq_postln_d1_jaxref_r4_c37fb6'

def setup_inputs(seed: int=0):
    np.random.seed(seed)
    _w = jnp.asarray

    def _L0_attn_setup():
        import jax, jax.numpy as jnp
        import numpy as np
        B, T, D, H, STRIDE, MLP = (2, 512, 256, 16, 8, 1024)
        HD = D // H
        EPS = 1e-05

        def _ln(x, g, b):
            m = x.mean(-1, keepdims=True)
            v = x.var(-1, keepdims=True)
            return (x - m) * jax.lax.rsqrt(v + EPS) * g + b
        key = jax.random.key(seed)
        ks = jax.random.split(key, 6)
        s = lambda k, shape: jax.random.normal(k, shape, jnp.float32) * 0.02
        return {'x': jax.random.normal(ks[0], (B, T, D), jnp.float32), 'w_in': s(ks[1], (3 * D, D)), 'b_in': jnp.zeros((3 * D,), jnp.float32), 'w_out': s(ks[2], (D, D)), 'b_out': jnp.zeros((D,), jnp.float32), 'w1': s(ks[3], (MLP, D)), 'b1': jnp.zeros((MLP,), jnp.float32), 'w2': s(ks[4], (D, MLP)), 'b2': jnp.zeros((D,), jnp.float32), 'ln1_g': jnp.ones((D,), jnp.float32), 'ln1_b': jnp.zeros((D,), jnp.float32), 'ln2_g': jnp.ones((D,), jnp.float32), 'ln2_b': jnp.zeros((D,), jnp.float32)}
    _L0_attn_in = _L0_attn_setup()

    def _L0_ffn_setup():
        import jax, jax.numpy as jnp
        import numpy as np
        B, S, D, F, E, R = (4, 512, 256, 1024, 8, 4)
        key = jax.random.key(seed)
        ks = jax.random.split(key, 8)
        s_in = 1.0 / np.sqrt(D)
        s_ff = 1.0 / np.sqrt(F)
        return {'hidden_states': jax.random.normal(ks[0], (B, S, D), jnp.float32), 'gate_W': jax.random.normal(ks[1], (E, D), jnp.float32) * s_in, 'gate_b': jnp.zeros((E,), jnp.float32), 'wi_W': jax.random.normal(ks[2], (F, D), jnp.float32) * s_in, 'wi_b': jnp.zeros((F,), jnp.float32), 'wo_W': jax.random.normal(ks[3], (D, F), jnp.float32) * s_ff, 'wo_b': jnp.zeros((D,), jnp.float32), 'lora_A': jax.random.normal(ks[4], (E, R, D), jnp.float32) * s_in, 'lora_B': jax.random.normal(ks[5], (E, F, R), jnp.float32) * 0.02}
    _L0_ffn_in = _L0_ffn_setup()
    _d = {'L0_attn_x': _L0_attn_in['x'], 'L0_attn_w_in': _L0_attn_in['w_in'], 'L0_attn_b_in': _L0_attn_in['b_in'], 'L0_attn_w_out': _L0_attn_in['w_out'], 'L0_attn_b_out': _L0_attn_in['b_out'], 'L0_attn_w1': _L0_attn_in['w1'], 'L0_attn_b1': _L0_attn_in['b1'], 'L0_attn_w2': _L0_attn_in['w2'], 'L0_attn_b2': _L0_attn_in['b2'], 'L0_attn_ln1_g': _L0_attn_in['ln1_g'], 'L0_attn_ln1_b': _L0_attn_in['ln1_b'], 'L0_attn_ln2_g': _L0_attn_in['ln2_g'], 'L0_attn_ln2_b': _L0_attn_in['ln2_b'], 'L0_ffn_gate_W': _L0_ffn_in['gate_W'], 'L0_ffn_gate_b': _L0_ffn_in['gate_b'], 'L0_ffn_wi_W': _L0_ffn_in['wi_W'], 'L0_ffn_wi_b': _L0_ffn_in['wi_b'], 'L0_ffn_wo_W': _L0_ffn_in['wo_W'], 'L0_ffn_wo_b': _L0_ffn_in['wo_b'], 'L0_ffn_lora_A': _L0_ffn_in['lora_A'], 'L0_ffn_lora_B': _L0_ffn_in['lora_B']}
    _x0 = _d['L0_attn_x']
    _d['L0_attn_x'] = jax.random.normal(jax.random.fold_in(jax.random.key(seed), 1), (4, 2048, 256), dtype=_x0.dtype)
    del _x0
    return _d

def reference(L0_attn_x, L0_attn_w_in, L0_attn_b_in, L0_attn_w_out, L0_attn_b_out, L0_attn_w1, L0_attn_b1, L0_attn_w2, L0_attn_b2, L0_attn_ln1_g, L0_attn_ln1_b, L0_attn_ln2_g, L0_attn_ln2_b, L0_ffn_gate_W, L0_ffn_gate_b, L0_ffn_wi_W, L0_ffn_wi_b, L0_ffn_wo_W, L0_ffn_wo_b, L0_ffn_lora_A, L0_ffn_lora_B):

    def _L0_attn_ref(x, w_in, b_in, w_out, b_out, w1, b1, w2, b2, ln1_g, ln1_b, ln2_g, ln2_b):
        import jax, jax.numpy as jnp
        import numpy as np
        B, T, D, H, STRIDE, MLP = (2, 512, 256, 16, 8, 1024)
        HD = D // H
        EPS = 1e-05

        def _ln(x, g, b):
            m = x.mean(-1, keepdims=True)
            v = x.var(-1, keepdims=True)
            return (x - m) * jax.lax.rsqrt(v + EPS) * g + b
        Bs, Ts, Ds = x.shape
        xn = _ln(x, ln1_g, ln1_b)
        qkv = xn @ w_in.T + b_in
        q, k, v = jnp.split(qkv, 3, axis=-1)
        to_heads = lambda t: t.reshape(Bs, Ts, H, HD).transpose(0, 2, 1, 3)
        q, k, v = (to_heads(q), to_heads(k), to_heads(v))
        scores = jnp.einsum('bhqd,bhkd->bhqk', q, k) / jnp.sqrt(jnp.float32(HD))
        idx = jnp.arange(Ts)
        allowed = (idx % STRIDE == 0)[:, None] | (idx[:, None] == idx[None, :])
        scores = jnp.where(allowed, scores, -jnp.inf)
        attn = jax.nn.softmax(scores, axis=-1)
        o = jnp.einsum('bhqk,bhkd->bhqd', attn, v)
        o = o.transpose(0, 2, 1, 3).reshape(Bs, Ts, Ds)
        o = o @ w_out.T + b_out
        x = x + o
        xn = _ln(x, ln2_g, ln2_b)
        h = jax.nn.gelu(xn @ w1.T + b1, approximate=False)
        x = x + (h @ w2.T + b2)
        return x

    def _L0_ffn_ref(hidden_states, gate_W, gate_b, wi_W, wi_b, wo_W, wo_b, lora_A, lora_B):
        import jax, jax.numpy as jnp
        import numpy as np
        B, S, D, F, E, R = (4, 512, 256, 1024, 8, 4)
        x = hidden_states
        logits = jnp.einsum('bsd,ed->bse', x, gate_W) + gate_b
        top1 = jnp.argmax(jax.nn.softmax(logits, axis=-1), axis=-1)
        base = jnp.einsum('bsd,fd->bsf', x, wi_W) + wi_b
        out = jnp.zeros_like(x)
        for i in range(lora_A.shape[0]):
            lora = jnp.einsum('bsr,fr->bsf', jnp.einsum('bsd,rd->bsr', x, lora_A[i]), lora_B[i])
            inter = jax.nn.relu(base + lora)
            expert_out = jnp.einsum('bsf,df->bsd', inter, wo_W) + wo_b
            mask = (top1 == i).astype(x.dtype)[..., None]
            out = out + mask * expert_out
        return out
    x = L0_attn_x
    x = _layernorm(x + _L0_attn_ref(x, L0_attn_w_in, L0_attn_b_in, L0_attn_w_out, L0_attn_b_out, L0_attn_w1, L0_attn_b1, L0_attn_w2, L0_attn_b2, L0_attn_ln1_g, L0_attn_ln1_b, L0_attn_ln2_g, L0_attn_ln2_b), axis=-1)
    x = _layernorm(x + _L0_ffn_ref(x, L0_ffn_gate_W, L0_ffn_gate_b, L0_ffn_wi_W, L0_ffn_wi_b, L0_ffn_wo_W, L0_ffn_wo_b, L0_ffn_lora_A, L0_ffn_lora_B), axis=-1)
    return x

_drawn_inputs = setup_inputs


def setup_inputs(seed=0):
    import zlib

    import numpy as np

    out = dict(_drawn_inputs(seed))
    spreads = {'L0_attn_b_in': (0.0, 0.531),
     'L0_attn_b_out': (0.0, 0.1),
     'L0_attn_b1': (0.0, 0.468),
     'L0_attn_b2': (0.0, 0.1),
     'L0_attn_ln1_g': (1.0, 0.6),
     'L0_attn_ln1_b': (0.0, 0.8),
     'L0_attn_ln2_g': (1.0, 0.6),
     'L0_attn_ln2_b': (0.0, 0.8),
     'L0_ffn_gate_b': (0.0, 0.8),
     'L0_ffn_wi_b': (0.0, 0.1),
     'L0_ffn_wo_b': (0.0, 0.1)}
    factors = {'L0_ffn_gate_W': 2.695}
    for name, (base, spread) in spreads.items():
        noise = np.random.default_rng([zlib.crc32(name.encode()), seed]).standard_normal(out[name].shape)
        drawn = base * np.exp(spread * noise) if base else spread * noise
        out[name] = jnp.asarray(drawn.astype(out[name].dtype))
    for name, factor in factors.items():
        out[name] = (out[name] * factor).astype(out[name].dtype)
    return out
```

```python
from contextlib import ExitStack

import concourse.bass as bass
from concourse import mybir

F32 = mybir.dt.float32
F32R = mybir.dt.float32r
ALU = mybir.AluOpType
ACT = mybir.ActivationFunctionType
AX = mybir.AxisListType

P = 128
B, T, D = 4, 2048, 256
H, HD = 16, 16
STRIDE = 8
F = 1024
E, R = 8, 4
EPS = 1e-5

NT = T // P
KT = D // P
FT = F // P
CT = 4
NC = NT // CT
CW = CT * P
GLOBAL = [j for j in range(NT) if j % STRIDE == 0]
NQ = len(GLOBAL)
QW = NQ * P
PAIRS = H // 2
PR = 2 * HD
GROUPS = 4
GP = PAIRS // GROUPS
VW = HD + 1
SROWS = 3 * PR
MROWS = SROWS + 2
UNITS = GP * 2 * NQ
KQ = T // 512
NMAX = UNITS * KQ
STEPS = GROUPS * NT
LEAD = NMAX + NMAX // 4
ER = E * R
UROWS = 3 * ER + 2
GW = 2 * (E + ER)
ITEMS = 2 * NC * FT
LAG = 2
RING = 3

ORDER = [1, 3, 0, 2]
BLOCKS = [("M", 0), ("M", 1), ("F", 0), ("M", 2), ("F", 1), ("M", 3), ("F", 2), ("F", 3)]
BEFORE = {
    -1: [("ln2a", 0), ("ln2b", 0), ("t2", 0)],
    0: [("ln2a", 1)], 1: [("ln2b", 1)], 3: [("t2", 1)],
    10: [("sumy", 0), ("ln3a", 0)], 11: [("ln3b", 0)], 13: [("t3", 0)], 14: [("gate", 0), ("ln2a", 2)],
    16: [("pick", 0)], 17: [("ln2b", 2)],
    18: [("sumy", 1), ("ln3a", 1)], 19: [("ln3b", 1), ("t2", 2)],
    26: [("sumz", 0), ("ln4a", 0), ("t3", 1)], 27: [("ln4b", 0), ("gate", 1)], 28: [("ln2a", 3)],
    29: [("pick", 1), ("ln2b", 3)],
    34: [("sumy", 2), ("ln3a", 2)], 35: [("ln3b", 2), ("t2", 3)],
    42: [("sumz", 1), ("ln4a", 1), ("t3", 2)], 43: [("ln4b", 1), ("gate", 2)], 45: [("pick", 2)],
    50: [("sumy", 3), ("ln3a", 3)], 51: [("ln3b", 3)], 53: [("t3", 3)], 54: [("gate", 3)],
    56: [("pick", 3)], 58: [("sumz", 2), ("ln4a", 2)], 59: [("ln4b", 2)],
    66: [("sumz", 3), ("ln4a", 3), ("ln4b", 3)],
}


def ffn_steps():
    steps = list(BEFORE[-1])
    for i in range(ITEMS + LAG + 1):
        steps += BEFORE.get(i, [])
        if i < ITEMS:
            steps.append(("up", i))
        if LAG <= i < ITEMS + LAG:
            steps.append(("down", i - LAG))
    return steps


FFN_STEPS = ffn_steps()
LN = {("ln1", c): c for c in range(NC)}
for _what, _n in FFN_STEPS:
    if _what in ("ln2a", "ln3a", "ln4a"):
        LN[(_what[:3], _n)] = len(LN)
NLN = len(LN)
SPARE = {s: k for k, s in enumerate(s for s in FFN_STEPS if s[0] in ("t2", "t3", "gate", "pick"))}
TURNS = {s: k for k, s in enumerate(s for s in FFN_STEPS if s[0] in ("t2", "t3"))}
GELU = {8 * k + f: 8 * sum(w == "M" for w, _ in BLOCKS[:k]) + f
        for k, (w, _) in enumerate(BLOCKS) for f in range(FT) if w == "M"}
RELU = {8 * k + f: 8 * sum(w == "F" for w, _ in BLOCKS[:k]) + f
        for k, (w, _) in enumerate(BLOCKS) for f in range(FT) if w == "F"}
BLOCK_OF = {s: k for k, s in enumerate(BLOCKS)}


def attention_ffn_kernel(nc, x, w_in, b_in, w_out, b_out, w1, b1, w2, b2, ln1_g, ln1_b, ln2_g, ln2_b,
                         gate_W, gate_b, wi_W, wi_b, wo_W, wo_b, lora_A, lora_B, out):
    nc.disable_value_cache = True
    ctx = ExitStack()
    with ctx:
        top = [nc.sbuf_base]

        def place(name, shape, dt, at=None):
            size = 4
            for n in shape[1:]:
                size *= n
            size = -(-size // 32) * 32
            if at is None:
                at = -(-top[0] // 32) * 32
                top[0] = at + size
            return nc.alloc_sbuf_tensor_at(name, shape, dt, offset=at), at + size

        def keep(name, shape, dt=F32):
            return place(name, shape, dt)[0]

        def sem(name):
            return ctx.enter_context(nc.semaphore(name))

        wa = [keep(f"wa{s}", [P, KT, 4 * D], F32R) for s in "hl"]
        wo = [keep(f"wo{s}", [P, KT, D], F32R) for s in "hl"]
        wup = {"M": [keep(f"w1{s}", [P, KT, F], F32R) for s in "hl"],
               "F": [keep(f"wi{s}", [P, KT, F], F32R) for s in "hl"]}
        wdn = {"M": [keep(f"w2{s}", [P, FT, D], F32R) for s in "hl"],
               "F": [keep(f"wf{s}", [P, FT, D], F32R) for s in "hl"]}
        bst = keep("bst", [UROWS, F], F32R)
        ga = keep("ga", [P, KT, 256], F32R)
        ident = keep("ident", [P, P])
        crow = keep("crow", [P, D])
        gateb = keep("gateb", [P, E])
        rank = keep("rank", [P, E])
        cols = keep("cols", [P, 64])
        vals = keep("vals", [P, NT * H * VW + P])
        stats = keep("stats", [P, CT, 6])
        mv = keep("mv", [P, CT, 2])
        vare = keep("vare", [P, CT])
        rstd = keep("rstd", [P, CT])
        mhalf = keep("mhalf", [P, CT])
        mx = keep("mx", [P, 2, NMAX])
        negm = keep("negm", [P, UNITS])
        negs = keep("negs", [P, 2 * UNITS])
        mT = keep("mT", [2 * UNITS, P])
        rsum = keep("rsum", [P, NQ, 4])
        xg = keep("xg", [P, NQ, D])
        xn, _ = place("xn", [P, CT, D], F32, xn_at := -(-top[0] // 32) * 32)
        top[0] = xn_at + 4 * CT * D
        qf, _ = place("qf", [P, 2, QW], F32, xn_at)
        oraw, o_at = place("oraw", [P, QW], F32, xn_at)
        otok, _ = place("otok", [P, NQ, D], F32, o_at)
        qat = top[0]
        xin = [place(f"xin{i}", [P, CT, D], F32, qat + 4096 * i)[0] for i in range(2)]
        xt = [place(f"xt{s}", [P, KT, CW], F32R, qat + 8192 + 4096 * i)[0] for i, s in enumerate("hl")]
        xgt = [place(f"xgt{s}", [P, KT, QW], F32R, qat + 16384 + 2048 * i)[0] for i, s in enumerate("hl")]
        ks = [place(f"ks{s}", [P, CW], F32R, qat + 20480 + 2048 * i)[0] for i, s in enumerate("hl")]
        qstack, _ = place("qstack", [MROWS, PAIRS, 2, QW], F32R, qat)
        prob = [place(f"prob{i}", [P, 2 * GP, QW], F32, qat + 16384 + 4096 * i)[0] for i in range(2)]
        ot = [place(f"ot{s}", [P, KT, QW], F32R, qat + 16384 + 2048 * i)[0] for i, s in enumerate("hl")]
        kat = qat + 24576
        kstack, end = place("kstack", [MROWS, PAIRS, T], F32R, kat)
        assert end <= nc.sbuf_usable_end, (end, nc.sbuf_usable_end)
        at = [kat]

        def ffn(name, shape, dt=F32):
            t, at[0] = place(name, shape, dt, at[0])
            assert at[0] <= end, (name, at[0], end)
            return t

        xrow = [ffn(f"xrow{i}", [P, CT, D]) for i in range(2)]
        x1in = ffn("x1in", [P, CT, D])
        xn2 = ffn("xn2", [P, CT, D])
        srow = [ffn(f"srow{i}", [P, CT, D]) for i in range(2)]
        turned = [[ffn(f"turned{i}{s}", [P, KT, CW], F32R) for s in "hl"] for i in range(2)]
        gel = [ffn(f"gel{i}", [P, CW]) for i in range(2)]
        hid = [[ffn(f"hid{i}{s}", [P, CW], F32R) for s in "hl"] for i in range(RING)]
        ust = ffn("ust", [UROWS, CW], F32R)
        us = ffn("us", [P, CT, UROWS])
        gcopy = ffn("gcopy", [P, CT, GW])
        uall = ffn("uall", [P, CT, E + ER])
        pickm = ffn("pickm", [P, CT])
        picke = ffn("picke", [P, CT, E])
        rows2 = ffn("rows2", [P, 2, D])
        at[0] = kat
        nwin = ffn("nwin", [P, 6, D])
        nwout = ffn("nwout", [P, KT, D])
        nw1 = ffn("nw1", [P, FT, D])
        nw2 = ffn("nw2", [P, KT, F])
        nwi = ffn("nwi", [P, FT, D])
        nwo = ffn("nwo", [P, KT, F])
        nga = ffn("nga", [E + ER, D])
        nlb = ffn("nlb", [P, FT, E, R])
        lbs = ffn("lbs", [P, FT, UROWS])
        wibc = ffn("wibc", [P, FT])
        lnb = ffn("lnb", [P, 2, D])
        junk = ffn("junk", [P, D])
        wof = ffn("wof", [P, KT, D])
        cvb = ffn("cvb", [P, KT, P])
        boutr = ffn("boutr", [P, D])

        ps = ctx.enter_context(nc.psum_tensor("ps", [P, 8, 512], F32))
        scratch = nc.dram_tensor("x1_scratch", [B, T, D], F32, kind="Internal").ap()

        G1, G2, BIN, BINS, B1C, B1S, MASK, QB, LNW = 0, 2, 4, 10, 16, 24, 32, 34, 40

        wload = [sem(f"wload{i}") for i in range(14)]
        p_const, p_ident = sem("p_const"), sem("p_ident")
        d_setup, a_setup, pe_setup = sem("d_setup"), sem("a_setup"), sem("pe_setup")
        xld = [sem(f"xld{i}") for i in range(2)]
        x1st = [sem(f"x1st{i}") for i in range(2)]
        x1gst = sem("x1gst")
        kcp = [sem(f"kcp{i}") for i in range(KT)]
        qcp = [sem(f"qcp{i}") for i in range(KT)]
        mcp = sem("mcp")
        fld = [sem(f"fld{i}") for i in range(2)]
        rld = sem("rld")
        ost = [sem(f"ost{i}") for i in range(2)]
        stat_done, aggr_done = sem("stat_done"), sem("aggr_done")
        vare_done, rstd_done, norm_done = sem("vare_done"), sem("rstd_done"), sem("norm_done")
        ones_done = sem("ones_done")
        xc_done = sem("xc_done")
        ta_done, tah_done, tal_done = sem("ta_done"), sem("tah_done"), sem("tal_done")
        kmm_done, kh_done, kl_done = sem("kmm_done"), sem("kh_done"), sem("kl_done")
        vmm_done, vcp_done, x1_done = sem("vmm_done"), sem("vcp_done"), sem("x1_done")
        qmm_done, qf_done, qh_done, ql_done = sem("qmm_done"), sem("qf_done"), sem("qh_done"), sem("ql_done")
        maxmm_done, maxr_done, negm_done, negs_done = (
            sem("maxmm_done"), sem("maxr_done"), sem("negm_done"), sem("negs_done"))
        mturn_done, mt_done = sem("mturn_done"), sem("mt_done")
        score_done, exp_done, av_done = sem("score_done"), sem("exp_done"), sem("av_done")
        oraw_done, oturn_done, rsum_done, otok_done = (
            sem("oraw_done"), sem("oturn_done"), sem("rsum_done"), sem("otok_done"))
        ott_done, oth_done, otl_done, oproj_done, x1g_done = (
            sem("ott_done"), sem("oth_done"), sem("otl_done"), sem("oproj_done"), sem("x1g_done"))
        res_done, resb_done, x3w_done = sem("res_done"), sem("resb_done"), sem("x3w_done")
        turn_done, turnh_done, turnl_done = sem("turn_done"), sem("turnh_done"), sem("turnl_done")
        up_done, down_done = sem("up_done"), sem("down_done")
        gelu_done, gh_done, gl_done = sem("gelu_done"), sem("gh_done"), sem("gl_done")
        rh_done, rl_done = sem("rh_done"), sem("rl_done")
        sumy_done, sumz_done = sem("sumy_done"), sem("sumz_done")
        gate_done, gatec_done, pick_done = sem("gate_done"), sem("gatec_done"), sem("pick_done")
        pickt_done, ust_done = sem("pickt_done"), sem("ust_done")

        x_v = x.rearrange("b (p j) d -> b p j d", j=NT)
        o_v = out.rearrange("b (p j) d -> b p j d", j=NT)
        s_v = scratch.rearrange("b (p j) d -> b p j d", j=NT)

        block = ctx.enter_context(nc.Block())

        LOCAL = [[j for j in range(CT * c, CT * c + CT) if j not in GLOBAL] for c in range(NC)]
        LOCALS = [sum(len(LOCAL[k]) for k in range(c + 1)) for c in range(NC)]
        NL = LOCALS[-1]

        def setup_groups():
            g = [("wout", 0)]
            g += [("qk", k) for k in range(KT)] + [("vo", k) for k in range(KT)] + [("crow", 0)]
            for w in ("M", "F"):
                g += [("up" + w, i) for i in range(4)] + [("dn" + w, i) for i in range(4)]
            g += [("ga", 0), ("bst", 0), ("bst", 1)]
            return g

        SG = setup_groups()

        def rows_bc(v):
            return v.rearrange("(a d) -> a d", a=1).to_broadcast([P, v.shape[0]])

        @block.sync
        def _(sp):
            sp.dma_start(nwin[:], w_in.rearrange("(m p) d -> p m d", p=P)).then_inc(wload[0], 16)
            sp.dma_start(nwout[:], w_out.rearrange("(m p) d -> p m d", p=P)).then_inc(wload[1], 16)
            sp.dma_start(lnb[:, 0, :], rows_bc(ln1_b)).then_inc(wload[2], 16)
            sp.dma_start(lnb[:, 1, :], rows_bc(ln2_b)).then_inc(wload[2], 16)
            sp.dma_start(boutr[:], rows_bc(b_out)).then_inc(wload[2], 16)
            sp.dma_start(gateb[:], rows_bc(gate_b)).then_inc(wload[2], 16)
            with nc.allow_non_contiguous_dma(reason="vectors turned into columns, once"):
                for t, v, n in ((G1, ln1_g, KT), (G2, ln2_g, KT), (BIN, b_in, 6), (B1C, b1, FT)):
                    sp.dma_start(cols[:, t:t + n], v.rearrange("(m p) -> p m", p=P)).then_inc(wload[3], 16)
                sp.dma_start(wibc[:], wi_b.rearrange("(m p) -> p m", p=P)).then_inc(wload[3], 16)
            sp.dma_start(nw1[:], w1.rearrange("(m p) d -> p m d", p=P)).then_inc(wload[4], 16)
            sp.dma_start(nw2[:], w2.rearrange("(m p) f -> p m f", p=P)).then_inc(wload[5], 16)
            sp.dma_start(nwi[:], wi_W.rearrange("(m p) d -> p m d", p=P)).then_inc(wload[6], 16)
            sp.dma_start(nwo[:], wo_W.rearrange("(m p) f -> p m f", p=P)).then_inc(wload[7], 16)
            sp.dma_start(nga[0:E], gate_W).then_inc(wload[8], 16)
            sp.dma_start(nga[E:E + ER], lora_A.rearrange("e r d -> (e r) d")).then_inc(wload[8], 16)
            for e in range(E):
                sp.dma_start(nlb[:, :, e, :], lora_B[e].rearrange("(m p) r -> p m r", p=P)).then_inc(wload[9], 16)

            for s in [*xld, *x1st, x1gst, *kcp, *qcp, mcp, *fld, rld, *ost]:
                sp.sem_inc(s, 1)
            with sp.Fori(2, B + 2) as turn:
                b = turn - 2

                def load_x(c):
                    if c < 2:
                        sp.wait_ge(score_done, 1 + b * STEPS)
                        sp.wait_ge(x1st[c], 1 + b * 32)
                    else:
                        sp.wait_ge(x1st[c % 2], 1 + b * 32 + 16)
                    if c == 2:
                        sp.wait_ge(xc_done, 1 + b * NC + 1)
                    sp.dma_start(xin[c % 2][:], x_v[b, :, CT * c:CT * c + CT, :]).then_inc(xld[c % 2], 16)

                load_x(0)
                load_x(1)
                for c in range(NC):
                    for m in range(KT):
                        n = KT * c + m
                        sp.wait_ge(kh_done, 1 + b * NC * KT + n + 1)
                        sp.wait_ge(kl_done, 1 + b * NC * KT + n + 1)
                        if n == 0:
                            for i in range(2):
                                sp.wait_ge(ost[i], 1 + b * 32)
                            sp.wait_ge(ust_done, 1 + b * NC)
                            sp.wait_ge(pe_setup, len(SG))
                            sp.wait_ge(d_setup, D_SETUP)
                            sp.wait_ge(a_setup, A_SETUP)
                        for i in range(4):
                            for blk, part in ((0, 0), (1, 1), (2, 0)):
                                sp.dma_start(
                                    kstack[PR * blk:PR * (blk + 1), 4 * m + i, CW * c:CW * (c + 1)].bitcast(F32),
                                    ks[part][PR * i:PR * (i + 1), :].bitcast(F32)).then_inc(kcp[m], 16)
                    sp.wait_ge(x1_done, 1 + b * NL + LOCALS[c])
                    i0, n = LOCAL[c][0] - CT * c, len(LOCAL[c])
                    sp.dma_start(s_v[b, :, LOCAL[c][0]:LOCAL[c][0] + n, :],
                                 xin[c % 2][:, i0:i0 + n, :]).then_inc(x1st[c % 2], 16)
                    if c + 2 < NC:
                        load_x(c + 2)
                for i in range(2):
                    sp.wait_ge(x1st[i], 1 + b * 32 + 32)
                sp.wait_ge(vmm_done, 1 + b * NT + NT)
                for m in range(KT):
                    sp.wait_ge(qh_done, 1 + b * KT + m + 1)
                    sp.wait_ge(ql_done, 1 + b * KT + m + 1)
                    for i in range(4):
                        for blk, part in ((0, 0), (1, 0), (2, 1)):
                            sp.dma_start(
                                qstack[PR * blk:PR * (blk + 1), 4 * m + i, :, :].rearrange(
                                    "p e q -> p (e q)").bitcast(F32),
                                ks[part][PR * i:PR * (i + 1), :].bitcast(F32)).then_inc(qcp[m], 16)
                for g in range(GROUPS):
                    sp.wait_ge(mt_done, 1 + b * GROUPS + g + 1)
                    for h in range(2):
                        sp.dma_start(
                            qstack[SROWS + h:SROWS + h + 1, GP * g:GP * (g + 1), :, :].rearrange(
                                "p a e q -> p (a e q)").rearrange("p (u q) -> p u q", q=P).bitcast(F32),
                            mT[UNITS * h:UNITS * (h + 1), :]).then_inc(mcp, 16)
                sp.wait_ge(x1g_done, 1 + b * NQ + NQ)
                for i, j in enumerate(GLOBAL):
                    sp.dma_start(s_v[b, :, j, :], xg[:, i, :]).then_inc(x1gst, 16)

                sp.wait_ge(score_done, 1 + b * STEPS + STEPS)
                sp.dma_start(rows2[:, 0, :], rows_bc(b2)).then_inc(rld, 16)
                sp.dma_start(rows2[:, 1, :], rows_bc(wo_b)).then_inc(rld, 16)
                for n in range(NC):
                    c = ORDER[n]
                    if n >= 2:
                        sp.wait_ge(sumy_done, 1 + b * 2 * NC + 2 * (n - 1))
                    if n >= 1:
                        sp.wait_ge(norm_done, 1 + b * NLN * CT + CT * (LN[("ln2", n - 1)] + 1))
                        sp.wait_ge(res_done, 1 + b * NC + n)
                    if n == 2:
                        sp.wait_ge(x1gst, 1 + b * 32 + 32)
                    sp.dma_start(xrow[n % 2][:], x_v[b, :, CT * c:CT * c + CT, :]).then_inc(fld[n % 2], 16)
                    sp.dma_start(x1in[:], s_v[b, :, CT * c:CT * c + CT, :]).then_inc(fld[n % 2], 16)
                for n in range(NC):
                    c = ORDER[n]
                    sp.wait_ge(norm_done, 1 + b * NLN * CT + CT * (LN[("ln4", n)] + 1))
                    sp.dma_start(o_v[b, :, CT * c:CT * c + CT, :], srow[n % 2][:]).then_inc(ost[n % 2], 16)
            for i in range(2):
                sp.wait_ge(ost[i], 1 + B * 32)
                sp.wait_ge(x1st[i], 1 + B * 32)
            sp.wait_ge(x1gst, 1 + B * 32)

        @block.gpsimd
        def _(pool):
            nc.gpsimd.memset(ident[:], 0.0).then_inc(p_ident, 1)
            nc.gpsimd.memset(vals[:], 1.0).then_inc(p_const, 1)
            nc.gpsimd.memset(mhalf[:], -0.5).then_inc(p_const, 1)
            nc.gpsimd.memset(ga[:].bitcast(F32), 0.0).then_inc(p_const, 1)
            for e in range(E):
                nc.gpsimd.memset(rank[:, e:e + 1], float(E - e)).then_inc(p_const, 1)
            pool.wait_ge(p_ident, 1)
            nc.gpsimd.affine_select(out=ident[:], in_=ident[:], compare_op=ALU.not_equal, fill=1.0, base=0,
                                    pattern=[[-1, P]], channel_multiplier=1).then_inc(p_ident, 1)
            pool.wait_ge(d_setup, D_SETUP)

            written = nc.alloc_register(pool.engine)
            nc.gpsimd.reg_mov(written, 1)
            for s in [rstd_done, ones_done, xc_done, res_done, resb_done, x3w_done, gl_done]:
                pool.sem_inc(s, 1)
            with pool.Fori(0, B) as b:
                def rsqrt(k):
                    pool.wait_ge(vare_done, 1 + b * NLN + k + 1)
                    nc.gpsimd.tensor_tensor(rstd[:], vare[:], mhalf[:], ALU.pow).then_inc(rstd_done, 1)

                for c in range(NC):
                    rsqrt(LN[("ln1", c)])
                    if c == 0:
                        for i in range(2):
                            pool.wait_ge(ost[i], 1 + b * 32)
                        pool.wait_ge(ust_done, 1 + b * NC)
                        pool.wait_ge(pe_setup, len(SG))
                        pool.wait_ge(a_setup, A_SETUP)
                        pool.wait_ge(rstd_done, 1 + b * NLN + 1)
                        nc.gpsimd.reg_add(written, written, 1)
                        nc.gpsimd.memset(kstack[SROWS:MROWS, :, :].bitcast(F32), 1.0).then_inc(ones_done, 1)
                        pool.wait_ge(ones_done, pool.snap(written, min_val=2))
                        pool.wait_ge(x1gst, 1 + b * 32)
                    pool.wait_ge(norm_done, 1 + b * NLN * CT + CT * (c + 1))
                    i0, n = LOCAL[c][0] - CT * c, len(LOCAL[c])
                    rows = xin[c % 2][:, i0:i0 + n, :]
                    if i0:
                        nc.gpsimd.tensor_tensor(xg[:, c // 2, :], xin[c % 2][:, 0, :], crow[:], ALU.add)
                    nc.gpsimd.tensor_tensor(rows, rows, crow[:, None, :].to_broadcast([P, n, D]),
                                            ALU.add).then_inc(xc_done, 1)

                for what, n in FFN_STEPS:
                    if what in ("ln2a", "ln3a", "ln4a"):
                        rsqrt(LN[(what[:3], n)])
                    if what == "ln2b":
                        pool.wait_ge(fld[n % 2], 1 + b * 64 + 32 * (n // 2 + 1))
                        nc.gpsimd.tensor_tensor(xrow[n % 2][:], xrow[n % 2][:], x1in[:], ALU.add).then_inc(res_done, 1)
                        pool.wait_ge(res_done, 1 + b * NC + n + 1)
                        pool.wait_ge(rld, 1 + b * 32 + 32)
                        nc.gpsimd.tensor_tensor(xrow[n % 2][:], xrow[n % 2][:],
                                                rows2[:, 0:1, :].to_broadcast([P, CT, D]), ALU.add).then_inc(resb_done, 1)
                    if what == "t3":
                        pool.wait_ge(turn_done, 1 + b * 2 * NC + TURNS[(what, n)] + 1)
                        nc.gpsimd.tensor_tensor(srow[n % 2][:], srow[n % 2][:],
                                                rows2[:, 1:2, :].to_broadcast([P, CT, D]), ALU.add).then_inc(x3w_done, 1)
                    if what == "up" and n in GELU:
                        k = GELU[n]
                        pool.wait_ge(gh_done, 1 + b * NC * FT + k + 1)
                        nc.gpsimd.tensor_tensor(hid[n % RING][1][:], gel[k % 2][:], hid[n % RING][0][:],
                                                ALU.subtract).then_inc(gl_done, 1)

        @block.scalar
        def _(act):
            for k, (what, i) in enumerate(SG):
                act.wait_ge(pe_setup, k + 1)
                bank = ps[:, k % 8, :]
                if what == "wout":
                    nc.scalar.activation(wof[:].rearrange("p k d -> p (k d)"), bank, ACT.Copy).then_inc(a_setup, 1)
                    act.wait_ge(a_setup, 1)
                    nc.scalar.activation(wo[0][:].rearrange("p k d -> p (k d)"), bank, ACT.Copy).then_inc(a_setup, 1)
                elif what == "qk":
                    act.wait_ge(wload[3], 16 * 5)
                    nc.scalar.activation(wa[0][:, i, 0:512], bank, ACT.Copy, scale=cols[:, G1 + i:G1 + i + 1]
                                         ).then_inc(a_setup, 1)
                elif what == "vo":
                    nc.scalar.activation(wa[0][:, i, 512:1024], bank, ACT.Copy, scale=cols[:, G1 + i:G1 + i + 1]
                                         ).then_inc(a_setup, 1)
                elif what in ("upM", "upF"):
                    kt, half = i // 2, i % 2
                    s = cols[:, G2 + kt:G2 + kt + 1] if what == "upM" else 1.0
                    nc.scalar.activation(wup[what[2]][0][:, kt, 512 * half:512 * half + 512], bank, ACT.Copy,
                                         scale=s).then_inc(a_setup, 1)
                elif what in ("dnM", "dnF"):
                    nc.scalar.activation(wdn[what[2]][0][:, 2 * i:2 * i + 2, :].rearrange("p k d -> p (k d)"), bank,
                                         ACT.Copy).then_inc(a_setup, 1)
                elif what == "ga":
                    act.wait_ge(p_const, 3 + E)
                    nc.scalar.activation(ga[:, :, 0:E + ER], ps[:, k % 8, 0:2 * (E + ER)].rearrange(
                        "p (k n) -> p k n", k=KT), ACT.Copy).then_inc(a_setup, 1)
                elif what == "bst":
                    nc.scalar.activation(bst[:, 512 * i:512 * i + 512], ps[0:UROWS, k % 8, :], ACT.Copy
                                         ).then_inc(a_setup, 1)

            for s in [tah_done, kh_done, vcp_done, qf_done, mt_done, exp_done, oth_done, turnh_done,
                      gelu_done, rh_done, ust_done]:
                act.sem_inc(s, 1)
            with act.Fori(0, B) as b:
                for c in range(NC):
                    act.wait_ge(ta_done, 1 + b * NC + c + 1)
                    act.wait_ge(vmm_done, 1 + b * NT + CT * c)
                    if c == 0:
                        act.wait_ge(oproj_done, 1 + b)
                        act.wait_ge(score_done, 1 + b * STEPS)
                    turned_a = ps[:, 6:8, :]
                    nc.scalar.activation(xt[0][:], turned_a, ACT.Copy).then_inc(tah_done, 1)
                    if c % 2 == 0:
                        g = c // 2
                        nc.scalar.activation(xgt[0][:, :, P * g:P * g + P], turned_a[:, :, 0:P], ACT.Copy
                                             ).then_inc(tah_done, 1)
                    for m in range(KT):
                        n = KT * c + m
                        act.wait_ge(kmm_done, 1 + b * NC * KT + n + 1)
                        if n == 0:
                            act.wait_ge(qcp[1], 1 + b * 192)
                        elif m:
                            act.wait_ge(kcp[0], 1 + b * 192 * NC + 192 * (c + 1))
                        else:
                            act.wait_ge(kcp[1], 1 + b * 192 * NC + 192 * c)
                        nc.scalar.activation(ks[0][:], ps[:, m, :], ACT.Identity,
                                             bias=cols[:, BIN + KT + m:BIN + KT + m + 1]).then_inc(kh_done, 1)
                    for i in range(CT):
                        j = CT * c + i
                        act.wait_ge(vmm_done, 1 + b * NT + j + 1)
                        if j == 0:
                            act.wait_ge(av_done, 1 + b * STEPS)
                            act.wait_ge(p_const, 3 + E)
                        nc.scalar.activation(
                            vals[:, j * H * VW:(j + 1) * H * VW].rearrange("p (h v) -> p h v", v=VW)[:, :, 0:HD],
                            ps[:, 2 + i, 0:D].rearrange("p (h v) -> p h v", v=HD), ACT.Copy).then_inc(vcp_done, 1)
                for m in range(KT):
                    act.wait_ge(qmm_done, 1 + b * KT + m + 1)
                    if m:
                        act.wait_ge(qh_done, 1 + b * KT + m)
                        act.wait_ge(ql_done, 1 + b * KT + m)
                    for e in range(2):
                        nc.scalar.activation(qf[:, e, :], ps[:, m, 0:QW], ACT.Identity, scale=cols[:, MASK + e:MASK + e + 1],
                                             bias=cols[:, QB + 2 * m + e:QB + 2 * m + e + 1]).then_inc(qf_done, 1)

                def turn_max(g):
                    act.wait_ge(mturn_done, 1 + b * GROUPS + g + 1)
                    act.wait_ge(mcp, 1 + b * 32 * GROUPS + 32 * g)
                    nc.scalar.activation(mT[:], ps[0:2 * UNITS, 7, 0:P], ACT.Copy).then_inc(mt_done, 1)

                turn_max(0)
                for s in range(STEPS):
                    act.wait_ge(score_done, 1 + b * STEPS + s + 1)
                    if s >= 2:
                        act.wait_ge(av_done, 1 + b * STEPS + s - 1)
                    nc.scalar.activation(prob[s % 2][:].rearrange("p h q -> p (h q)"),
                                         ps[:, 2 * (s % 2):2 * (s % 2) + 2, :].rearrange("p a n -> p (a n)"),
                                         ACT.Exp).then_inc(exp_done, 1)
                    if s % NT == TURN_MAX and s // NT + 1 < GROUPS:
                        turn_max(s // NT + 1)
                act.wait_ge(ott_done, 1 + b + 1)
                act.wait_ge(av_done, 1 + b * STEPS + STEPS)
                nc.scalar.activation(ot[0][:].rearrange("p k q -> p (k q)"), ps[:, 7, :], ACT.Copy).then_inc(oth_done, 1)

                for what, n in FFN_STEPS:
                    if what in ("t2", "t3"):
                        k = TURNS[(what, n)]
                        blk = BLOCK_OF[("M" if what == "t2" else "F", n)]
                        act.wait_ge(turn_done, 1 + b * 2 * NC + k + 1)
                        if blk >= 2:
                            act.wait_ge(up_done, 1 + b * ITEMS + 8 * (blk - 1))
                        nc.scalar.activation(turned[blk % 2][0][:], ps[:, 6:8, :], ACT.Copy).then_inc(turnh_done, 1)
                    elif what == "pick":
                        act.wait_ge(pickt_done, 1 + b * NC + n + 1)
                        if n:
                            act.wait_ge(up_done, 1 + b * ITEMS + 8 * (BLOCK_OF[("F", n - 1)] + 1))
                        nc.scalar.activation(ust[:], ps[0:UROWS, 6, :], ACT.Copy).then_inc(ust_done, 1)
                    elif what == "up":
                        act.wait_ge(up_done, 1 + b * ITEMS + n + 1)
                        if n in GELU:
                            k, f = GELU[n], n % FT
                            if k >= 2:
                                act.wait_ge(gl_done, 1 + b * NC * FT + k - 1)
                            nc.scalar.activation(gel[k % 2][:], ps[:, n % 2, :], ACT.Gelu,
                                                 bias=cols[:, B1C + f:B1C + f + 1]).then_inc(gelu_done, 1)
                        else:
                            if n >= RING:
                                act.wait_ge(down_done, 1 + b * ITEMS + n - RING + 1)
                            nc.scalar.activation(hid[n % RING][0][:], ps[:, n % 2, :], ACT.Relu).then_inc(rh_done, 1)

        @block.vector
        def _(dve):
            chain = [0]

            def link(ins, hold=True):
                chain[0] += 1
                ins.then_inc(d_setup, 1)
                if hold:
                    dve.wait_ge(d_setup, chain[0])

            dve.wait_ge(wload[0], 16)
            dve.wait_ge(wload[2], 64)
            dve.wait_ge(wload[3], 80)
            for m in range(6):
                link(nc.vector.tensor_tensor_reduce(out=junk[:], in0=nwin[:, m, :], in1=lnb[:, 0, :], scale=1.0, scalar=0.0,
                                                    op0=ALU.mult, op1=ALU.add, accum_out=cols[:, BINS + m:BINS + m + 1]))
            link(nc.vector.tensor_tensor(cols[:, BIN:BIN + 6], cols[:, BIN:BIN + 6], cols[:, BINS:BINS + 6], ALU.add))
            dve.wait_ge(p_const, 3 + E)
            for k in range(KT):
                link(nc.vector.tensor_scalar(cvb[:, k, :], vals[:, 0:P], cols[:, BIN + 4 + k:BIN + 5 + k], None, ALU.mult))
            assert chain[0] == CVB
            dve.wait_ge(p_ident, 2)
            for e in range(2):
                link(nc.vector.tensor_reduce(cols[:, MASK + e:MASK + e + 1],
                                             ident[:].rearrange("p (a e d) -> p e a d", e=2, d=HD)[:, e],
                                             AX.XY, ALU.add))
            link(nc.vector.tensor_scalar(cols[:, MASK:MASK + 2], cols[:, MASK:MASK + 2], float(HD) ** -0.5, None, ALU.mult))
            for m in range(KT):
                link(nc.vector.tensor_scalar(cols[:, QB + 2 * m:QB + 2 * m + 2], cols[:, MASK:MASK + 2],
                                             cols[:, BIN + m:BIN + m + 1], None, ALU.mult))
            dve.wait_ge(wload[4], 16)
            for m in range(FT):
                link(nc.vector.tensor_tensor_reduce(out=junk[:], in0=nw1[:, m, :], in1=lnb[:, 1, :], scale=1.0, scalar=0.0,
                                                    op0=ALU.mult, op1=ALU.add, accum_out=cols[:, B1S + m:B1S + m + 1]))
            link(nc.vector.tensor_tensor(cols[:, B1C:B1C + FT], cols[:, B1C:B1C + FT], cols[:, B1S:B1S + FT], ALU.add))
            dve.wait_ge(wload[9], 16 * E)
            src = nlb[:].rearrange("p m e r -> p m (e r)")
            link(nc.vector.tensor_copy(lbs[:, :, 0:ER].bitcast(F32R), src))
            link(nc.vector.tensor_copy(lbs[:, :, ER:2 * ER], lbs[:, :, 0:ER]))
            link(nc.vector.tensor_tensor(lbs[:, :, 2 * ER:3 * ER].bitcast(F32R), src, lbs[:, :, 0:ER], ALU.subtract))
            link(nc.vector.tensor_copy(lbs[:, :, 3 * ER].bitcast(F32R), wibc[:]))
            link(nc.vector.tensor_tensor(lbs[:, :, 3 * ER + 1].bitcast(F32R), wibc[:], lbs[:, :, 3 * ER], ALU.subtract))
            assert chain[0] == LBS
            n_act = 0
            for k, (what, i) in enumerate(SG):
                dve.wait_ge(pe_setup, k + 1)
                n_act += {"wout": 2, "crow": 0}.get(what, 1)
                dve.wait_ge(a_setup, max(n_act, 1))
                bank = ps[:, k % 8, :]
                if what == "crow":
                    link(nc.vector.tensor_tensor(crow[:], ps[:, k % 8, 0:D], boutr[:], ALU.add), False)
                elif what == "wout":
                    link(nc.vector.tensor_tensor(wo[1][:].rearrange("p k d -> p (k d)"), bank,
                                                 wo[0][:].rearrange("p k d -> p (k d)"), ALU.subtract), False)
                elif what in ("qk", "vo"):
                    o = 0 if what == "qk" else 512
                    link(nc.vector.scalar_tensor_tensor(out=wa[1][:, i, o:o + 512], in0=bank, scalar=cols[:, G1 + i:G1 + i + 1],
                                                        in1=wa[0][:, i, o:o + 512], op0=ALU.mult, op1=ALU.subtract), False)
                elif what == "upM":
                    kt, o = i // 2, 512 * (i % 2)
                    link(nc.vector.scalar_tensor_tensor(out=wup["M"][1][:, kt, o:o + 512], in0=bank,
                                                        scalar=cols[:, G2 + kt:G2 + kt + 1], in1=wup["M"][0][:, kt, o:o + 512],
                                                        op0=ALU.mult, op1=ALU.subtract), False)
                elif what == "upF":
                    kt, o = i // 2, 512 * (i % 2)
                    link(nc.vector.tensor_tensor(wup["F"][1][:, kt, o:o + 512], bank, wup["F"][0][:, kt, o:o + 512],
                                                 ALU.subtract), False)
                elif what in ("dnM", "dnF"):
                    w = wdn[what[2]]
                    link(nc.vector.tensor_tensor(w[1][:, 2 * i:2 * i + 2, :].rearrange("p k d -> p (k d)"), bank,
                                                 w[0][:, 2 * i:2 * i + 2, :].rearrange("p k d -> p (k d)"), ALU.subtract), False)
                elif what == "ga":
                    link(nc.vector.tensor_tensor(
                        ga[:, :, E + ER:GW], ps[:, k % 8, 0:GW].rearrange("p (k n) -> p k n", k=KT),
                        ga[:, :, 0:E + ER], ALU.subtract), False)
            assert chain[0] == D_SETUP, chain[0]

            aggregated = nc.alloc_register(dve.engine)
            nc.vector.reg_mov(aggregated, 1)
            for s in [stat_done, aggr_done, vare_done, norm_done, tal_done, kl_done, x1_done,
                      qh_done, ql_done, maxr_done, negm_done, negs_done, oraw_done, rsum_done,
                      otok_done, otl_done, x1g_done, turnl_done, gh_done, rl_done, sumy_done,
                      sumz_done, gatec_done, pick_done]:
                dve.sem_inc(s, 1)
            with dve.Fori(0, B) as b:
                def ln_a(k, rows):
                    for i in range(CT):
                        nc.vector.bn_stats(stats[:, i, :], rows[:, i, :]).then_inc(stat_done, 1)
                    dve.wait_ge(stat_done, 1 + b * NLN * CT + CT * (k + 1))
                    dve.wait_ge(norm_done, 1 + b * NLN * CT + CT * k)
                    nc.vector.reg_add(aggregated, aggregated, CT)
                    for i in range(CT):
                        nc.vector.bn_aggr(mv[:, i, :], stats[:, i, :]).then_inc(aggr_done, 1)
                    dve.wait_ge(aggr_done, dve.snap(aggregated, min_val=CT + 1))
                    nc.vector.tensor_scalar(vare[:], mv[:, :, 1], EPS, None, ALU.add).then_inc(vare_done, 1)

                def ln_b(k, dst, rows):
                    dve.wait_ge(rstd_done, 1 + b * NLN + k + 1)
                    for i in range(CT):
                        nc.vector.tensor_scalar(dst[:, i, :], rows[:, i, :], mv[:, i, 0:1], rstd[:, i:i + 1],
                                                ALU.subtract, ALU.mult).then_inc(norm_done, 1)

                def norm_input(c):
                    dve.wait_ge(xld[c % 2], 1 + b * 32 + 16 * (c // 2 + 1))
                    ln_a(c, xin[c % 2])
                    dve.wait_ge(ta_done, 1 + b * NC + c)
                    if c == 0:
                        dve.wait_ge(ott_done, 1 + b)
                    ln_b(c, xn, xin[c % 2])

                norm_input(0)
                for c in range(NC):
                    dve.wait_ge(tah_done, 1 + b * (NC + NQ) + c + 2 + c // 2)
                    turned_a = ps[:, 6:8, :]
                    nc.vector.tensor_tensor(xt[1][:], turned_a, xt[0][:], ALU.subtract).then_inc(tal_done, 1)
                    if c % 2 == 0:
                        g = c // 2
                        nc.vector.tensor_tensor(xgt[1][:, :, P * g:P * g + P], turned_a[:, :, 0:P],
                                                xgt[0][:, :, P * g:P * g + P], ALU.subtract).then_inc(tal_done, 1)
                    if c + 1 < NC:
                        norm_input(c + 1)
                    for m in range(KT):
                        dve.wait_ge(kh_done, 1 + b * NC * KT + KT * c + m + 1)
                        nc.vector.scalar_tensor_tensor(out=ks[1][:], in0=ps[:, m, :], scalar=cols[:, BIN + KT + m:BIN + KT + m + 1],
                                                       in1=ks[0][:], op0=ALU.add, op1=ALU.subtract).then_inc(kl_done, 1)
                    dve.wait_ge(xc_done, 1 + b * NC + c + 1)
                    for j in LOCAL[c]:
                        i = j - CT * c
                        dve.wait_ge(vcp_done, 1 + b * NT + j + 1)
                        nc.vector.tensor_tensor(xin[c % 2][:, i, :], xin[c % 2][:, i, :], ps[:, 2 + i, D:2 * D],
                                                ALU.add).then_inc(x1_done, 1)
                for m in range(KT):
                    dve.wait_ge(qf_done, 1 + b * 2 * KT + 2 * m + 2)
                    if m:
                        dve.wait_ge(qcp[0], 1 + b * 192 + 192)
                    else:
                        dve.wait_ge(kcp[1], 1 + b * 192 * NC + 192 * NC)
                    q2 = qf[:].rearrange("p e q -> p (e q)")
                    nc.vector.tensor_copy(ks[0][:], q2).then_inc(qh_done, 1)
                    dve.wait_ge(qh_done, 1 + b * KT + m + 1)
                    nc.vector.tensor_tensor(ks[1][:], q2, ks[0][:], ALU.subtract).then_inc(ql_done, 1)

                def row_max(u):
                    g, n = u // NMAX, u % NMAX
                    dve.wait_ge(maxmm_done, 1 + b * GROUPS * NMAX + u + 1)
                    if n == 0 and g >= 2:
                        dve.wait_ge(negm_done, 1 + b * GROUPS + g - 1)
                    nc.vector.tensor_reduce(mx[:, g % 2, n:n + 1], ps[:, 4 + u % 2, :], AX.X, ALU.max).then_inc(maxr_done, 1)
                    if n == NMAX - 1:
                        dve.wait_ge(maxr_done, 1 + b * GROUPS * NMAX + u + 1)
                        if g:
                            dve.wait_ge(negs_done, 1 + b * 2 * GROUPS + 2 * g)
                        nc.vector.tensor_reduce(negm[:], mx[:, g % 2, :].rearrange("p (u k) -> p u k", k=KQ), AX.X, ALU.max,
                                                negate=True).then_inc(negm_done, 1)
                        dve.wait_ge(negm_done, 1 + b * GROUPS + g + 1)
                        dve.wait_ge(mturn_done, 1 + b * GROUPS + g)
                        nc.vector.tensor_copy(negs[:, 0:UNITS].bitcast(F32R), negm[:]).then_inc(negs_done, 1)
                        dve.wait_ge(negs_done, 1 + b * 2 * GROUPS + 2 * g + 1)
                        nc.vector.tensor_tensor(negs[:, UNITS:].bitcast(F32R), negm[:], negs[:, 0:UNITS],
                                                ALU.subtract).then_inc(negs_done, 1)

                def out_raw(g):
                    dve.wait_ge(av_done, 1 + b * STEPS + NT * (g + 1))
                    dve.wait_ge(oturn_done, 1 + b * GROUPS + g)
                    if g == 0:
                        dve.wait_ge(ql_done, 1 + b * KT + KT)
                    nc.vector.tensor_copy(oraw[:], ps[:, 6, 0:QW]).then_inc(oraw_done, 1)

                def out_norm(g):
                    dve.wait_ge(oturn_done, 1 + b * GROUPS + g + 1)
                    if g:
                        dve.wait_ge(otok_done, 1 + b * GROUPS * NQ + NQ * g)
                    turned_o = ps[:, 7, 0:NQ * P].rearrange("p (t h v) -> p t h v", t=NQ, h=4)
                    nc.vector.reciprocal(rsum[:], turned_o[:, :, :, HD]).then_inc(rsum_done, 1)
                    dve.wait_ge(rsum_done, 1 + b * GROUPS + g + 1)
                    for t in range(NQ):
                        nc.vector.tensor_tensor(
                            otok[:, t, 4 * HD * g:4 * HD * (g + 1)].rearrange("p (h v) -> p h v", h=4),
                            turned_o[:, t, :, 0:HD], rsum[:, t, :, None].to_broadcast([P, 4, HD]),
                            ALU.mult).then_inc(otok_done, 1)

                for u in range(LEAD):
                    row_max(u)
                u = LEAD
                for s in range(STEPS):
                    for _ in range(2):
                        if u < GROUPS * NMAX:
                            row_max(u)
                            u += 1
                    g, k = s // NT, s % NT
                    if g and k == OUT_TURN:
                        out_norm(g - 1)
                    if k == NT - 1:
                        out_raw(g)
                out_norm(GROUPS - 1)
                dve.wait_ge(oth_done, 1 + b + 1)
                nc.vector.tensor_tensor(ot[1][:].rearrange("p k q -> p (k q)"), ps[:, 7, :],
                                        ot[0][:].rearrange("p k q -> p (k q)"), ALU.subtract).then_inc(otl_done, 1)
                dve.wait_ge(oproj_done, 1 + b + 1)
                dve.wait_ge(xc_done, 1 + b * NC + NC)
                for t in range(NQ):
                    nc.vector.tensor_tensor(xg[:, t, :], xg[:, t, :], ps[:, 6, D * t:D * t + D], ALU.add).then_inc(x1g_done, 1)

                for what, n in FFN_STEPS:
                    if what == "ln2a":
                        dve.wait_ge(fld[n % 2], 1 + b * 64 + 32 * (n // 2 + 1))
                        ln_a(LN[("ln2", n)], x1in)
                    elif what == "ln2b":
                        if n:
                            dve.wait_ge(turn_done, 1 + b * 2 * NC + TURNS[("t2", n - 1)] + 1)
                        ln_b(LN[("ln2", n)], xn2, x1in)
                    elif what == "ln3a":
                        dve.wait_ge(sumy_done, 1 + b * 2 * NC + 2 * (n + 1))
                        ln_a(LN[("ln3", n)], srow[n % 2])
                    elif what == "ln3b":
                        ln_b(LN[("ln3", n)], srow[n % 2], srow[n % 2])
                    elif what == "ln4a":
                        dve.wait_ge(sumz_done, 1 + b * 2 * NC + 2 * (n + 1))
                        ln_a(LN[("ln4", n)], srow[n % 2])
                    elif what == "ln4b":
                        ln_b(LN[("ln4", n)], srow[n % 2], srow[n % 2])
                    elif what in ("t2", "t3"):
                        k = TURNS[(what, n)]
                        blk = BLOCK_OF[("M" if what == "t2" else "F", n)]
                        dve.wait_ge(turnh_done, 1 + b * 2 * NC + k + 1)
                        nc.vector.tensor_tensor(turned[blk % 2][1][:], ps[:, 6:8, :], turned[blk % 2][0][:],
                                                ALU.subtract).then_inc(turnl_done, 1)
                    elif what == "sumy":
                        dve.wait_ge(down_done, 1 + b * ITEMS + 8 * (BLOCK_OF[("M", n)] + 1))
                        dve.wait_ge(resb_done, 1 + b * NC + n + 1)
                        if n >= 2:
                            dve.wait_ge(ost[n % 2], 1 + b * 32 + 16)
                        for h in range(2):
                            nc.vector.tensor_tensor(
                                srow[n % 2][:, 2 * h:2 * h + 2, :].rearrange("p t d -> p (t d)"),
                                xrow[n % 2][:, 2 * h:2 * h + 2, :].rearrange("p t d -> p (t d)"), ps[:, 2 + h, :],
                                ALU.add).then_inc(sumy_done, 1)
                    elif what == "sumz":
                        dve.wait_ge(down_done, 1 + b * ITEMS + 8 * (BLOCK_OF[("F", n)] + 1))
                        dve.wait_ge(x3w_done, 1 + b * NC + n + 1)
                        for h in range(2):
                            rows = srow[n % 2][:, 2 * h:2 * h + 2, :].rearrange("p t d -> p (t d)")
                            nc.vector.tensor_tensor(rows, rows, ps[:, 4 + h, :], ALU.add).then_inc(sumz_done, 1)
                    elif what == "gate":
                        dve.wait_ge(gate_done, 1 + b * NC + n + 1)
                        nc.vector.tensor_copy(gcopy[:].rearrange("p (a t) g -> p a t g", a=2),
                                              ps[:, 6:8, :].rearrange("p a (t g) -> p a t g", t=2)[:, :, :, 0:GW]
                                              ).then_inc(gatec_done, 1)
                        dve.wait_ge(gatec_done, 1 + b * NC + n + 1)
                        steps = [1 + b * NPICK * NC + NPICK * n]

                        def then(ins, steps=steps):
                            ins.then_inc(pick_done, 1)
                            steps[0] = steps[0] + 1
                            dve.wait_ge(pick_done, steps[0])

                        then(nc.vector.tensor_tensor(uall[:], gcopy[:, :, 0:E + ER], gcopy[:, :, E + ER:GW], ALU.add))
                        logits = uall[:, :, 0:E]
                        then(nc.vector.tensor_tensor(logits, logits, gateb[:, None, :].to_broadcast([P, CT, E]), ALU.add))
                        then(nc.vector.tensor_reduce(pickm[:], logits, AX.X, ALU.max))
                        top_of = pickm[:, :, None].to_broadcast([P, CT, E])
                        then(nc.vector.tensor_tensor(picke[:], logits, top_of, ALU.is_equal))
                        then(nc.vector.tensor_tensor(picke[:], picke[:], rank[:, None, :].to_broadcast([P, CT, E]), ALU.mult))
                        then(nc.vector.tensor_reduce(pickm[:], picke[:], AX.X, ALU.max))
                        then(nc.vector.tensor_tensor(picke[:], picke[:], top_of, ALU.is_equal))
                        u4 = uall[:, :, E:].rearrange("p t (e r) -> p t e r", r=R)
                        then(nc.vector.tensor_tensor(u4, u4, picke[:, :, :, None].to_broadcast([P, CT, E, R]), ALU.mult))
                        u2 = uall[:, :, E:]
                        if n:
                            dve.wait_ge(pickt_done, 1 + b * NC + n)
                        then(nc.vector.tensor_copy(us[:, :, 0:ER].bitcast(F32R), u2))
                        then(nc.vector.tensor_tensor(us[:, :, ER:2 * ER].bitcast(F32R), u2, us[:, :, 0:ER], ALU.subtract))
                        then(nc.vector.tensor_copy(us[:, :, 2 * ER:3 * ER], us[:, :, 0:ER]))
                        then(nc.vector.memset(us[:, :, 3 * ER:], 1.0))
                    elif what == "up":
                        if n >= RING:
                            dve.wait_ge(down_done, 1 + b * ITEMS + n - RING + 1)
                        if n in GELU:
                            k = GELU[n]
                            dve.wait_ge(gelu_done, 1 + b * NC * FT + k + 1)
                            nc.vector.tensor_copy(hid[n % RING][0][:], gel[k % 2][:]).then_inc(gh_done, 1)
                        else:
                            dve.wait_ge(rh_done, 1 + b * NC * FT + RELU[n] + 1)
                            nc.vector.scalar_tensor_tensor(out=hid[n % RING][1][:], in0=ps[:, n % 2, :], scalar=0.0,
                                                           in1=hid[n % RING][0][:], op0=ALU.max, op1=ALU.subtract
                                                           ).then_inc(rl_done, 1)

        @block.tensor
        def _(pe):
            mm = nc.tensor.matmul

            def three(o, l, r, start, stop, part=None):
                mm(o, l[0], r[0], start=start, stop=False, skip_group_check=True)
                mm(o, l[0], r[1], start=False, stop=False, skip_group_check=True)
                return mm(o, l[1], r[0], start=False, stop=stop, skip_group_check=True)

            pe.wait_ge(p_ident, 2)
            n_a = n_d = 0
            freed = []
            for k, (what, i) in enumerate(SG):
                if k >= 8:
                    pe.wait_ge(a_setup, freed[k - 8][0])
                    pe.wait_ge(d_setup, LBS + freed[k - 8][1])
                n_a += {"wout": 2, "crow": 0}.get(what, 1)
                n_d += what != "bst"
                freed.append((n_a, n_d))
                o = ps[:, k % 8, :]

                def turn(col, src, rows=P, n=P):
                    return nc.tensor.transpose(o[0:n, col:col + rows], src, ident[0:rows, 0:rows])

                if what == "wout":
                    pe.wait_ge(wload[1], 16)
                    for f in range(KT):
                        for m in range(KT):
                            last = turn(D * f + P * m, nwout[:, m, P * f:P * f + P])
                elif what == "qk":
                    pe.wait_ge(wload[0], 16)
                    for m in range(4):
                        last = turn(P * m, nwin[:, m, P * i:P * i + P])
                elif what == "vo":
                    pe.wait_ge(a_setup, 1)
                    for m in range(2):
                        turn(P * m, nwin[:, 4 + m, P * i:P * i + P])
                    for m in range(2):
                        last = mm(o[:, D:2 * D], nwin[:, 4 + m, P * i:P * i + P], wof[:, m, :], start=m == 0, stop=m == 1)
                elif what == "crow":
                    pe.wait_ge(d_setup, CVB)
                    for m in range(KT):
                        last = mm(o[:, 0:D], cvb[:, m, :], wof[:, m, :], start=m == 0, stop=m == 1)
                elif what in ("upM", "upF"):
                    pe.wait_ge(wload[4 if what == "upM" else 6], 16)
                    w = nw1 if what == "upM" else nwi
                    kt, half = i // 2, i % 2
                    for m in range(4):
                        last = turn(P * m, w[:, 4 * half + m, P * kt:P * kt + P])
                elif what in ("dnM", "dnF"):
                    pe.wait_ge(wload[5 if what == "dnM" else 7], 16)
                    w = nw2 if what == "dnM" else nwo
                    for f in range(2):
                        for m in range(2):
                            last = turn(D * f + P * m, w[:, m, P * (2 * i + f):P * (2 * i + f) + P])
                elif what == "ga":
                    pe.wait_ge(wload[8], 32)
                    for m in range(KT):
                        last = turn((E + ER) * m, nga[:, P * m:P * m + P], rows=E + ER)
                elif what == "bst":
                    pe.wait_ge(d_setup, LBS)
                    for m in range(4):
                        last = turn(P * m, lbs[:, 4 * i + m, :], n=UROWS)
                last.then_inc(pe_setup, 1)
            pe.wait_ge(a_setup, A_SETUP)
            pe.wait_ge(d_setup, D_SETUP)

            for s in [ta_done, kmm_done, vmm_done, qmm_done, maxmm_done, mturn_done, score_done,
                      av_done, oturn_done, ott_done, oproj_done, turn_done, up_done, down_done,
                      gate_done, pickt_done]:
                pe.sem_inc(s, 1)
            with pe.Fori(0, B) as b:
                def turn_input(c):
                    pe.wait_ge(norm_done, 1 + b * NLN * CT + CT * (c + 1))
                    if c:
                        pe.wait_ge(tah_done, 1 + b * (NC + NQ) + c + (c + 1) // 2)
                        pe.wait_ge(tal_done, 1 + b * (NC + NQ) + c + (c + 1) // 2)
                    for k in range(KT):
                        for i in range(CT):
                            last = nc.tensor.transpose(ps[:, 6 + k, P * i:P * i + P], xn[:, i, P * k:P * k + P], ident[:])
                    last.then_inc(ta_done, 1)

                turn_input(0)
                for c in range(NC):
                    pe.wait_ge(tah_done, 1 + b * (NC + NQ) + c + 1 + (c + 1) // 2)
                    pe.wait_ge(tal_done, 1 + b * (NC + NQ) + c + 1 + (c + 1) // 2)
                    for m in range(KT):
                        if c:
                            pe.wait_ge(kh_done, 1 + b * NC * KT + KT * (c - 1) + m + 1)
                            pe.wait_ge(kl_done, 1 + b * NC * KT + KT * (c - 1) + m + 1)
                        for k in range(KT):
                            last = three(ps[:, m, :], [w[:, k, D + P * m:D + P * m + P] for w in wa],
                                         [t[:, k, :] for t in xt], k == 0, k == KT - 1)
                        last.then_inc(kmm_done, 1)
                    if c + 1 < NC:
                        turn_input(c + 1)
                    for i in range(CT):
                        j = CT * c + i
                        n = D if j in GLOBAL else 2 * D
                        if c and i == 0:
                            pe.wait_ge(vcp_done, 1 + b * NT + CT * c)
                            pe.wait_ge(x1_done, 1 + b * NL + LOCALS[c - 1])
                        for k in range(KT):
                            last = three(ps[:, 2 + i, 0:n], [t[:, k, P * i:P * i + P] for t in xt],
                                         [w[:, k, 2 * D:2 * D + n] for w in wa], k == 0, k == KT - 1)
                        last.then_inc(vmm_done, 1)
                pe.wait_ge(tah_done, 1 + b * (NC + NQ) + NC + NQ)
                pe.wait_ge(tal_done, 1 + b * (NC + NQ) + NC + NQ)
                for m in range(KT):
                    pe.wait_ge(kl_done, 1 + b * NC * KT + KT * (NC - 1) + m + 1)
                    for k in range(KT):
                        last = three(ps[:, m, 0:QW], [w[:, k, P * m:P * m + P] for w in wa],
                                     [t[:, k, :] for t in xgt], k == 0, k == KT - 1)
                    last.then_inc(qmm_done, 1)

                def score_max(u):
                    g, n = u // NMAX, u % NMAX
                    unit, piece = n // KQ, n % KQ
                    pair, e, t = GP * g + unit // (2 * NQ), unit // NQ % 2, unit % NQ
                    if u == 0:
                        for i in range(KT):
                            pe.wait_ge(kcp[i], 1 + b * 192 * NC + 192 * NC)
                            pe.wait_ge(qcp[i], 1 + b * 192 + 192)
                        pe.wait_ge(x1_done, 1 + b * NL + NL)
                        pe.wait_ge(vcp_done, 1 + b * NT + NT)
                    elif u >= 2:
                        pe.wait_ge(maxr_done, 1 + b * GROUPS * NMAX + u - 1)
                    mm(ps[:, 4 + u % 2, :], qstack[0:SROWS, pair, e, P * t:P * t + P],
                       kstack[0:SROWS, pair, 512 * piece:512 * piece + 512], start=True, stop=True).then_inc(maxmm_done, 1)

                def turn_max(g):
                    pe.wait_ge(negs_done, 1 + b * 2 * GROUPS + 2 * g + 2)
                    if g >= 2:
                        pe.wait_ge(otok_done, 1 + b * GROUPS * NQ + NQ * (g - 1))
                    nc.tensor.transpose(ps[0:2 * UNITS, 7, 0:P], negs[:], ident[:]).then_inc(mturn_done, 1)

                def scores(s):
                    g, k = s // NT, s % NT
                    if k == 0:
                        pe.wait_ge(mcp, 1 + b * 32 * GROUPS + 32 * (g + 1))
                    if s >= 2:
                        pe.wait_ge(exp_done, 1 + b * STEPS + s - 1)
                    for i in range(GP):
                        last = mm(ps[:, 2 * (s % 2) + i, :], kstack[:, GP * g + i, P * k:P * k + P],
                                  qstack[:, GP * g + i, :, :].rearrange("p e q -> p (e q)"), start=True, stop=True)
                    last.then_inc(score_done, 1)

                def attend(s):
                    g, k = s // NT, s % NT
                    pe.wait_ge(exp_done, 1 + b * STEPS + s + 1)
                    if k == 0:
                        if g:
                            pe.wait_ge(oraw_done, 1 + b * GROUPS + g)
                    for h in range(4):
                        v = (k * H + 4 * g + h) * VW
                        last = mm(ps[32 * h:32 * h + 32, 6, 0:QW], vals[:, v:v + 32], prob[s % 2][:, h, :],
                                  start=k == 0, stop=k == NT - 1)
                    last.then_inc(av_done, 1)

                def turn_out(g):
                    pe.wait_ge(oraw_done, 1 + b * GROUPS + g + 1)
                    pe.wait_ge(mt_done, 1 + b * GROUPS + min(g + 2, GROUPS) if g + 1 < GROUPS else b * GROUPS + GROUPS)
                    for t in range(NQ):
                        last = nc.tensor.transpose(ps[:, 7, P * t:P * t + P], oraw[:, P * t:P * t + P], ident[:])
                    last.then_inc(oturn_done, 1)

                pe.wait_ge(ones_done, 1 + b + 1)
                for u in range(LEAD):
                    score_max(u)
                turn_max(0)
                scores(0)
                scores(1)
                u = LEAD
                for s in range(STEPS):
                    for _ in range(2):
                        if u < GROUPS * NMAX:
                            score_max(u)
                            u += 1
                    g, k = s // NT, s % NT
                    if k == TURN_MAX and g + 1 < GROUPS:
                        turn_max(g + 1)
                    if g and k == OUT_TURN:
                        turn_out(g - 1)
                    attend(s)
                    if s + 2 < STEPS:
                        scores(s + 2)
                turn_out(GROUPS - 1)
                pe.wait_ge(otok_done, 1 + b * GROUPS * NQ + GROUPS * NQ)
                for k in range(KT):
                    for t in range(NQ):
                        last = nc.tensor.transpose(ps[:, 7, QW * k + P * t:QW * k + P * t + P], otok[:, t, P * k:P * k + P], ident[:])
                last.then_inc(ott_done, 1)
                pe.wait_ge(oth_done, 1 + b + 1)
                pe.wait_ge(otl_done, 1 + b + 1)
                for t in range(NQ):
                    for k in range(KT):
                        last = three(ps[:, 6, D * t:D * t + D], [o[:, k, P * t:P * t + P] for o in ot],
                                     [w[:, k, :] for w in wo], t == 0 and k == 0, k == KT - 1)
                last.then_inc(oproj_done, 1)

                def spare_free(step):
                    k = SPARE[step]
                    if k == 0:
                        pe.wait_ge(x1g_done, 1 + b * NQ + NQ)
                        return
                    (what, n), = [s for s, i in SPARE.items() if i == k - 1]
                    if what in ("t2", "t3"):
                        pe.wait_ge(turnl_done, 1 + b * 2 * NC + TURNS[(what, n)] + 1)
                    elif what == "gate":
                        pe.wait_ge(gatec_done, 1 + b * NC + n + 1)
                    else:
                        pe.wait_ge(ust_done, 1 + b * NC + n + 1)

                for what, n in FFN_STEPS:
                    if what in ("t2", "t3"):
                        spare_free((what, n))
                        pe.wait_ge(norm_done, 1 + b * NLN * CT + CT * (LN[("ln2" if what == "t2" else "ln3", n)] + 1))
                        rows = xn2 if what == "t2" else srow[n % 2]
                        for k in range(KT):
                            for i in range(CT):
                                last = nc.tensor.transpose(ps[:, 6 + k, P * i:P * i + P], rows[:, i, P * k:P * k + P], ident[:])
                        last.then_inc(turn_done, 1)
                    elif what == "gate":
                        spare_free((what, n))
                        t = turned[BLOCK_OF[("F", n)] % 2]
                        for i in range(CT):
                            for k in range(KT):
                                for h in range(2):
                                    last = mm(ps[:, 6 + i // 2, 256 * (i % 2):256 * (i % 2) + 256],
                                              t[h][:, k, P * i:P * i + P], ga[:, k, :],
                                              start=i % 2 == 0 and k == 0 and h == 0, stop=k == KT - 1 and h == 1,
                                              skip_group_check=True)
                        last.then_inc(gate_done, 1)
                    elif what == "pick":
                        spare_free((what, n))
                        pe.wait_ge(pick_done, 1 + b * NPICK * NC + NPICK * (n + 1))
                        for i in range(CT):
                            last = nc.tensor.transpose(ps[0:UROWS, 6, P * i:P * i + P], us[:, i, :], ident[:])
                        last.then_inc(pickt_done, 1)
                    elif what == "up":
                        blk, f = n // FT, n % FT
                        w, ch = BLOCKS[blk]
                        if f == 0:
                            k = TURNS[("t2" if w == "M" else "t3", ch)]
                            pe.wait_ge(turnh_done, 1 + b * 2 * NC + k + 1)
                            pe.wait_ge(turnl_done, 1 + b * 2 * NC + k + 1)
                        if n >= 2:
                            if n - 2 in GELU:
                                pe.wait_ge(gelu_done, 1 + b * NC * FT + GELU[n - 2] + 1)
                            else:
                                pe.wait_ge(rl_done, 1 + b * NC * FT + RELU[n - 2] + 1)
                        for k in range(KT):
                            last = three(ps[:, n % 2, :], [t[:, k, P * f:P * f + P] for t in wup[w]],
                                         [t[:, k, :] for t in turned[blk % 2]], k == 0, w == "M" and k == KT - 1)
                        if w == "F":
                            if f == 0:
                                pe.wait_ge(ust_done, 1 + b * NC + ch + 1)
                            last = mm(ps[:, n % 2, :], bst[:, P * f:P * f + P], ust[:], start=False, stop=True,
                                      skip_group_check=True)
                        last.then_inc(up_done, 1)
                    elif what == "down":
                        blk, f = n // FT, n % FT
                        w, ch = BLOCKS[blk]
                        if n in GELU:
                            pe.wait_ge(gl_done, 1 + b * NC * FT + GELU[n] + 1)
                        else:
                            pe.wait_ge(rl_done, 1 + b * NC * FT + RELU[n] + 1)
                        if f == 0 and ch:
                            pe.wait_ge(sumy_done if w == "M" else sumz_done, 1 + b * 2 * NC + 2 * ch)
                        for i in range(CT):
                            bank = (2 if w == "M" else 4) + i // 2
                            last = three(ps[:, bank, D * (i % 2):D * (i % 2) + D],
                                         [t[:, P * i:P * i + P] for t in hid[n % RING]],
                                         [t[:, f, :] for t in wdn[w]], f == 0 and i % 2 == 0, f == FT - 1)
                        last.then_inc(down_done, 1)


TURN_MAX = 13
OUT_TURN = 3
NPICK = 12
CVB = 9
LBS = CVB + 5 + 9 + 5
D_SETUP = LBS + 23
A_SETUP = 25


_INS = ["L0_attn_x", "L0_attn_w_in", "L0_attn_b_in", "L0_attn_w_out", "L0_attn_b_out", "L0_attn_w1", "L0_attn_b1",
        "L0_attn_w2", "L0_attn_b2", "L0_attn_ln1_g", "L0_attn_ln1_b", "L0_attn_ln2_g", "L0_attn_ln2_b",
        "L0_ffn_gate_W", "L0_ffn_gate_b", "L0_ffn_wi_W", "L0_ffn_wi_b", "L0_ffn_wo_W", "L0_ffn_wo_b",
        "L0_ffn_lora_A", "L0_ffn_lora_B"]


def kernel(**inputs):
    import numpy as _np
    import concourse.bacc as _bacc
    from concourse.bass_utils import run_bass_kernel_spmd as _run

    nc = _bacc.Bacc("TRN2", target_bir_lowering=False, num_devices=1)
    arrays, args = {}, []
    for name in _INS:
        a = _np.ascontiguousarray(inputs[name])
        arrays[f"in_{name}"] = a
        args.append(nc.dram_tensor(f"in_{name}", a.shape, mybir.dt.from_np(a.dtype), kind="ExternalInput").ap())
    args.append(nc.dram_tensor("out_0", (B, T, D), F32, kind="ExternalOutput").ap())
    attention_ffn_kernel(nc, *args)
    r = _run(nc, [arrays], core_ids=[0])
    return r.results[0]["out_0"]
```

```python
from contextlib import ExitStack

import concourse.bass as bass
from concourse import mybir

F32 = mybir.dt.float32
F32R = mybir.dt.float32r
ALU = mybir.AluOpType
ACT = mybir.ActivationFunctionType
AX = mybir.AxisListType

P = 128
B, T, D = 4, 2048, 256
H, HD = 16, 16
STRIDE = 8
F = 1024
E, R = 8, 4
EPS = 1e-5

NT = T // P
KT = D // P
FT = F // P
NQ = NT // STRIDE
QW = NQ * P
AT = 2
NA = NT // AT
AW = AT * P
XB = 3
CT = 4
NC = NT // CT
CW = CT * P
PAIRS = H // 2
PR = 2 * HD
GROUPS = 4
GP = PAIRS // GROUPS
VW = HD + 1
SROWS = 3 * PR
MROWS = SROWS + 2
UNITS = GP * 2 * NQ
KQ = T // 512
NMAX = UNITS * KQ
STEPS = GROUPS * NT
EARLY = NMAX // 2
LEAD = NMAX + NMAX // 4
ER = E * R
UROWS = 3 * ER + 2
GW = 2 * (E + ER)
ITEMS = 2 * NC * FT
LAG = 2
RING = 3

ORDER = [1, 2, 3, 0]
BLOCKS = [("M", 0), ("M", 1), ("F", 0), ("M", 2), ("F", 1), ("M", 3), ("F", 2), ("F", 3)]
BEFORE = {
    0: [("oturn", 0)], 1: [("onorm", 0), ("oturned", 0)], 2: [("ln2a", 1), ("oproj", 0)], 3: [("ln2b", 1)],
    5: [("t2", 1)],
    10: [("sumy", 0), ("ln3a", 0)], 11: [("ln3b", 0)], 13: [("t3", 0)], 14: [("gate", 0), ("ln2a", 2)],
    16: [("pick", 0)], 17: [("ln2b", 2)],
    18: [("sumy", 1), ("ln3a", 1)], 19: [("ln3b", 1), ("t2", 2)],
    26: [("sumz", 0), ("ln4a", 0), ("t3", 1)], 27: [("ln4b", 0), ("gate", 1)], 28: [("ln2a", 3)],
    29: [("pick", 1), ("ln2b", 3)],
    34: [("sumy", 2), ("ln3a", 2)], 35: [("ln3b", 2), ("t2", 3)],
    42: [("sumz", 1), ("ln4a", 1), ("t3", 2)], 43: [("ln4b", 1), ("gate", 2)], 45: [("pick", 2)],
    50: [("sumy", 3), ("ln3a", 3)], 51: [("ln3b", 3)], 53: [("t3", 3)], 54: [("gate", 3)],
    56: [("pick", 3)], 58: [("sumz", 2), ("ln4a", 2)], 59: [("ln4b", 2), ("nexta", 0)],
    60: [("nextb", 0), ("nexta", 1)], 61: [("nextt", 0), ("nextb", 1)], 62: [("nextt", 1)],
    66: [("sumz", 3), ("ln4a", 3), ("ln4b", 3)],
}


HEAD = [("ln2a", 0), ("ln2b", 0), ("t2", 0)]
HEAD_LN, HEAD_TURN = 5, 10


def ffn_steps():
    steps = list(HEAD)
    for i in range(ITEMS + LAG + 1):
        steps += BEFORE.get(i, [])
        if i < ITEMS:
            steps.append(("up", i))
        if LAG <= i < ITEMS + LAG:
            steps.append(("down", i - LAG))
    return steps


FFN_STEPS = ffn_steps()


def turn_banks(what, n):
    return slice(4, 6) if (what, n) in HEAD else slice(6, 8)


def input_bank(c):
    return 7 if c == 1 else 6


def max_bank(u):
    return 7 if u < EARLY else 4 + u % 2


def early(c, place):
    return 4 * (c - NA // 2) + place if c >= NA // 2 else None


def max_unit(u):
    g, n = u // NMAX, u % NMAX
    piece, unit = n // UNITS, n % UNITS
    return g, n, GP * g + unit // (2 * NQ), unit // NQ % 2, unit % NQ, piece


LN = {}
for _what, _n in FFN_STEPS:
    if _what in ("ln2a", "ln3a", "ln4a"):
        LN[(_what[:3], _n)] = len(LN)
NLN = len(LN)
SPARE = {s: k for k, s in enumerate(s for s in FFN_STEPS[len(HEAD):] if s[0] in ("oturn", "oproj", "t2", "t3", "gate", "pick"))}
TURNS = {s: k for k, s in enumerate(s for s in FFN_STEPS if s[0] in ("t2", "t3"))}
GELU = {8 * k + f: 8 * sum(w == "M" for w, _ in BLOCKS[:k]) + f
        for k, (w, _) in enumerate(BLOCKS) for f in range(FT) if w == "M"}
RELU = {8 * k + f: 8 * sum(w == "F" for w, _ in BLOCKS[:k]) + f
        for k, (w, _) in enumerate(BLOCKS) for f in range(FT) if w == "F"}
BLOCK_OF = {s: k for k, s in enumerate(BLOCKS)}


def attention_ffn_kernel(nc, x, w_in, b_in, w_out, b_out, w1, b1, w2, b2, ln1_g, ln1_b, ln2_g, ln2_b,
                         gate_W, gate_b, wi_W, wi_b, wo_W, wo_b, lora_A, lora_B, out):
    nc.disable_value_cache = True
    ctx = ExitStack()
    with ctx:
        top = [nc.sbuf_base]

        def place(name, shape, dt, at=None):
            size = 4
            for n in shape[1:]:
                size *= n
            size = -(-size // 32) * 32
            if at is None:
                at = -(-top[0] // 32) * 32
                top[0] = at + size
            return nc.alloc_sbuf_tensor_at(name, shape, dt, offset=at), at + size

        def keep(name, shape, dt=F32):
            return place(name, shape, dt)[0]

        def sem(name):
            return ctx.enter_context(nc.semaphore(name))

        wa = [keep(f"wa{s}", [P, KT, 4 * D], F32R) for s in "hl"]
        wo = [keep(f"wo{s}", [P, KT, D], F32R) for s in "hl"]
        wup = {"M": [keep(f"w1{s}", [P, KT, F], F32R) for s in "hl"],
               "F": [keep(f"wi{s}", [P, KT, F], F32R) for s in "hl"]}
        wdn = {"M": [keep(f"w2{s}", [P, FT, D], F32R) for s in "hl"],
               "F": [keep(f"wf{s}", [P, FT, D], F32R) for s in "hl"]}
        ga = keep("ga", [P, KT, GW], F32R)
        ident = keep("ident", [P, P])
        crow = keep("crow", [P, D])
        gateb = keep("gateb", [P, E])
        rank = keep("rank", [P, E])
        cols = keep("cols", [P, 64])
        vals = keep("vals", [P, NT * H * VW + P])
        stats = keep("stats", [P, CT, 6])
        mv = keep("mv", [P, CT, 2])
        vare = keep("vare", [P, CT])
        rstd = keep("rstd", [P, CT])
        astats = keep("astats", [P, 2, AT, 6])
        amv = keep("amv", [P, 2, AT, 2])
        avare = keep("avare", [P, 2, AT])
        arstd = keep("arstd", [P, 2, AT])
        mhalf = keep("mhalf", [P, CT])
        mx = keep("mx", [P, 2, NMAX])
        negm = keep("negm", [P, UNITS])
        negs = keep("negs", [P, 2 * UNITS])
        mT = keep("mT", [2 * UNITS, P])
        rsum = keep("rsum", [P, NQ, 4])
        xg = keep("xg", [P, NQ, D])
        xn = keep("xn", [P, AT, D])
        kstage = keep("kstage", [P, 2, KT * AW], F32R)
        qstack = keep("qstack", [MROWS, PAIRS, 2, QW], F32R)
        pat = -(-top[0] // 32) * 32
        xin = [place(f"xin{i}", [P, AT, D], F32, pat + 2048 * i)[0] for i in range(XB)]
        xt = [[place(f"xt{i}{s}", [P, KT, AW], F32R, pat + 2048 * XB + 4096 * i + 2048 * k)[0]
               for k, s in enumerate("hl")] for i in range(2)]
        prob = [place(f"prob{i}", [P, 2 * GP, QW], F32, pat + 4096 * i)[0] for i in range(2)]
        ot = [place(f"ot{s}", [P, KT, QW], F32R, pat + 2048 * i)[0] for i, s in enumerate("hl")]
        oraw, _ = place("oraw", [P, QW], F32, pat + 8192)
        otok, _ = place("otok", [P, NQ, D], F32, pat + 9216)
        kat = pat + 2048 * XB + 8192
        kstack, end = place("kstack", [MROWS, PAIRS, T], F32R, kat)
        assert end <= nc.sbuf_usable_end, (end, nc.sbuf_usable_end)
        at = [kat]

        def ffn(name, shape, dt=F32):
            t, at[0] = place(name, shape, dt, at[0])
            assert at[0] <= end, (name, at[0], end)
            return t

        xrow = [ffn(f"xrow{i}", [P, CT, D]) for i in range(2)]
        x1in = ffn("x1in", [P, CT, D])
        bst = ffn("bst", [UROWS, F], F32R)
        srow = [ffn(f"srow{i}", [P, CT, D]) for i in range(2)]
        turned = [[ffn(f"turned{i}{s}", [P, KT, CW], F32R) for s in "hl"] for i in range(2)]
        gel = [ffn(f"gel{i}", [P, CW]) for i in range(2)]
        hid = [[ffn(f"hid{i}{s}", [P, CW], F32R) for s in "hl"] for i in range(RING)]
        ust = ffn("ust", [UROWS, CW], F32R)
        us = ffn("us", [P, CT, UROWS])
        gcopy = ffn("gcopy", [P, CT, GW])
        uall = ffn("uall", [P, CT, E + ER])
        pickm = ffn("pickm", [P, CT])
        picke = ffn("picke", [P, CT, E])
        rows2 = ffn("rows2", [P, 2, D])
        tail = [end - 4 * T * n - 2 * T for n in range(3)]
        qf = [place(f"qf{m}", [P, 2, QW], F32, tail[2] + 2048 * m)[0] for m in range(KT)]
        qstage = [place(f"qstage{m}", [P, 2, 2 * QW], F32R, tail[m])[0] for m in range(KT)]
        at[0] = kat
        nwin = ffn("nwin", [P, 6, D])
        nwout = ffn("nwout", [P, KT, D])
        nw1 = ffn("nw1", [P, FT, D])
        nw2 = ffn("nw2", [P, KT, F])
        nwi = ffn("nwi", [P, FT, D])
        nwo = ffn("nwo", [P, KT, F])
        nga = ffn("nga", [E + ER, D])
        nlb = ffn("nlb", [P, FT, E, R])
        lbs = ffn("lbs", [P, FT, UROWS])
        wibc = ffn("wibc", [P, FT])
        lnb = ffn("lnb", [P, 2, D])
        junk = ffn("junk", [P, D])
        wof = ffn("wof", [P, KT, D])
        cvb = ffn("cvb", [P, KT, P])
        boutr = ffn("boutr", [P, D])
        bsts = ffn("bsts", [UROWS, F], F32R)

        ps = ctx.enter_context(nc.psum_tensor("ps", [P, 8, 512], F32))
        x1_d = nc.dram_tensor("x1_d", [B, P, NQ, STRIDE, D], F32, kind="Internal").ap()
        k_d = nc.dram_tensor("k_d", [NA, 2, KT * P, AW], F32, kind="Internal").ap()
        q_d = nc.dram_tensor("q_d", [KT, 2, P, 2 * QW], F32, kind="Internal").ap()
        bst_d = nc.dram_tensor("bst_d", [UROWS, F], F32, kind="Internal").ap()

        G1, G2, BIN, BINS, B1C, B1S, MASK, QB, LNW = 0, 2, 4, 10, 16, 24, 32, 34, 40

        wload = [sem(f"wload{i}") for i in range(14)]
        p_const, p_ident = sem("p_const"), sem("p_ident")
        d_setup, a_setup, pe_setup = sem("d_setup"), sem("a_setup"), sem("pe_setup")
        xld = [sem(f"xld{i}") for i in range(XB)]
        x1st = [sem(f"x1st{i}") for i in range(XB)]
        x1gst = sem("x1gst")
        stw = [sem(f"stw{i}") for i in range(2)]
        stq = sem("stq")
        kcp = [sem(f"kcp{i}") for i in range(KQ)]
        qcp = sem("qcp")
        mcp = sem("mcp")
        bstw, bstl = sem("bstw"), sem("bstl")
        fld = [sem(f"fld{i}") for i in range(2)]
        rld = sem("rld")
        ost = [sem(f"ost{i}") for i in range(2)]
        astat_done, aaggr_done = sem("astat_done"), sem("aaggr_done")
        avare_done, arstd_done, anorm_done = sem("avare_done"), sem("arstd_done"), sem("anorm_done")
        stat_done, aggr_done = sem("stat_done"), sem("aggr_done")
        vare_done, rstd_done, norm_done = sem("vare_done"), sem("rstd_done"), sem("norm_done")
        ones_done = sem("ones_done")
        xc_done = sem("xc_done")
        ta_done, tah_done, tal_done = sem("ta_done"), sem("tah_done"), sem("tal_done")
        kmm_done, kh_done, kl_done = sem("kmm_done"), sem("kh_done"), sem("kl_done")
        vmm_done, vcp_done, x1_done = sem("vmm_done"), sem("vcp_done"), sem("x1_done")
        qmm_done, qf_done, qh_done, ql_done = sem("qmm_done"), sem("qf_done"), sem("qh_done"), sem("ql_done")
        maxmm_done, maxr_done, negm_done, negs_done = (
            sem("maxmm_done"), sem("maxr_done"), sem("negm_done"), sem("negs_done"))
        mturn_done, mt_done = sem("mturn_done"), sem("mt_done")
        score_done, exp_done, av_done = sem("score_done"), sem("exp_done"), sem("av_done")
        oraw_done, oturn_done, rsum_done, otok_done = (
            sem("oraw_done"), sem("oturn_done"), sem("rsum_done"), sem("otok_done"))
        ott_done, oth_done, otl_done, oproj_done, x1g_done = (
            sem("ott_done"), sem("oth_done"), sem("otl_done"), sem("oproj_done"), sem("x1g_done"))
        res_done, resb_done, x3w_done = sem("res_done"), sem("resb_done"), sem("x3w_done")
        turn_done, turnh_done, turnl_done = sem("turn_done"), sem("turnh_done"), sem("turnl_done")
        up_done, down_done = sem("up_done"), sem("down_done")
        gelu_done, gh_done, gl_done = sem("gelu_done"), sem("gh_done"), sem("gl_done")
        rh_done, rl_done = sem("rh_done"), sem("rl_done")
        sumy_done, sumz_done = sem("sumy_done"), sem("sumz_done")
        gate_done, gatec_done, pick_done = sem("gate_done"), sem("gatec_done"), sem("pick_done")
        pickt_done, ust_done = sem("pickt_done"), sem("ust_done")

        x_v = x.rearrange("b (p t j) d -> b p t j d", t=2, j=STRIDE)
        o_v = out.rearrange("b (p t j) d -> b p t j d", t=2, j=STRIDE)

        block = ctx.enter_context(nc.Block())

        def setup_groups():
            g = [("wout", 0)]
            g += [("qk", k) for k in range(KT)] + [("vo", k) for k in range(KT)] + [("crow", 0)]
            for w in ("M", "F"):
                g += [("up" + w, i) for i in range(4)] + [("dn" + w, i) for i in range(4)]
            g += [("ga", 0), ("bst", 0), ("bst", 1)]
            return g

        SG = setup_groups()

        def rows_bc(v):
            return v.rearrange("(a d) -> a d", a=1).to_broadcast([P, v.shape[0]])

        @block.sync
        def _(sp):
            sp.dma_start(nwin[:], w_in.rearrange("(m p) d -> p m d", p=P)).then_inc(wload[0], 16)
            sp.dma_start(nwout[:], w_out.rearrange("(m p) d -> p m d", p=P)).then_inc(wload[1], 16)
            sp.dma_start(lnb[:, 0, :], rows_bc(ln1_b)).then_inc(wload[2], 16)
            sp.dma_start(lnb[:, 1, :], rows_bc(ln2_b)).then_inc(wload[2], 16)
            sp.dma_start(boutr[:], rows_bc(b_out)).then_inc(wload[2], 16)
            sp.dma_start(gateb[:], rows_bc(gate_b)).then_inc(wload[2], 16)
            with nc.allow_non_contiguous_dma(reason="vectors turned into columns, once"):
                for t, v, n in ((G1, ln1_g, KT), (G2, ln2_g, KT), (BIN, b_in, 6), (B1C, b1, FT)):
                    sp.dma_start(cols[:, t:t + n], v.rearrange("(m p) -> p m", p=P)).then_inc(wload[3], 16)
                sp.dma_start(wibc[:], wi_b.rearrange("(m p) -> p m", p=P)).then_inc(wload[3], 16)
            sp.dma_start(nw1[:], w1.rearrange("(m p) d -> p m d", p=P)).then_inc(wload[4], 16)
            sp.dma_start(nw2[:], w2.rearrange("(m p) f -> p m f", p=P)).then_inc(wload[5], 16)
            sp.dma_start(nwi[:], wi_W.rearrange("(m p) d -> p m d", p=P)).then_inc(wload[6], 16)
            sp.dma_start(nwo[:], wo_W.rearrange("(m p) f -> p m f", p=P)).then_inc(wload[7], 16)
            sp.dma_start(nga[0:E], gate_W).then_inc(wload[8], 16)
            sp.dma_start(nga[E:E + ER], lora_A.rearrange("e r d -> (e r) d")).then_inc(wload[8], 16)
            for e in range(E):
                sp.dma_start(nlb[:, :, e, :], lora_B[e].rearrange("(m p) r -> p m r", p=P)).then_inc(wload[9], 16)

            sp.wait_ge(a_setup, A_SETUP)
            sp.dma_start(bst_d, bsts[:].bitcast(F32)).then_inc(bstw, 16)
            for s in [*xld, *x1st, x1gst, *stw, stq, *kcp, qcp, mcp, *fld, rld, bstl, *ost]:
                sp.sem_inc(s, 1)
            for c in range(2):
                sp.dma_start(xin[c][:], x_v[0, :, :, c, :]).then_inc(xld[c], 16)

            with sp.Fori(2, B + 2) as turn:
                b = turn - 2

                def k_stack(c):
                    sp.wait_ge(stw[c % 2], 1 + b * 8 * NA + 16 * (c // 2 + 1))
                    for blk, part in enumerate((0, 1, 0)):
                        sp.dma_start(kstack[PR * blk:PR * (blk + 1), :, AW * c:AW * (c + 1)].bitcast(F32),
                                     k_d[c, part].rearrange("(a r) n -> r a n", r=PR)).then_inc(kcp[c * KQ // NA], 16)

                sp.dma_start(xin[2][:], x_v[b, :, :, 2, :]).then_inc(xld[2], 16)
                for c in range(NA):
                    if c and c + 2 < NA:
                        i = (c + 2) % XB
                        if c == 1:
                            sp.wait_ge(xc_done, 1 + b * NA + 1)
                        else:
                            sp.wait_ge(x1st[i], 1 + b * 16 * X1S[i] + 16 * ((c - 1) // XB + (i > 0)))
                        sp.dma_start(xin[i][:], x_v[b, :, :, c + 2, :]).then_inc(xld[i], 16)
                    sp.wait_ge(kh_done, 1 + b * NA * KT + KT * (c + 1))
                    sp.wait_ge(kl_done, 1 + b * NA * KT + KT * (c + 1))
                    if c == 0:
                        for i in range(KQ):
                            sp.wait_ge(kcp[i], 1 + b * KCP)
                    sp.dma_start(k_d[c].rearrange("h (m p) n -> p (h m) n", p=P),
                                 kstage[:].rearrange("p h (m n) -> p (h m) n", m=KT).bitcast(F32)
                                 ).then_inc(stw[c % 2], 16)
                    if c:
                        sp.wait_ge(x1_done, 1 + b * (NA - 1) + c)
                        sp.dma_start(x1_d[b, :, :, c, :], xin[c % XB][:]).then_inc(x1st[c % XB], 16)
                    if c == 1:
                        for i in range(2):
                            sp.wait_ge(ost[i], 1 + b * 32)
                        sp.wait_ge(ust_done, 1 + b * NC)
                        sp.wait_ge(pe_setup, len(SG))
                        sp.wait_ge(d_setup, D_SETUP)
                        sp.wait_ge(bstw, 16)
                    if c:
                        k_stack(c - 1)
                    if c == 1:
                        sp.wait_ge(qh_done, 1 + b * 2 * KT + 2 * KT)
                        sp.wait_ge(ql_done, 1 + b * KT + KT)
                        sp.wait_ge(qcp, 1 + b * 48 * KT)
                        for m in range(KT):
                            sp.dma_start(q_d[m].rearrange("h p n -> p h n"), qstage[m][:].bitcast(F32)).then_inc(stq, 16)
                    if c in (2, 3):
                        m = c - 2
                        if m == 0:
                            sp.wait_ge(stq, 1 + b * 16 * KT + 16 * KT)
                            sp.wait_ge(score_done, 1 + b * STEPS)
                        for blk, part in enumerate((0, 0, 1)):
                            sp.dma_start(
                                qstack[PR * blk:PR * (blk + 1), 4 * m:4 * m + 4, :, :].rearrange(
                                    "r a e q -> r a (e q)").bitcast(F32),
                                q_d[m, part].rearrange("(a r) n -> r a n", r=PR)).then_inc(qcp, 16)
                k_stack(NA - 1)
                for g in range(GROUPS):
                    sp.wait_ge(mt_done, 1 + b * GROUPS + g + 1)
                    for h in range(2):
                        sp.dma_start(
                            qstack[SROWS + h:SROWS + h + 1, GP * g:GP * (g + 1), :, :].rearrange(
                                "p a e q -> p (a e q)").rearrange("p (u q) -> p u q", q=P).bitcast(F32),
                            mT[UNITS * h:UNITS * (h + 1), :]).then_inc(mcp, 16)

                sp.wait_ge(score_done, 1 + b * STEPS + STEPS - NT)
                sp.wait_ge(maxmm_done, 1 + b * GROUPS * NMAX + GROUPS * NMAX)
                sp.wait_ge(ones_done, 1 + b * 2 + 2)
                for n in range(NC):
                    c = ORDER[n]
                    if n >= 2:
                        sp.wait_ge(sumy_done, 1 + b * 2 * NC + 2 * (n - 1))
                    sp.dma_start(xrow[n % 2][:].rearrange("p (t j) d -> p t j d", t=2),
                                 x_v[b, :, :, 2 * c:2 * c + 2, :]).then_inc(fld[n % 2], 16)
                    if n == 0:
                        for i in range(XB):
                            sp.wait_ge(x1st[i], 1 + b * 16 * X1S[i] + 16 * X1S[i])
                    else:
                        sp.wait_ge(turn_done, 1 + b * 2 * NC + TURNS[("t2", n - 1)] + 1)
                    if n == NC - 1:
                        sp.wait_ge(x1gst, 1 + b * 16 + 16)
                    sp.dma_start(x1in[:].rearrange("p (t j) d -> p t j d", t=2),
                                 x1_d[b, :, :, 2 * c:2 * c + 2, :]).then_inc(fld[n % 2], 16)
                    if n == 0:
                        sp.dma_start(bst[:].bitcast(F32), bst_d).then_inc(bstl, 16)
                        sp.wait_ge(score_done, 1 + b * STEPS + STEPS)
                        sp.dma_start(rows2[:, 0, :], rows_bc(b2)).then_inc(rld, 16)
                        sp.dma_start(rows2[:, 1, :], rows_bc(wo_b)).then_inc(rld, 16)
                    if n == 1:
                        sp.wait_ge(x1g_done, 1 + b * NQ + NQ)
                        sp.dma_start(x1_d[b, :, :, 0, :], xg[:]).then_inc(x1gst, 16)
                for c in range(2):
                    sp.dma_start(xin[c][:], x_v[(b + 1) % B, :, :, c, :]).then_inc(xld[c], 16)
                for n in range(NC):
                    c = ORDER[n]
                    sp.wait_ge(norm_done, 1 + b * NLN * CT + CT * (LN[("ln4", n)] + 1))
                    sp.dma_start(o_v[b, :, :, 2 * c:2 * c + 2, :],
                                 srow[n % 2][:].rearrange("p (t j) d -> p t j d", t=2)).then_inc(ost[n % 2], 16)
            for i in range(2):
                sp.wait_ge(ost[i], 1 + B * 32)
            for i in range(XB):
                sp.wait_ge(x1st[i], 1 + B * 16 * X1S[i])
                sp.wait_ge(xld[i], 1 + B * 16 * XLD[i] + (16 if i < 2 else 0))
            sp.wait_ge(x1gst, 1 + B * 16)

        @block.gpsimd
        def _(pool):
            nc.gpsimd.memset(ident[:], 0.0).then_inc(p_ident, 1)
            nc.gpsimd.memset(vals[:], 1.0).then_inc(p_const, 1)
            nc.gpsimd.memset(mhalf[:], -0.5).then_inc(p_const, 1)
            for e in range(E):
                nc.gpsimd.memset(rank[:, e:e + 1], float(E - e)).then_inc(p_const, 1)
            pool.wait_ge(p_ident, 1)
            nc.gpsimd.affine_select(out=ident[:], in_=ident[:], compare_op=ALU.not_equal, fill=1.0, base=0,
                                    pattern=[[-1, P]], channel_multiplier=1).then_inc(p_ident, 1)
            pool.wait_ge(d_setup, D_SETUP)

            for s in [rstd_done, arstd_done, ones_done, xc_done, res_done, resb_done, x3w_done, gl_done]:
                pool.sem_inc(s, 1)

            def rsqrt_input(b, c):
                pool.wait_ge(avare_done, 1 + b * NA + c + 1)
                nc.gpsimd.tensor_tensor(arstd[:, c % 2, :], avare[:, c % 2, :], mhalf[:, 0:AT],
                                        ALU.pow).then_inc(arstd_done, 1)

            for c in range(2):
                rsqrt_input(0, c)
            written = nc.alloc_register(pool.engine)
            nc.gpsimd.reg_mov(written, 1)
            with pool.Fori(0, B) as b:
                def rsqrt(k):
                    pool.wait_ge(vare_done, 1 + b * NLN + k + 1)
                    nc.gpsimd.tensor_tensor(rstd[:], vare[:], mhalf[:], ALU.pow).then_inc(rstd_done, 1)

                for c in range(NA):
                    pool.wait_ge(anorm_done, 1 + b * NA * AT + AT * (c + 1))
                    if c == 0:
                        pool.wait_ge(x1gst, 1 + b * 16)
                    nc.gpsimd.tensor_tensor((xin[c % XB] if c else xg)[:], xin[c % XB][:],
                                            crow[:, None, :].to_broadcast([P, AT, D]), ALU.add).then_inc(xc_done, 1)
                    if c + 2 < NA:
                        rsqrt_input(b, c + 2)
                for i in range(2):
                    pool.wait_ge(ost[i], 1 + b * 32)
                pool.wait_ge(pe_setup, len(SG))
                pool.wait_ge(bstw, 16)
                pool.wait_ge(xc_done, 1 + b * NA + NA)
                nc.gpsimd.reg_add(written, written, 2)
                for h in range(2):
                    nc.gpsimd.memset(kstack[SROWS:MROWS, 4 * h:4 * h + 4, :].bitcast(F32), 1.0).then_inc(ones_done, 1)
                pool.wait_ge(ones_done, pool.snap(written, min_val=3))

                for what, n in FFN_STEPS:
                    if what in ("ln2a", "ln3a", "ln4a"):
                        rsqrt(LN[(what[:3], n)])
                    if what == "nexta":
                        rsqrt_input(b + 1, n)
                    if what == "ln2a":
                        pool.wait_ge(fld[n % 2], 1 + b * 64 + 32 * (n // 2 + 1))
                        nc.gpsimd.tensor_tensor(xrow[n % 2][:], xrow[n % 2][:], x1in[:], ALU.add).then_inc(res_done, 1)
                        pool.wait_ge(res_done, 1 + b * NC + n + 1)
                        pool.wait_ge(rld, 1 + b * 32 + 32)
                        nc.gpsimd.tensor_tensor(xrow[n % 2][:], xrow[n % 2][:],
                                                rows2[:, 0:1, :].to_broadcast([P, CT, D]), ALU.add).then_inc(resb_done, 1)
                    if what == "t3":
                        pool.wait_ge(turn_done, 1 + b * 2 * NC + TURNS[(what, n)] + 1)
                        nc.gpsimd.tensor_tensor(srow[n % 2][:], srow[n % 2][:],
                                                rows2[:, 1:2, :].to_broadcast([P, CT, D]), ALU.add).then_inc(x3w_done, 1)
                    if what == "up" and n in GELU:
                        k = GELU[n]
                        pool.wait_ge(gh_done, 1 + b * NC * FT + k + 1)
                        nc.gpsimd.tensor_tensor(hid[n % RING][1][:], gel[k % 2][:], hid[n % RING][0][:],
                                                ALU.subtract).then_inc(gl_done, 1)

        @block.scalar
        def _(act):
            for k, (what, i) in enumerate(SG):
                act.wait_ge(pe_setup, k + 1)
                bank = ps[:, k % 8, :]
                if what == "wout":
                    nc.scalar.activation(wof[:].rearrange("p k d -> p (k d)"), bank, ACT.Copy).then_inc(a_setup, 1)
                    act.wait_ge(a_setup, 1)
                    nc.scalar.activation(wo[0][:].rearrange("p k d -> p (k d)"), bank, ACT.Copy).then_inc(a_setup, 1)
                elif what == "qk":
                    act.wait_ge(wload[3], 16 * 5)
                    nc.scalar.activation(wa[0][:, i, 0:512], bank, ACT.Copy, scale=cols[:, G1 + i:G1 + i + 1]
                                         ).then_inc(a_setup, 1)
                elif what == "vo":
                    nc.scalar.activation(wa[0][:, i, 512:1024], bank, ACT.Copy, scale=cols[:, G1 + i:G1 + i + 1]
                                         ).then_inc(a_setup, 1)
                elif what in ("upM", "upF"):
                    kt, half = i // 2, i % 2
                    s = cols[:, G2 + kt:G2 + kt + 1] if what == "upM" else 1.0
                    nc.scalar.activation(wup[what[2]][0][:, kt, 512 * half:512 * half + 512], bank, ACT.Copy,
                                         scale=s).then_inc(a_setup, 1)
                elif what in ("dnM", "dnF"):
                    nc.scalar.activation(wdn[what[2]][0][:, 2 * i:2 * i + 2, :].rearrange("p k d -> p (k d)"), bank,
                                         ACT.Copy).then_inc(a_setup, 1)
                elif what == "ga":
                    act.wait_ge(p_const, 2 + E)
                    nc.scalar.activation(ga[:, :, 0:E + ER], ps[:, k % 8, 0:2 * (E + ER)].rearrange(
                        "p (k n) -> p k n", k=KT), ACT.Copy).then_inc(a_setup, 1)
                elif what == "bst":
                    nc.scalar.activation(bsts[:, 512 * i:512 * i + 512], ps[0:UROWS, k % 8, :], ACT.Copy
                                         ).then_inc(a_setup, 1)

            for s in [tah_done, kh_done, vcp_done, mt_done, exp_done, oth_done, turnh_done, gelu_done, rh_done,
                      ust_done, qh_done]:
                act.sem_inc(s, 1)

            def turned_high(b, c):
                act.wait_ge(ta_done, 1 + b * NA + c + 1)
                if c >= 2:
                    act.wait_ge(vmm_done, 1 + b * NA + c - 1)
                elif c == 0:
                    act.wait_ge(oproj_done, 1 + b)
                nc.scalar.activation(xt[c % 2][0][:].rearrange("p k n -> p (k n)"), ps[:, input_bank(c), :],
                                     ACT.Copy).then_inc(tah_done, 1)

            for c in range(2):
                turned_high(0, c)
            with act.Fori(0, B) as b:
                for c in range(NA):
                    act.wait_ge(kmm_done, 1 + b * NA + c + 1)
                    act.wait_ge(stw[(c + 1) % 2], 1 + b * 8 * NA + 16 * ((c + 1) // 2))
                    for m in range(KT):
                        nc.scalar.activation(kstage[:, 0, AW * m:AW * (m + 1)], ps[:, c % 2, AW * m:AW * (m + 1)],
                                             ACT.Identity, bias=cols[:, BIN + KT + m:BIN + KT + m + 1]).then_inc(kh_done, 1)
                    act.wait_ge(vmm_done, 1 + b * NA + c + 1)
                    if c == 0:
                        act.wait_ge(av_done, 1 + b * STEPS)
                        act.wait_ge(p_const, 2 + E)
                    v0 = 2 + 2 * (c % 2)
                    nc.scalar.activation(
                        vals[:, AT * c * H * VW:AT * (c + 1) * H * VW].rearrange("p (h v) -> p h v", v=VW)[:, :, 0:HD],
                        ps[:, v0:v0 + 2, 0:D].rearrange("p t (h v) -> p t h v", v=HD), ACT.Copy).then_inc(vcp_done, 1)
                    if c == 0:
                        act.wait_ge(qmm_done, 1 + b + 1)
                        act.wait_ge(bstw, 16)
                        for m in range(KT):
                            for e in range(2):
                                nc.scalar.activation(
                                    qstage[m][:, 0, QW * e:QW * (e + 1)], ps[:, 4 + m, 0:QW], ACT.Identity,
                                    scale=cols[:, MASK + e:MASK + e + 1],
                                    bias=cols[:, QB + 2 * m + e:QB + 2 * m + e + 1]).then_inc(qh_done, 1)
                    if c + 2 < NA:
                        turned_high(b, c + 2)

                def turn_max(g):
                    act.wait_ge(mturn_done, 1 + b * GROUPS + g + 1)
                    act.wait_ge(mcp, 1 + b * 32 * GROUPS + 32 * g)
                    nc.scalar.activation(mT[:], ps[0:2 * UNITS, 7, 0:P], ACT.Copy).then_inc(mt_done, 1)

                def ffn_step(what, n):
                    if what in ("t2", "t3"):
                        k = TURNS[(what, n)]
                        blk = BLOCK_OF[("M" if what == "t2" else "F", n)]
                        act.wait_ge(turn_done, 1 + b * 2 * NC + k + 1)
                        if blk >= 2:
                            act.wait_ge(up_done, 1 + b * ITEMS + 8 * (blk - 1))
                        nc.scalar.activation(turned[blk % 2][0][:], ps[:, turn_banks(what, n), :], ACT.Copy).then_inc(turnh_done, 1)
                    elif what == "nextt":
                        turned_high(b + 1, n)
                    elif what == "oproj":
                        act.wait_ge(ott_done, 1 + b + 1)
                        nc.scalar.activation(ot[0][:].rearrange("p k q -> p (k q)"), ps[:, 7, :],
                                             ACT.Copy).then_inc(oth_done, 1)
                    elif what == "pick":
                        act.wait_ge(pickt_done, 1 + b * NC + n + 1)
                        if n:
                            act.wait_ge(up_done, 1 + b * ITEMS + 8 * (BLOCK_OF[("F", n - 1)] + 1))
                        nc.scalar.activation(ust[:], ps[0:UROWS, 6, :], ACT.Copy).then_inc(ust_done, 1)
                    elif what == "up":
                        act.wait_ge(up_done, 1 + b * ITEMS + n + 1)
                        if n in GELU:
                            k, f = GELU[n], n % FT
                            if k >= 2:
                                act.wait_ge(gl_done, 1 + b * NC * FT + k - 1)
                            nc.scalar.activation(gel[k % 2][:], ps[:, n % 2, :], ACT.Gelu,
                                                 bias=cols[:, B1C + f:B1C + f + 1]).then_inc(gelu_done, 1)
                        else:
                            if n >= RING:
                                act.wait_ge(down_done, 1 + b * ITEMS + n - RING + 1)
                            nc.scalar.activation(hid[n % RING][0][:], ps[:, n % 2, :], ACT.Relu).then_inc(rh_done, 1)

                turn_max(0)
                for i in range(XB):
                    act.wait_ge(x1st[i], 1 + b * 16 * X1S[i] + 16 * X1S[i])
                for s in range(STEPS):
                    act.wait_ge(score_done, 1 + b * STEPS + s + 1)
                    if s >= 2:
                        act.wait_ge(av_done, 1 + b * STEPS + s - 1)
                    nc.scalar.activation(prob[s % 2][:].rearrange("p h q -> p (h q)"),
                                         ps[:, 2 * (s % 2):2 * (s % 2) + 2, :].rearrange("p a n -> p (a n)"),
                                         ACT.Exp).then_inc(exp_done, 1)
                    if s % NT == TURN_MAX and s // NT + 1 < GROUPS:
                        turn_max(s // NT + 1)
                    if s == STEPS - NT + HEAD_TURN:
                        ffn_step("t2", 0)
                for step in FFN_STEPS[len(HEAD):]:
                    ffn_step(*step)

        @block.vector
        def _(dve):
            chain = [0]

            def link(ins, hold=True):
                chain[0] += 1
                ins.then_inc(d_setup, 1)
                if hold:
                    dve.wait_ge(d_setup, chain[0])

            dve.wait_ge(wload[0], 16)
            dve.wait_ge(wload[2], 64)
            dve.wait_ge(wload[3], 80)
            for m in range(6):
                link(nc.vector.tensor_tensor_reduce(out=junk[:], in0=nwin[:, m, :], in1=lnb[:, 0, :], scale=1.0, scalar=0.0,
                                                    op0=ALU.mult, op1=ALU.add, accum_out=cols[:, BINS + m:BINS + m + 1]))
            link(nc.vector.tensor_tensor(cols[:, BIN:BIN + 6], cols[:, BIN:BIN + 6], cols[:, BINS:BINS + 6], ALU.add))
            dve.wait_ge(p_const, 2 + E)
            for k in range(KT):
                link(nc.vector.tensor_scalar(cvb[:, k, :], vals[:, 0:P], cols[:, BIN + 4 + k:BIN + 5 + k], None, ALU.mult))
            assert chain[0] == CVB
            dve.wait_ge(p_ident, 2)
            for e in range(2):
                link(nc.vector.tensor_reduce(cols[:, MASK + e:MASK + e + 1],
                                             ident[:].rearrange("p (a e d) -> p e a d", e=2, d=HD)[:, e],
                                             AX.XY, ALU.add))
            link(nc.vector.tensor_scalar(cols[:, MASK:MASK + 2], cols[:, MASK:MASK + 2], float(HD) ** -0.5, None, ALU.mult))
            for m in range(KT):
                link(nc.vector.tensor_scalar(cols[:, QB + 2 * m:QB + 2 * m + 2], cols[:, MASK:MASK + 2],
                                             cols[:, BIN + m:BIN + m + 1], None, ALU.mult))
            dve.wait_ge(wload[4], 16)
            for m in range(FT):
                link(nc.vector.tensor_tensor_reduce(out=junk[:], in0=nw1[:, m, :], in1=lnb[:, 1, :], scale=1.0, scalar=0.0,
                                                    op0=ALU.mult, op1=ALU.add, accum_out=cols[:, B1S + m:B1S + m + 1]))
            link(nc.vector.tensor_tensor(cols[:, B1C:B1C + FT], cols[:, B1C:B1C + FT], cols[:, B1S:B1S + FT], ALU.add))
            dve.wait_ge(wload[9], 16 * E)
            src = nlb[:].rearrange("p m e r -> p m (e r)")
            link(nc.vector.tensor_copy(lbs[:, :, 0:ER].bitcast(F32R), src))
            link(nc.vector.tensor_copy(lbs[:, :, ER:2 * ER], lbs[:, :, 0:ER]))
            link(nc.vector.tensor_tensor(lbs[:, :, 2 * ER:3 * ER].bitcast(F32R), src, lbs[:, :, 0:ER], ALU.subtract))
            link(nc.vector.tensor_copy(lbs[:, :, 3 * ER].bitcast(F32R), wibc[:]))
            link(nc.vector.tensor_tensor(lbs[:, :, 3 * ER + 1].bitcast(F32R), wibc[:], lbs[:, :, 3 * ER], ALU.subtract))
            assert chain[0] == LBS
            n_act = 0
            for k, (what, i) in enumerate(SG):
                dve.wait_ge(pe_setup, k + 1)
                n_act += {"wout": 2, "crow": 0}.get(what, 1)
                dve.wait_ge(a_setup, max(n_act, 1))
                bank = ps[:, k % 8, :]
                if what == "crow":
                    link(nc.vector.tensor_tensor(crow[:], ps[:, k % 8, 0:D], boutr[:], ALU.add), False)
                elif what == "wout":
                    link(nc.vector.tensor_tensor(wo[1][:].rearrange("p k d -> p (k d)"), bank,
                                                 wo[0][:].rearrange("p k d -> p (k d)"), ALU.subtract), False)
                elif what in ("qk", "vo"):
                    o = 0 if what == "qk" else 512
                    link(nc.vector.scalar_tensor_tensor(out=wa[1][:, i, o:o + 512], in0=bank, scalar=cols[:, G1 + i:G1 + i + 1],
                                                        in1=wa[0][:, i, o:o + 512], op0=ALU.mult, op1=ALU.subtract), False)
                elif what == "upM":
                    kt, o = i // 2, 512 * (i % 2)
                    link(nc.vector.scalar_tensor_tensor(out=wup["M"][1][:, kt, o:o + 512], in0=bank,
                                                        scalar=cols[:, G2 + kt:G2 + kt + 1], in1=wup["M"][0][:, kt, o:o + 512],
                                                        op0=ALU.mult, op1=ALU.subtract), False)
                elif what == "upF":
                    kt, o = i // 2, 512 * (i % 2)
                    link(nc.vector.tensor_tensor(wup["F"][1][:, kt, o:o + 512], bank, wup["F"][0][:, kt, o:o + 512],
                                                 ALU.subtract), False)
                elif what in ("dnM", "dnF"):
                    w = wdn[what[2]]
                    link(nc.vector.tensor_tensor(w[1][:, 2 * i:2 * i + 2, :].rearrange("p k d -> p (k d)"), bank,
                                                 w[0][:, 2 * i:2 * i + 2, :].rearrange("p k d -> p (k d)"), ALU.subtract), False)
                elif what == "ga":
                    link(nc.vector.tensor_tensor(
                        ga[:, :, E + ER:GW], ps[:, k % 8, 0:GW].rearrange("p (k n) -> p k n", k=KT),
                        ga[:, :, 0:E + ER], ALU.subtract), False)
            assert chain[0] == D_SETUP, chain[0]

            for s in [stat_done, aggr_done, vare_done, norm_done, astat_done, aaggr_done, avare_done, anorm_done,
                      tal_done, kl_done, x1_done, qf_done, ql_done, maxr_done, negm_done, negs_done, oraw_done,
                      rsum_done, otok_done, otl_done, x1g_done, turnl_done, gh_done, rl_done, sumy_done, sumz_done,
                      gatec_done, pick_done]:
                dve.sem_inc(s, 1)

            aggregated = nc.alloc_register(dve.engine)
            nc.vector.reg_mov(aggregated, 1)
            aaggregated = nc.alloc_register(dve.engine)
            nc.vector.reg_mov(aaggregated, 1)

            def input_a(b, c):
                i = c % 2
                dve.wait_ge(xld[c % XB], 1 + b * 16 * XLD[c % XB] + 16 * (c // XB + 1))
                for t in range(AT):
                    nc.vector.bn_stats(astats[:, i, t, :], xin[c % XB][:, t, :]).then_inc(astat_done, 1)
                dve.wait_ge(astat_done, 1 + b * NA * AT + AT * (c + 1))
                nc.vector.reg_add(aaggregated, aaggregated, AT)
                for t in range(AT):
                    nc.vector.bn_aggr(amv[:, i, t, :], astats[:, i, t, :]).then_inc(aaggr_done, 1)
                dve.wait_ge(aaggr_done, dve.snap(aaggregated, min_val=AT + 1))
                nc.vector.tensor_scalar(avare[:, i, :], amv[:, i, :, 1], EPS, None, ALU.add).then_inc(avare_done, 1)

            def input_b(b, c):
                i = c % 2
                dve.wait_ge(arstd_done, 1 + b * NA + c + 1)
                dve.wait_ge(ta_done, 1 + b * NA + c)
                for t in range(AT):
                    nc.vector.tensor_scalar(xn[:, t, :], xin[c % XB][:, t, :], amv[:, i, t, 0:1], arstd[:, i, t:t + 1],
                                            ALU.subtract, ALU.mult).then_inc(anorm_done, 1)

            def turned_low(b, c):
                dve.wait_ge(tah_done, 1 + b * NA + c + 1)
                nc.vector.tensor_tensor(xt[c % 2][1][:].rearrange("p k n -> p (k n)"), ps[:, input_bank(c), :],
                                        xt[c % 2][0][:].rearrange("p k n -> p (k n)"), ALU.subtract).then_inc(tal_done, 1)

            for c in range(2):
                input_a(0, c)
                input_b(0, c)
            for c in range(2):
                turned_low(0, c)
            with dve.Fori(0, B) as b:
                def ln_a(k, rows):
                    for i in range(CT):
                        nc.vector.bn_stats(stats[:, i, :], rows[:, i, :]).then_inc(stat_done, 1)
                    dve.wait_ge(stat_done, 1 + b * NLN * CT + CT * (k + 1))
                    dve.wait_ge(norm_done, 1 + b * NLN * CT + CT * k)
                    nc.vector.reg_add(aggregated, aggregated, CT)
                    for i in range(CT):
                        nc.vector.bn_aggr(mv[:, i, :], stats[:, i, :]).then_inc(aggr_done, 1)
                    dve.wait_ge(aggr_done, dve.snap(aggregated, min_val=CT + 1))
                    nc.vector.tensor_scalar(vare[:], mv[:, :, 1], EPS, None, ALU.add).then_inc(vare_done, 1)

                def ln_b(k, dst, rows):
                    dve.wait_ge(rstd_done, 1 + b * NLN + k + 1)
                    for i in range(CT):
                        nc.vector.tensor_scalar(dst[:, i, :], rows[:, i, :], mv[:, i, 0:1], rstd[:, i:i + 1],
                                                ALU.subtract, ALU.mult).then_inc(norm_done, 1)

                def row_max(u):
                    if u is None:
                        return
                    g, n = max_unit(u)[:2]
                    dve.wait_ge(maxmm_done, 1 + b * GROUPS * NMAX + u + 1)
                    if n == 0 and g >= 2:
                        dve.wait_ge(negm_done, 1 + b * GROUPS + g - 1)
                    nc.vector.tensor_reduce(mx[:, g % 2, n:n + 1], ps[:, max_bank(u), :], AX.X, ALU.max).then_inc(maxr_done, 1)
                    if n == NMAX - 1:
                        dve.wait_ge(maxr_done, 1 + b * GROUPS * NMAX + u + 1)
                        if g:
                            dve.wait_ge(negs_done, 1 + b * 2 * GROUPS + 2 * g)
                        nc.vector.tensor_reduce(negm[:], mx[:, g % 2, :].rearrange("p (k u) -> p u k", k=KQ), AX.X, ALU.max,
                                                negate=True).then_inc(negm_done, 1)
                        dve.wait_ge(negm_done, 1 + b * GROUPS + g + 1)
                        dve.wait_ge(mturn_done, 1 + b * GROUPS + g)
                        nc.vector.tensor_copy(negs[:, 0:UNITS].bitcast(F32R), negm[:]).then_inc(negs_done, 1)
                        dve.wait_ge(negs_done, 1 + b * 2 * GROUPS + 2 * g + 1)
                        nc.vector.tensor_tensor(negs[:, UNITS:].bitcast(F32R), negm[:], negs[:, 0:UNITS],
                                                ALU.subtract).then_inc(negs_done, 1)

                for c in range(NA):
                    for m in range(KT):
                        dve.wait_ge(kh_done, 1 + b * NA * KT + KT * (c + 1))
                        nc.vector.scalar_tensor_tensor(
                            out=kstage[:, 1, AW * m:AW * (m + 1)], in0=ps[:, c % 2, AW * m:AW * (m + 1)],
                            scalar=cols[:, BIN + KT + m:BIN + KT + m + 1], in1=kstage[:, 0, AW * m:AW * (m + 1)],
                            op0=ALU.add, op1=ALU.subtract).then_inc(kl_done, 1)
                    row_max(early(c, 0))
                    if c + 2 < NA:
                        input_a(b, c + 2)
                    row_max(early(c, 1))
                    if c:
                        dve.wait_ge(xc_done, 1 + b * NA + c + 1)
                        dve.wait_ge(vcp_done, 1 + b * NA + c + 1)
                        v0 = 2 + 2 * (c % 2)
                        nc.vector.tensor_tensor(xin[c % XB][:], xin[c % XB][:], ps[:, v0:v0 + 2, D:2 * D],
                                                ALU.add).then_inc(x1_done, 1)
                    row_max(early(c, 2))
                    if c + 2 < NA:
                        input_b(b, c + 2)
                    if c == 0:
                        dve.wait_ge(bstw, 16)
                        for m in range(KT):
                            dve.wait_ge(qh_done, 1 + b * 2 * KT + 2 * (m + 1))
                            for e in range(2):
                                nc.vector.tensor_scalar(
                                    qf[m][:, e, :], ps[:, 4 + m, 0:QW], cols[:, MASK + e:MASK + e + 1],
                                    cols[:, QB + 2 * m + e:QB + 2 * m + e + 1], ALU.mult, ALU.add).then_inc(qf_done, 1)
                            dve.wait_ge(qf_done, 1 + b * 2 * KT + 2 * (m + 1))
                            nc.vector.tensor_tensor(qstage[m][:, 1, :], qf[m][:].rearrange("p e q -> p (e q)"),
                                                    qstage[m][:, 0, :], ALU.subtract).then_inc(ql_done, 1)
                    if c + 2 < NA:
                        turned_low(b, c + 2)
                    row_max(early(c, 3))

                def out_raw(g):
                    dve.wait_ge(av_done, 1 + b * STEPS + NT * (g + 1))
                    dve.wait_ge(oturn_done, 1 + b * GROUPS + g)
                    nc.vector.tensor_copy(oraw[:], ps[:, 6, 0:QW]).then_inc(oraw_done, 1)

                def out_norm(g):
                    dve.wait_ge(oturn_done, 1 + b * GROUPS + g + 1)
                    if g:
                        dve.wait_ge(otok_done, 1 + b * GROUPS * NQ + NQ * g)
                    turned_o = ps[:, 7, 0:NQ * P].rearrange("p (t h v) -> p t h v", t=NQ, h=4)
                    nc.vector.reciprocal(rsum[:], turned_o[:, :, :, HD]).then_inc(rsum_done, 1)
                    dve.wait_ge(rsum_done, 1 + b * GROUPS + g + 1)
                    for t in range(NQ):
                        nc.vector.tensor_tensor(
                            otok[:, t, 4 * HD * g:4 * HD * (g + 1)].rearrange("p (h v) -> p h v", h=4),
                            turned_o[:, t, :, 0:HD], rsum[:, t, :, None].to_broadcast([P, 4, HD]),
                            ALU.mult).then_inc(otok_done, 1)

                def ffn_step(what, n):
                    if what == "ln2a":
                        dve.wait_ge(fld[n % 2], 1 + b * 64 + 32 * (n // 2 + 1))
                        ln_a(LN[("ln2", n)], x1in)
                    elif what == "ln2b":
                        dve.wait_ge(res_done, 1 + b * NC + n + 1)
                        ln_b(LN[("ln2", n)], x1in, x1in)
                    elif what == "onorm":
                        out_norm(GROUPS - 1)
                    elif what == "oproj":
                        dve.wait_ge(oth_done, 1 + b + 1)
                        nc.vector.tensor_tensor(ot[1][:].rearrange("p k q -> p (k q)"), ps[:, 7, :],
                                                ot[0][:].rearrange("p k q -> p (k q)"), ALU.subtract).then_inc(otl_done, 1)
                        dve.wait_ge(oproj_done, 1 + b + 1)
                        for t in range(NQ):
                            nc.vector.tensor_tensor(xg[:, t, :], xg[:, t, :], ps[:, 6, D * t:D * t + D],
                                                    ALU.add).then_inc(x1g_done, 1)
                    elif what == "nexta":
                        input_a(b + 1, n)
                    elif what == "nextb":
                        input_b(b + 1, n)
                    elif what == "nextt":
                        turned_low(b + 1, n)
                    elif what == "ln3a":
                        dve.wait_ge(sumy_done, 1 + b * 2 * NC + 2 * (n + 1))
                        ln_a(LN[("ln3", n)], srow[n % 2])
                    elif what == "ln3b":
                        ln_b(LN[("ln3", n)], srow[n % 2], srow[n % 2])
                    elif what == "ln4a":
                        dve.wait_ge(sumz_done, 1 + b * 2 * NC + 2 * (n + 1))
                        ln_a(LN[("ln4", n)], srow[n % 2])
                    elif what == "ln4b":
                        ln_b(LN[("ln4", n)], srow[n % 2], srow[n % 2])
                    elif what in ("t2", "t3"):
                        k = TURNS[(what, n)]
                        blk = BLOCK_OF[("M" if what == "t2" else "F", n)]
                        dve.wait_ge(turnh_done, 1 + b * 2 * NC + k + 1)
                        nc.vector.tensor_tensor(turned[blk % 2][1][:], ps[:, turn_banks(what, n), :], turned[blk % 2][0][:],
                                                ALU.subtract).then_inc(turnl_done, 1)
                    elif what == "sumy":
                        dve.wait_ge(down_done, 1 + b * ITEMS + 8 * (BLOCK_OF[("M", n)] + 1))
                        dve.wait_ge(resb_done, 1 + b * NC + n + 1)
                        if n >= 2:
                            dve.wait_ge(ost[n % 2], 1 + b * 32 + 16)
                        for h in range(2):
                            nc.vector.tensor_tensor(
                                srow[n % 2][:, 2 * h:2 * h + 2, :].rearrange("p t d -> p (t d)"),
                                xrow[n % 2][:, 2 * h:2 * h + 2, :].rearrange("p t d -> p (t d)"), ps[:, 2 + h, :],
                                ALU.add).then_inc(sumy_done, 1)
                    elif what == "sumz":
                        dve.wait_ge(down_done, 1 + b * ITEMS + 8 * (BLOCK_OF[("F", n)] + 1))
                        dve.wait_ge(x3w_done, 1 + b * NC + n + 1)
                        for h in range(2):
                            rows = srow[n % 2][:, 2 * h:2 * h + 2, :].rearrange("p t d -> p (t d)")
                            nc.vector.tensor_tensor(rows, rows, ps[:, 4 + h, :], ALU.add).then_inc(sumz_done, 1)
                    elif what == "gate":
                        dve.wait_ge(gate_done, 1 + b * NC + n + 1)
                        nc.vector.tensor_copy(gcopy[:].rearrange("p (a t) g -> p a t g", a=2),
                                              ps[:, 6:8, :].rearrange("p a (t g) -> p a t g", t=2)[:, :, :, 0:GW]
                                              ).then_inc(gatec_done, 1)
                        dve.wait_ge(gatec_done, 1 + b * NC + n + 1)
                        steps = [1 + b * NPICK * NC + NPICK * n]

                        def then(ins, steps=steps):
                            ins.then_inc(pick_done, 1)
                            steps[0] = steps[0] + 1
                            dve.wait_ge(pick_done, steps[0])

                        then(nc.vector.tensor_tensor(uall[:], gcopy[:, :, 0:E + ER], gcopy[:, :, E + ER:GW], ALU.add))
                        logits = uall[:, :, 0:E]
                        then(nc.vector.tensor_tensor(logits, logits, gateb[:, None, :].to_broadcast([P, CT, E]), ALU.add))
                        then(nc.vector.tensor_reduce(pickm[:], logits, AX.X, ALU.max))
                        top_of = pickm[:, :, None].to_broadcast([P, CT, E])
                        then(nc.vector.tensor_tensor(picke[:], logits, top_of, ALU.is_equal))
                        then(nc.vector.tensor_tensor(picke[:], picke[:], rank[:, None, :].to_broadcast([P, CT, E]), ALU.mult))
                        then(nc.vector.tensor_reduce(pickm[:], picke[:], AX.X, ALU.max))
                        then(nc.vector.tensor_tensor(picke[:], picke[:], top_of, ALU.is_equal))
                        u4 = uall[:, :, E:].rearrange("p t (e r) -> p t e r", r=R)
                        then(nc.vector.tensor_tensor(u4, u4, picke[:, :, :, None].to_broadcast([P, CT, E, R]), ALU.mult))
                        u2 = uall[:, :, E:]
                        if n:
                            dve.wait_ge(pickt_done, 1 + b * NC + n)
                        then(nc.vector.tensor_copy(us[:, :, 0:ER].bitcast(F32R), u2))
                        then(nc.vector.tensor_tensor(us[:, :, ER:2 * ER].bitcast(F32R), u2, us[:, :, 0:ER], ALU.subtract))
                        then(nc.vector.tensor_copy(us[:, :, 2 * ER:3 * ER], us[:, :, 0:ER]))
                        then(nc.vector.memset(us[:, :, 3 * ER:], 1.0))
                    elif what == "up":
                        if n >= RING:
                            dve.wait_ge(down_done, 1 + b * ITEMS + n - RING + 1)
                        if n in GELU:
                            k = GELU[n]
                            dve.wait_ge(gelu_done, 1 + b * NC * FT + k + 1)
                            nc.vector.tensor_copy(hid[n % RING][0][:], gel[k % 2][:]).then_inc(gh_done, 1)
                        else:
                            dve.wait_ge(rh_done, 1 + b * NC * FT + RELU[n] + 1)
                            nc.vector.scalar_tensor_tensor(out=hid[n % RING][1][:], in0=ps[:, n % 2, :], scalar=0.0,
                                                           in1=hid[n % RING][0][:], op0=ALU.max, op1=ALU.subtract
                                                           ).then_inc(rl_done, 1)

                for u in range(EARLY, LEAD):
                    row_max(u)
                u = LEAD
                for s in range(STEPS):
                    for _ in range(2):
                        if u < GROUPS * NMAX:
                            row_max(u)
                            u += 1
                    g, k = s // NT, s % NT
                    if g and k == OUT_TURN:
                        out_norm(g - 1)
                    if s == STEPS - NT + HEAD_LN:
                        ffn_step("ln2a", 0)
                        ffn_step("ln2b", 0)
                    if s == STEPS - NT + HEAD_TURN:
                        ffn_step("t2", 0)
                    if k == NT - 1:
                        out_raw(g)
                for step in FFN_STEPS[len(HEAD):]:
                    ffn_step(*step)

        @block.tensor
        def _(pe):
            mm = nc.tensor.matmul

            def three(o, l, r, start, stop, part=None):
                mm(o, l[0], r[0], start=start, stop=False, skip_group_check=True)
                mm(o, l[0], r[1], start=False, stop=False, skip_group_check=True)
                return mm(o, l[1], r[0], start=False, stop=stop, skip_group_check=True)

            pe.wait_ge(p_ident, 2)
            n_a = n_d = 0
            freed = []
            for k, (what, i) in enumerate(SG):
                if k >= 8:
                    pe.wait_ge(a_setup, freed[k - 8][0])
                    pe.wait_ge(d_setup, LBS + freed[k - 8][1])
                n_a += {"wout": 2, "crow": 0}.get(what, 1)
                n_d += what != "bst"
                freed.append((n_a, n_d))
                o = ps[:, k % 8, :]

                def turn(col, src, rows=P, n=P):
                    return nc.tensor.transpose(o[0:n, col:col + rows], src, ident[0:rows, 0:rows])

                if what == "wout":
                    pe.wait_ge(wload[1], 16)
                    for f in range(KT):
                        for m in range(KT):
                            last = turn(D * f + P * m, nwout[:, m, P * f:P * f + P])
                elif what == "qk":
                    pe.wait_ge(wload[0], 16)
                    for m in range(4):
                        last = turn(P * m, nwin[:, m, P * i:P * i + P])
                elif what == "vo":
                    pe.wait_ge(a_setup, 1)
                    for m in range(2):
                        turn(P * m, nwin[:, 4 + m, P * i:P * i + P])
                    for m in range(2):
                        last = mm(o[:, D:2 * D], nwin[:, 4 + m, P * i:P * i + P], wof[:, m, :], start=m == 0, stop=m == 1)
                elif what == "crow":
                    pe.wait_ge(d_setup, CVB)
                    for m in range(KT):
                        last = mm(o[:, 0:D], cvb[:, m, :], wof[:, m, :], start=m == 0, stop=m == 1)
                elif what in ("upM", "upF"):
                    pe.wait_ge(wload[4 if what == "upM" else 6], 16)
                    w = nw1 if what == "upM" else nwi
                    kt, half = i // 2, i % 2
                    for m in range(4):
                        last = turn(P * m, w[:, 4 * half + m, P * kt:P * kt + P])
                elif what in ("dnM", "dnF"):
                    pe.wait_ge(wload[5 if what == "dnM" else 7], 16)
                    w = nw2 if what == "dnM" else nwo
                    for f in range(2):
                        for m in range(2):
                            last = turn(D * f + P * m, w[:, m, P * (2 * i + f):P * (2 * i + f) + P])
                elif what == "ga":
                    pe.wait_ge(wload[8], 32)
                    for m in range(KT):
                        last = turn((E + ER) * m, nga[:, P * m:P * m + P], rows=E + ER)
                elif what == "bst":
                    pe.wait_ge(d_setup, LBS)
                    for m in range(4):
                        last = turn(P * m, lbs[:, 4 * i + m, :], n=UROWS)
                last.then_inc(pe_setup, 1)
            pe.wait_ge(a_setup, A_SETUP)
            pe.wait_ge(d_setup, D_SETUP)

            for s in [ta_done, kmm_done, vmm_done, qmm_done, maxmm_done, mturn_done, score_done, av_done,
                      oturn_done, ott_done, oproj_done, turn_done, up_done, down_done, gate_done, pickt_done]:
                pe.sem_inc(s, 1)

            def turn_input(b, c):
                pe.wait_ge(anorm_done, 1 + b * NA * AT + AT * (c + 1))
                if c >= 2:
                    pe.wait_ge(tal_done, 1 + b * NA + c)
                for k in range(KT):
                    for i in range(AT):
                        last = nc.tensor.transpose(ps[:, input_bank(c), AW * k + P * i:AW * k + P * i + P],
                                                   xn[:, i, P * k:P * k + P], ident[:])
                last.then_inc(ta_done, 1)

            for c in range(2):
                turn_input(0, c)
            with pe.Fori(0, B) as b:
                def score_max(u):
                    g, n, pair, e, t, piece = max_unit(u)
                    if u == 0:
                        pe.wait_ge(qcp, 1 + b * 48 * KT + 48 * KT)
                    if g == 0 and n % UNITS == 0:
                        pe.wait_ge(kcp[piece], 1 + b * KCP + KCP)
                    if u == EARLY:
                        pe.wait_ge(x1_done, 1 + b * (NA - 1) + NA - 1)
                        pe.wait_ge(vcp_done, 1 + b * NA + NA)
                    elif 0 < u < EARLY:
                        pe.wait_ge(maxr_done, 1 + b * GROUPS * NMAX + u)
                    elif u >= EARLY + 2:
                        pe.wait_ge(maxr_done, 1 + b * GROUPS * NMAX + u - 1)
                    mm(ps[:, max_bank(u), :], qstack[0:SROWS, pair, e, P * t:P * t + P],
                       kstack[0:SROWS, pair, 512 * piece:512 * piece + 512], start=True, stop=True).then_inc(maxmm_done, 1)

                for c in range(NA):
                    t = xt[c % 2]
                    pe.wait_ge(tal_done, 1 + b * NA + c + 1)
                    if c >= 2:
                        pe.wait_ge(kl_done, 1 + b * NA * KT + KT * (c - 1))
                    elif c == 0:
                        pe.wait_ge(rl_done, 1 + b * NC * FT)
                    for m in range(KT):
                        for k in range(KT):
                            last = three(ps[:, c % 2, AW * m:AW * (m + 1)], [w[:, k, D + P * m:D + P * m + P] for w in wa],
                                         [h[:, k, :] for h in t], m == 0 and k == 0, k == KT - 1)
                    last.then_inc(kmm_done, 1)
                    if c == 0:
                        pe.wait_ge(sumz_done, 1 + b * 2 * NC)
                        for m in range(KT):
                            for k in range(KT):
                                last = three(ps[:, 4 + m, 0:QW], [w[:, k, P * m:P * m + P] for w in wa],
                                             [h[:, k, :] for h in t], k == 0, k == KT - 1)
                        last.then_inc(qmm_done, 1)
                    v0 = 2 + 2 * (c % 2)
                    if c >= 2:
                        pe.wait_ge(vcp_done, 1 + b * NA + c - 1)
                        pe.wait_ge(x1_done, 1 + b * (NA - 1) + c - 2)
                    elif c == 1:
                        pe.wait_ge(qf_done, 1 + b * 2 * KT + 2 * KT)
                    n = 2 * D if c else D
                    for i in range(AT):
                        if early(c, i) is not None:
                            score_max(early(c, i))
                        for k in range(KT):
                            last = three(ps[:, v0 + i, 0:n], [h[:, k, P * i:P * i + P] for h in t],
                                         [w[:, k, 2 * D:2 * D + n] for w in wa], k == 0, k == KT - 1)
                    last.then_inc(vmm_done, 1)
                    if early(c, 2) is not None:
                        score_max(early(c, 2))
                    if c + 2 < NA:
                        turn_input(b, c + 2)
                    if early(c, 3) is not None:
                        score_max(early(c, 3))

                def turn_max(g):
                    pe.wait_ge(negs_done, 1 + b * 2 * GROUPS + 2 * g + 2)
                    if g >= 2:
                        pe.wait_ge(otok_done, 1 + b * GROUPS * NQ + NQ * (g - 1))
                    nc.tensor.transpose(ps[0:2 * UNITS, 7, 0:P], negs[:], ident[:]).then_inc(mturn_done, 1)

                def scores(s):
                    g, k = s // NT, s % NT
                    if k == 0:
                        pe.wait_ge(mcp, 1 + b * 32 * GROUPS + 32 * (g + 1))
                    if s >= 2:
                        pe.wait_ge(exp_done, 1 + b * STEPS + s - 1)
                    for i in range(GP):
                        last = mm(ps[:, 2 * (s % 2) + i, :], kstack[:, GP * g + i, P * k:P * k + P],
                                  qstack[:, GP * g + i, :, :].rearrange("p e q -> p (e q)"), start=True, stop=True)
                    last.then_inc(score_done, 1)

                def attend(s, heads):
                    g, k = s // NT, s % NT
                    pe.wait_ge(exp_done, 1 + b * STEPS + s + 1)
                    if k == 0 and g and heads[0] == 0:
                        pe.wait_ge(oraw_done, 1 + b * GROUPS + g)
                    for h in heads:
                        v = (k * H + 4 * g + h) * VW
                        last = mm(ps[32 * h:32 * h + 32, 6, 0:QW], vals[:, v:v + 32], prob[s % 2][:, h, :],
                                  start=k == 0, stop=k == NT - 1)
                    if heads[-1] == 3:
                        last.then_inc(av_done, 1)

                def turn_out(g):
                    pe.wait_ge(oraw_done, 1 + b * GROUPS + g + 1)
                    pe.wait_ge(mt_done, 1 + b * GROUPS + min(g + 2, GROUPS) if g + 1 < GROUPS else b * GROUPS + GROUPS)
                    for t in range(NQ):
                        last = nc.tensor.transpose(ps[:, 7, P * t:P * t + P], oraw[:, P * t:P * t + P], ident[:])
                    last.then_inc(oturn_done, 1)

                def spare_free(step):
                    k = SPARE[step]
                    if k == 0:
                        pe.wait_ge(oraw_done, 1 + b * GROUPS + GROUPS)
                        pe.wait_ge(otok_done, 1 + b * GROUPS * NQ + NQ * (GROUPS - 1))
                        return
                    (what, n), = [s for s, i in SPARE.items() if i == k - 1]
                    if what in ("t2", "t3"):
                        pe.wait_ge(turnl_done, 1 + b * 2 * NC + TURNS[(what, n)] + 1)
                    elif what == "gate":
                        pe.wait_ge(gatec_done, 1 + b * NC + n + 1)
                    elif what == "oturn":
                        pe.wait_ge(otok_done, 1 + b * GROUPS * NQ + NQ * GROUPS)
                    elif what == "oproj":
                        pe.wait_ge(x1g_done, 1 + b * NQ + NQ)
                    else:
                        pe.wait_ge(ust_done, 1 + b * NC + n + 1)

                def ffn_step(what, n):
                    if what in ("t2", "t3"):
                        if (what, n) not in HEAD:
                            spare_free((what, n))
                        else:
                            pe.wait_ge(maxr_done, 1 + b * GROUPS * NMAX + GROUPS * NMAX)
                        pe.wait_ge(norm_done, 1 + b * NLN * CT + CT * (LN[("ln2" if what == "t2" else "ln3", n)] + 1))
                        rows = x1in if what == "t2" else srow[n % 2]
                        for k in range(KT):
                            for i in range(CT):
                                last = nc.tensor.transpose(ps[:, turn_banks(what, n).start + k, P * i:P * i + P], rows[:, i, P * k:P * k + P], ident[:])
                        last.then_inc(turn_done, 1)
                    elif what == "nextt":
                        if n == 0:
                            pe.wait_ge(ust_done, 1 + b * NC + NC)
                        turn_input(b + 1, n)
                    elif what == "oturn":
                        spare_free((what, n))
                        turn_out(GROUPS - 1)
                    elif what == "oturned":
                        pe.wait_ge(otok_done, 1 + b * GROUPS * NQ + GROUPS * NQ)
                        for k in range(KT):
                            for t in range(NQ):
                                last = nc.tensor.transpose(ps[:, 7, QW * k + P * t:QW * k + P * t + P],
                                                           otok[:, t, P * k:P * k + P], ident[:])
                        last.then_inc(ott_done, 1)
                    elif what == "oproj":
                        spare_free((what, n))
                        pe.wait_ge(oth_done, 1 + b + 1)
                        pe.wait_ge(otl_done, 1 + b + 1)
                        for t in range(NQ):
                            for k in range(KT):
                                last = three(ps[:, 6, D * t:D * t + D], [o[:, k, P * t:P * t + P] for o in ot],
                                             [w[:, k, :] for w in wo], t == 0 and k == 0, k == KT - 1)
                        last.then_inc(oproj_done, 1)
                    elif what == "gate":
                        spare_free((what, n))
                        t = turned[BLOCK_OF[("F", n)] % 2]
                        for i in range(CT):
                            for k in range(KT):
                                for h in range(2):
                                    last = mm(ps[:, 6 + i // 2, 256 * (i % 2):256 * (i % 2) + GW],
                                              t[h][:, k, P * i:P * i + P], ga[:, k, :],
                                              start=i % 2 == 0 and k == 0 and h == 0, stop=k == KT - 1 and h == 1,
                                              skip_group_check=True)
                        last.then_inc(gate_done, 1)
                    elif what == "pick":
                        spare_free((what, n))
                        pe.wait_ge(pick_done, 1 + b * NPICK * NC + NPICK * (n + 1))
                        for i in range(CT):
                            last = nc.tensor.transpose(ps[0:UROWS, 6, P * i:P * i + P], us[:, i, :], ident[:])
                        last.then_inc(pickt_done, 1)
                    elif what == "up":
                        blk, f = n // FT, n % FT
                        w, ch = BLOCKS[blk]
                        if f == 0:
                            k = TURNS[("t2" if w == "M" else "t3", ch)]
                            pe.wait_ge(turnh_done, 1 + b * 2 * NC + k + 1)
                            pe.wait_ge(turnl_done, 1 + b * 2 * NC + k + 1)
                        if n >= 2:
                            if n - 2 in GELU:
                                pe.wait_ge(gelu_done, 1 + b * NC * FT + GELU[n - 2] + 1)
                            else:
                                pe.wait_ge(rl_done, 1 + b * NC * FT + RELU[n - 2] + 1)
                        for k in range(KT):
                            last = three(ps[:, n % 2, :], [t[:, k, P * f:P * f + P] for t in wup[w]],
                                         [t[:, k, :] for t in turned[blk % 2]], k == 0, w == "M" and k == KT - 1)
                        if w == "F":
                            if f == 0:
                                pe.wait_ge(ust_done, 1 + b * NC + ch + 1)
                                pe.wait_ge(bstl, 1 + b * 16 + 16)
                            last = mm(ps[:, n % 2, :], bst[:, P * f:P * f + P], ust[:], start=False, stop=True,
                                      skip_group_check=True)
                        last.then_inc(up_done, 1)
                    elif what == "down":
                        blk, f = n // FT, n % FT
                        w, ch = BLOCKS[blk]
                        if n in GELU:
                            pe.wait_ge(gl_done, 1 + b * NC * FT + GELU[n] + 1)
                        else:
                            pe.wait_ge(rl_done, 1 + b * NC * FT + RELU[n] + 1)
                        if f == 0 and ch:
                            pe.wait_ge(sumy_done if w == "M" else sumz_done, 1 + b * 2 * NC + 2 * ch)
                        for i in range(CT):
                            bank = (2 if w == "M" else 4) + i // 2
                            last = three(ps[:, bank, D * (i % 2):D * (i % 2) + D],
                                         [t[:, P * i:P * i + P] for t in hid[n % RING]],
                                         [t[:, f, :] for t in wdn[w]], f == 0 and i % 2 == 0, f == FT - 1)
                        last.then_inc(down_done, 1)

                for u in range(EARLY, NMAX):
                    score_max(u)
                turn_max(0)
                for u in range(NMAX, LEAD):
                    score_max(u)
                pe.wait_ge(ones_done, 1 + b * 2 + 2)
                scores(0)
                scores(1)
                u = LEAD
                for s in range(STEPS):
                    g, k = s // NT, s % NT
                    if k == TURN_MAX and g + 1 < GROUPS:
                        turn_max(g + 1)
                    if g and k == OUT_TURN:
                        turn_out(g - 1)
                    if s == STEPS - NT + HEAD_TURN:
                        ffn_step("t2", 0)
                    if u < GROUPS * NMAX:
                        score_max(u)
                        u += 1
                    attend(s, range(4))
                    if u < GROUPS * NMAX:
                        score_max(u)
                        u += 1
                    if s + 2 < STEPS:
                        scores(s + 2)

                for step in FFN_STEPS[len(HEAD):]:
                    ffn_step(*step)



XLD = [len(range(i, NA, XB)) for i in range(XB)]
KCP = 48 * NA // KQ
X1S = [XLD[0] - 1] + XLD[1:]
TURN_MAX = 13
OUT_TURN = 3
NPICK = 12
CVB = 9
LBS = CVB + 5 + 9 + 5
D_SETUP = LBS + 23
A_SETUP = 25


_INS = ["L0_attn_x", "L0_attn_w_in", "L0_attn_b_in", "L0_attn_w_out", "L0_attn_b_out", "L0_attn_w1", "L0_attn_b1",
        "L0_attn_w2", "L0_attn_b2", "L0_attn_ln1_g", "L0_attn_ln1_b", "L0_attn_ln2_g", "L0_attn_ln2_b",
        "L0_ffn_gate_W", "L0_ffn_gate_b", "L0_ffn_wi_W", "L0_ffn_wi_b", "L0_ffn_wo_W", "L0_ffn_wo_b",
        "L0_ffn_lora_A", "L0_ffn_lora_B"]


def kernel(**inputs):
    import numpy as _np
    import concourse.bacc as _bacc
    from concourse.bass_utils import run_bass_kernel_spmd as _run

    nc = _bacc.Bacc("TRN2", target_bir_lowering=False, num_devices=1)
    arrays, args = {}, []
    for name in _INS:
        a = _np.ascontiguousarray(inputs[name])
        arrays[f"in_{name}"] = a
        args.append(nc.dram_tensor(f"in_{name}", a.shape, mybir.dt.from_np(a.dtype), kind="ExternalInput").ap())
    args.append(nc.dram_tensor("out_0", (B, T, D), F32, kind="ExternalOutput").ap())
    attention_ffn_kernel(nc, *args)
    r = _run(nc, [arrays], core_ids=[0])
    return r.results[0]["out_0"]
```

```python
from contextlib import ExitStack

import concourse.bass as bass
from concourse import mybir

F32 = mybir.dt.float32
F32R = mybir.dt.float32r
ALU = mybir.AluOpType
ACT = mybir.ActivationFunctionType
AX = mybir.AxisListType

P = 128
B, T, D = 4, 2048, 256
H, HD = 16, 16
STRIDE = 8
F = 1024
E, R = 8, 4
EPS = 1e-5

NT = T // P
KT = D // P
FT = F // P
NQ = NT // STRIDE
QW = NQ * P
AT = 2
NA = NT // AT
AW = AT * P
XB = 4
CT = 4
NC = NT // CT
CW = CT * P
PAIRS = H // 2
PR = 2 * HD
GROUPS = 4
GP = PAIRS // GROUPS
VW = HD + 1
SROWS = 3 * PR
MROWS = SROWS + 2
UNITS = GP * 2 * NQ
KQ = T // 512
NMAX = UNITS * KQ
STEPS = GROUPS * NT
EARLY = NMAX * 3 // 8
LEAD = NMAX + NMAX // 4
ER = E * R
UROWS = 3 * ER + 2
GW = 2 * (E + ER)
ITEMS = 2 * NC * FT
LAG = 2
RING = 3

ORDER = [1, 2, 3, 0]
BLOCKS = [("M", 0), ("M", 1), ("F", 0), ("M", 2), ("F", 1), ("M", 3), ("F", 2), ("F", 3)]
BEFORE = {
    0: [("oturn", 0), ("res", 4)],
    1: [("onorm", 0), ("ln2a", 1), ("res", 5)],
    2: [("oturned", 0), ("res", 6)],
    3: [("olow", 0), ("res", 7)],
    4: [("oproj", 0), ("resb", 4)],
    5: [("oadd", 0), ("ln2b", 1), ("resb", 5)],
    6: [("t2", 1), ("resb", 6)], 7: [("resb", 7)],
    10: [("sumy", 0), ("ln3a", 0)], 11: [("ln3b", 0)], 13: [("t3", 0)],
    14: [("gate", 0), ("ln2a", 2), ("res", 8)], 15: [("res", 9)],
    16: [("pick", 0), ("res", 10), ("res", 11)], 17: [("ln2b", 2), ("x3w", 0), ("x3w", 1)],
    18: [("sumy", 1), ("ln3a", 1), ("x3w", 2), ("x3w", 3)],
    19: [("ln3b", 1), ("t2", 2)] + [("resb", n) for n in range(8, 12)],
    26: [("sumz", 0), ("ln4a", 0), ("t3", 1)], 27: [("ln4b", 0), ("gate", 1), ("x3w", 4)], 28: [("x3w", 5)],
    29: [("pick", 1), ("x3w", 6)], 30: [("x3w", 7)], 31: [("ln2a", 3), ("res", 12)],
    32: [("res", n) for n in range(13, 16)], 33: [("ln2b", 3)],
    34: [("sumy", 2), ("ln3a", 2)], 35: [("ln3b", 2), ("t2", 3)] + [("resb", n) for n in range(12, 16)],
    42: [("sumz", 1), ("ln4a", 1), ("t3", 2)], 43: [("ln4b", 1), ("gate", 2), ("x3w", 8)], 44: [("x3w", 9)],
    45: [("pick", 2), ("x3w", 10)], 46: [("x3w", 11)],
    50: [("sumy", 3), ("ln3a", 3)], 51: [("ln3b", 3)], 53: [("t3", 3)],
    54: [("gate", 3)] + [("x3w", n) for n in range(12, 16)],
    56: [("pick", 3)], 58: [("sumz", 2), ("ln4a", 2)], 59: [("ln4b", 2), ("nexta", 0)],
    60: [("nextb", 0), ("nexta", 1)], 61: [("nextt", 0), ("nextb", 1)], 62: [("nextt", 1), ("nexta", 2)], 63: [("nextb", 2)],
    66: [("sumz", 3), ("ln4a", 3), ("ln4b", 3)],
}


HEAD = [*[("res", _n) for _n in range(CT)], ("ln2a", 0), ("ln2b", 0), ("t2", 0),
        *[("resb", _n) for _n in range(CT)], ("xg", 0)]
HEAD_LN, HEAD_TURN = 6, 11


def ffn_steps():
    steps = list(HEAD)
    for i in range(ITEMS + LAG + 1):
        steps += BEFORE.get(i, [])
        if i < ITEMS:
            steps.append(("up", i))
        if LAG <= i < ITEMS + LAG:
            steps.append(("down", i - LAG))
    return steps


FFN_STEPS = ffn_steps()


def turn_banks(what, n):
    return slice(4, 6) if (what, n) in HEAD else slice(6, 8)


def input_bank(c):
    return 7 if c == 1 else 6


def max_bank(u):
    return 7 if u < EARLY else 4 + u % 2


def early(c, place):
    return 4 * (c - NA + 3) + place if c >= NA - 3 else None


def max_unit(u):
    g, n = u // NMAX, u % NMAX
    piece, unit = n // UNITS, n % UNITS
    return g, n, GP * g + unit // (2 * NQ), unit // NQ % 2, unit % NQ, piece


LN = {}
for _what, _n in FFN_STEPS:
    if _what in ("ln2a", "ln3a", "ln4a"):
        LN[(_what[:3], _n)] = len(LN)
NLN = len(LN)
SPARE = {s: k for k, s in enumerate(s for s in FFN_STEPS[len(HEAD):] if s[0] in ("oturn", "oproj", "t2", "t3", "gate", "pick"))}
TURNS = {s: k for k, s in enumerate(s for s in FFN_STEPS if s[0] in ("t2", "t3"))}
GELU = {8 * k + f: 8 * sum(w == "M" for w, _ in BLOCKS[:k]) + f
        for k, (w, _) in enumerate(BLOCKS) for f in range(FT) if w == "M"}
RELU = {8 * k + f: 8 * sum(w == "F" for w, _ in BLOCKS[:k]) + f
        for k, (w, _) in enumerate(BLOCKS) for f in range(FT) if w == "F"}
BLOCK_OF = {s: k for k, s in enumerate(BLOCKS)}


def attention_ffn_kernel(nc, x, w_in, b_in, w_out, b_out, w1, b1, w2, b2, ln1_g, ln1_b, ln2_g, ln2_b,
                         gate_W, gate_b, wi_W, wi_b, wo_W, wo_b, lora_A, lora_B, out):
    nc.disable_value_cache = True
    ctx = ExitStack()
    with ctx:
        top = [nc.sbuf_base]

        def place(name, shape, dt, at=None):
            size = 4
            for n in shape[1:]:
                size *= n
            size = -(-size // 32) * 32
            if at is None:
                at = -(-top[0] // 32) * 32
                top[0] = at + size
            return nc.alloc_sbuf_tensor_at(name, shape, dt, offset=at), at + size

        def keep(name, shape, dt=F32):
            return place(name, shape, dt)[0]

        def sem(name):
            return ctx.enter_context(nc.semaphore(name))

        wa = [keep(f"wa{s}", [P, KT, 4 * D], F32R) for s in "hl"]
        wo = [keep(f"wo{s}", [P, KT, D], F32R) for s in "hl"]
        wup = {"M": [keep(f"w1{s}", [P, KT, F], F32R) for s in "hl"],
               "F": [keep(f"wi{s}", [P, KT, F], F32R) for s in "hl"]}
        wdn = {"M": [keep(f"w2{s}", [P, FT, D], F32R) for s in "hl"],
               "F": [keep(f"wf{s}", [P, FT, D], F32R) for s in "hl"]}
        ga = keep("ga", [P, KT, GW], F32R)
        ident = keep("ident", [P, P])
        crow = keep("crow", [P, D])
        gateb = keep("gateb", [P, E])
        rank = keep("rank", [P, E])
        cols = keep("cols", [P, 64])
        vals = keep("vals", [P, NT * H * VW + P])
        stats = keep("stats", [P, CT, 6])
        mv = keep("mv", [P, CT, 2])
        vare = keep("vare", [P, CT])
        rstd = keep("rstd", [P, CT])
        astats = keep("astats", [P, 2, AT, 6])
        amv = keep("amv", [P, 2, AT, 2])
        avare = keep("avare", [P, 2, AT])
        arstd = keep("arstd", [P, 2, AT])
        mhalf = keep("mhalf", [P, CT])
        mx = keep("mx", [P, 2, NMAX])
        negm = keep("negm", [P, UNITS])
        negs = keep("negs", [P, 2 * UNITS])
        mT = keep("mT", [2 * UNITS, P])
        rsum = keep("rsum", [P, NQ, 4])
        xn = keep("xn", [P, AT, D])
        kst = keep("kst", [P, 2 * KT, AW], F32R)
        qstack = keep("qstack", [MROWS, PAIRS, 2, QW], F32R)
        pat = -(-top[0] // 32) * 32
        xin = [place(f"xin{i}", [P, AT, D], F32, pat + 2048 * i)[0] for i in range(XB)]
        xt = [[place(f"xt{i}{s}", [P, KT, AW], F32R, pat + 2048 * XB + 4096 * i + 2048 * k)[0]
               for k, s in enumerate("hl")] for i in range(2)]
        prob = [place(f"prob{i}", [P, 2 * GP, QW], F32, pat + 4096 * i)[0] for i in range(2)]
        ot = [place(f"ot{s}", [P, KT, QW], F32R, pat + 2048 * i)[0] for i, s in enumerate("hl")]
        oraw, _ = place("oraw", [P, QW], F32, pat + 8192)
        otok, _ = place("otok", [P, NQ, D], F32, pat + 9216)
        xg, _ = place("xg", [P, NQ, D], F32, pat + 11264)
        kat = pat + 2048 * XB + 8192
        kstack, end = place("kstack", [MROWS, PAIRS, T], F32R, kat)
        assert end <= nc.sbuf_usable_end, (end, nc.sbuf_usable_end)
        at = [kat]

        def ffn(name, shape, dt=F32):
            t, at[0] = place(name, shape, dt, at[0])
            assert at[0] <= end, (name, at[0], end)
            return t

        xrow = [ffn(f"xrow{i}", [P, CT, D]) for i in range(2)]
        x1in = ffn("x1in", [P, CT, D])
        bst = ffn("bst", [UROWS, F], F32R)
        srow = [ffn(f"srow{i}", [P, CT, D]) for i in range(2)]
        turned = [[ffn(f"turned{i}{s}", [P, KT, CW], F32R) for s in "hl"] for i in range(2)]
        rows2 = ffn("rows2", [P, 2, D])
        gel = [ffn(f"gel{i}", [P, CW]) for i in range(2)]
        hid = [[ffn(f"hid{i}{s}", [P, CW], F32R) for s in "hl"] for i in range(RING)]
        ust = ffn("ust", [UROWS, CW], F32R)
        us = ffn("us", [P, CT, UROWS])
        gcopy = ffn("gcopy", [P, CT, GW])
        uall = ffn("uall", [P, CT, E + ER])
        pickm = ffn("pickm", [P, CT])
        picke = ffn("picke", [P, CT, E])
        ktail, _ = place("ktail", [P, 2 * KT, T], F32R, kat)
        kstage = [kst, ktail[:, :, T - AW:T]]
        x1o, _ = place("x1o", [P, AT, D], F32, kat + 4 * (5 * T - 2 * AW))
        tail = [end - 4 * T * n - 2 * T for n in range(3)]
        qf = [place(f"qf{m}", [P, 2, QW], F32, tail[2] + 2048 * m)[0] for m in range(KT)]
        qstage = [place(f"qstage{m}", [P, 2, 2 * QW], F32R, tail[m])[0] for m in range(KT)]
        at[0] = kat
        nwin = ffn("nwin", [P, 6, D])
        nwout = ffn("nwout", [P, KT, D])
        nw1 = ffn("nw1", [P, FT, D])
        nw2 = ffn("nw2", [P, KT, F])
        nwi = ffn("nwi", [P, FT, D])
        nwo = ffn("nwo", [P, KT, F])
        nga = ffn("nga", [E + ER, D])
        nlb = ffn("nlb", [P, FT, E, R])
        lbs = ffn("lbs", [P, FT, UROWS])
        wibc = ffn("wibc", [P, FT])
        lnb = ffn("lnb", [P, 2, D])
        junk = ffn("junk", [P, D])
        wof = ffn("wof", [P, KT, D])
        cvb = ffn("cvb", [P, KT, P])
        boutr = ffn("boutr", [P, D])
        bsts = ffn("bsts", [UROWS, F], F32R)

        ps = ctx.enter_context(nc.psum_tensor("ps", [P, 8, 512], F32))
        x1_d = nc.dram_tensor("x1_d", [B, P, NQ, STRIDE, D], F32, kind="Internal").ap()
        k_d = nc.dram_tensor("k_d", [KQ, 2, KT * P, 2 * AW], F32, kind="Internal").ap()
        q_d = nc.dram_tensor("q_d", [KT, 2, P, 2 * QW], F32, kind="Internal").ap()
        bst_d = nc.dram_tensor("bst_d", [UROWS, F], F32, kind="Internal").ap()

        G1, G2, BIN, BINS, B1C, B1S, MASK, QB, LNW = 0, 2, 4, 10, 16, 24, 32, 34, 40

        wload = [sem(f"wload{i}") for i in range(14)]
        p_const, p_ident = sem("p_const"), sem("p_ident")
        d_setup, a_setup, pe_setup = sem("d_setup"), sem("a_setup"), sem("pe_setup")
        xld = [sem(f"xld{i}") for i in range(XB)]
        x1st = [sem(f"x1st{i}") for i in range(XB)]
        xgld, x1gst = sem("xgld"), sem("x1gst")
        xgc_done = sem("xgc_done")
        stw = [sem(f"stw{i}") for i in range(2)]
        stq = sem("stq")
        kcp = [sem(f"kcp{i}") for i in range(KQ)]
        qcp = [sem(f"qcp{m}") for m in range(KT)]
        mcp = sem("mcp")
        bstw, bstl = sem("bstw"), sem("bstl")
        fld = [sem(f"fld{i}") for i in range(2)]
        rld = sem("rld")
        ost = [sem(f"ost{i}") for i in range(2)]
        astat_done, aaggr_done = sem("astat_done"), sem("aaggr_done")
        avare_done, arstd_done, anorm_done = sem("avare_done"), sem("arstd_done"), sem("anorm_done")
        stat_done, aggr_done = sem("stat_done"), sem("aggr_done")
        vare_done, rstd_done, norm_done = sem("vare_done"), sem("rstd_done"), sem("norm_done")
        ones_done = sem("ones_done")
        xc_done = sem("xc_done")
        ta_done, tah_done, tal_done = sem("ta_done"), sem("tah_done"), sem("tal_done")
        kmm_done, kh_done, kl_done = sem("kmm_done"), sem("kh_done"), sem("kl_done")
        vmm_done, vcp_done, x1_done = sem("vmm_done"), sem("vcp_done"), sem("x1_done")
        qmm_done, qf_done, qh_done, ql_done = sem("qmm_done"), sem("qf_done"), sem("qh_done"), sem("ql_done")
        maxmm_done, maxr_done, negm_done, negs_done = (
            sem("maxmm_done"), sem("maxr_done"), sem("negm_done"), sem("negs_done"))
        mturn_done, mt_done = sem("mturn_done"), sem("mt_done")
        score_done, exp_done, av_done = sem("score_done"), sem("exp_done"), sem("av_done")
        oraw_done, oturn_done, rsum_done, otok_done = (
            sem("oraw_done"), sem("oturn_done"), sem("rsum_done"), sem("otok_done"))
        ott_done, oth_done, otl_done, oproj_done, x1g_done = (
            sem("ott_done"), sem("oth_done"), sem("otl_done"), sem("oproj_done"), sem("x1g_done"))
        res_done, resb_done, x3w_done = sem("res_done"), sem("resb_done"), sem("x3w_done")
        turn_done, turnh_done, turnl_done = sem("turn_done"), sem("turnh_done"), sem("turnl_done")
        up_done, down_done = sem("up_done"), sem("down_done")
        gelu_done, gh_done, gl_done = sem("gelu_done"), sem("gh_done"), sem("gl_done")
        rh_done, rl_done = sem("rh_done"), sem("rl_done")
        sumy_done, sumz_done = sem("sumy_done"), sem("sumz_done")
        gate_done, gatec_done, pick_done = sem("gate_done"), sem("gatec_done"), sem("pick_done")
        pickt_done, ust_done = sem("pickt_done"), sem("ust_done")

        x_v = x.rearrange("b (p t j) d -> b p t j d", t=2, j=STRIDE)
        o_v = out.rearrange("b (p t j) d -> b p t j d", t=2, j=STRIDE)

        block = ctx.enter_context(nc.Block())

        def setup_groups():
            g = [("wout", 0)]
            g += [("qk", k) for k in range(KT)] + [("vo", k) for k in range(KT)] + [("crow", 0)]
            for w in ("M", "F"):
                g += [("up" + w, i) for i in range(4)] + [("dn" + w, i) for i in range(4)]
            g += [("ga", 0), ("bst", 0), ("bst", 1)]
            return g

        SG = setup_groups()

        def rows_bc(v):
            return v.rearrange("(a d) -> a d", a=1).to_broadcast([P, v.shape[0]])

        @block.sync
        def _(sp):
            for s in [*xld, *x1st, xgld, x1gst, *stw, stq, *kcp, *qcp, mcp, *fld, rld, bstl, *ost]:
                sp.sem_inc(s, 1)
            sp.dma_start(nwin[:], w_in.rearrange("(m p) d -> p m d", p=P)).then_inc(wload[0], 16)
            sp.dma_start(nwout[:], w_out.rearrange("(m p) d -> p m d", p=P)).then_inc(wload[1], 16)
            for c in range(XB):
                sp.dma_start(xin[c][:], x_v[0, :, :, c, :]).then_inc(xld[c], 16)
            sp.dma_start(lnb[:, 0, :], rows_bc(ln1_b)).then_inc(wload[2], 16)
            sp.dma_start(lnb[:, 1, :], rows_bc(ln2_b)).then_inc(wload[2], 16)
            sp.dma_start(boutr[:], rows_bc(b_out)).then_inc(wload[2], 16)
            sp.dma_start(gateb[:], rows_bc(gate_b)).then_inc(wload[2], 16)
            with nc.allow_non_contiguous_dma(reason="vectors turned into columns, once"):
                for t, v, n in ((G1, ln1_g, KT), (G2, ln2_g, KT), (BIN, b_in, 6), (B1C, b1, FT)):
                    sp.dma_start(cols[:, t:t + n], v.rearrange("(m p) -> p m", p=P)).then_inc(wload[3], 16)
                sp.dma_start(wibc[:], wi_b.rearrange("(m p) -> p m", p=P)).then_inc(wload[3], 16)
            sp.dma_start(nw1[:], w1.rearrange("(m p) d -> p m d", p=P)).then_inc(wload[4], 16)
            sp.dma_start(nw2[:], w2.rearrange("(m p) f -> p m f", p=P)).then_inc(wload[5], 16)
            sp.dma_start(nwi[:], wi_W.rearrange("(m p) d -> p m d", p=P)).then_inc(wload[6], 16)
            sp.dma_start(nwo[:], wo_W.rearrange("(m p) f -> p m f", p=P)).then_inc(wload[7], 16)
            sp.dma_start(nga[0:E], gate_W).then_inc(wload[8], 16)
            sp.dma_start(nga[E:E + ER], lora_A.rearrange("e r d -> (e r) d")).then_inc(wload[8], 16)
            for e in range(E):
                sp.dma_start(nlb[:, :, e, :], lora_B[e].rearrange("(m p) r -> p m r", p=P)).then_inc(wload[9], 16)

            sp.wait_ge(a_setup, A_SETUP)
            sp.dma_start(bst_d, bsts[:].bitcast(F32)).then_inc(bstw, 16)

            with sp.Fori(2, B + 2) as turn:
                b = turn - 2

                def k_stack(c, n):
                    for i in range(c, c + n):
                        sp.wait_ge(stw[i % 2], 1 + b * 8 * NA + 16 * (i // 2 + 1))
                    piece, at = c // 2, AW * (c % 2)
                    for blk, part in enumerate((0, 1, 0)):
                        sp.dma_start(kstack[PR * blk:PR * (blk + 1), :, AW * c:AW * (c + n)].bitcast(F32),
                                     k_d[piece, part, :, at:at + AW * n].rearrange("(a r) n -> r a n", r=PR)
                                     ).then_inc(kcp[piece], 16)

                for c in range(NA):
                    sp.wait_ge(kh_done, 1 + b * NA * KT + KT * (c + 1))
                    sp.wait_ge(kl_done, 1 + b * NA * KT + KT * (c + 1))
                    if c == 0:
                        for i in range(KQ):
                            sp.wait_ge(kcp[i], 1 + b * KCP[i])
                    sp.dma_start(k_d[c // 2, :, :, AW * (c % 2):AW * (c % 2) + AW].rearrange("h (m p) n -> p (h m) n", p=P),
                                 kstage[c % 2][:, :, :].bitcast(F32)).then_inc(stw[c % 2], 16)
                    if c == 0:
                        sp.wait_ge(anorm_done, 1 + b * NA * AT + AT)
                        sp.dma_start(xin[0][:], x_v[b, :, :, XB, :]).then_inc(xld[0], 16)
                    if c:
                        sp.wait_ge(x1_done, 1 + b * (NA - 1) + c)
                        if c + XB < NA:
                            sp.dma_start(x1_d[b, :, :, c, :], x1o[:]).then_inc(x1st[c % XB], 16)
                            sp.dma_start(xin[c][:], x_v[b, :, :, c + XB, :]).then_inc(xld[c], 16)
                        else:
                            sp.dma_start(x1_d[b, :, :, c, :], xin[c % XB][:]).then_inc(x1st[c % XB], 16)
                    if c == NA - 2:
                        sp.wait_ge(x1st[NA - 1 - XB], 1 + b * 16 * X1S[NA - 1 - XB] + 16)
                    if c == 1:
                        for i in range(2):
                            sp.wait_ge(ost[i], 1 + b * 32)
                        sp.wait_ge(ust_done, 1 + b * NC)
                        sp.wait_ge(pe_setup, len(SG))
                        sp.wait_ge(d_setup, D_SETUP)
                        sp.wait_ge(bstw, 16)
                    if c in (2, NA - 2):
                        m = int(c > 2)
                        if m == 0:
                            sp.wait_ge(stq, 1 + b * 16 * KT + 16 * KT)
                            sp.wait_ge(score_done, 1 + b * STEPS)
                        for blk, part in enumerate((0, 0, 1)):
                            sp.dma_start(
                                qstack[PR * blk:PR * (blk + 1), 4 * m:4 * m + 4, :, :].rearrange(
                                    "r a e q -> r a (e q)").bitcast(F32),
                                q_d[m, part].rearrange("(a r) n -> r a n", r=PR)).then_inc(qcp[m], 16)
                    if c:
                        k_stack(c - 1, 1)
                    if c == 1:
                        sp.wait_ge(qh_done, 1 + b * KT + KT)
                        sp.wait_ge(ql_done, 1 + b * KT + KT)
                        for m in range(KT):
                            sp.wait_ge(qcp[m], 1 + b * 48)
                        for m in range(KT):
                            sp.dma_start(q_d[m].rearrange("h p n -> p h n"), qstage[m][:].bitcast(F32)).then_inc(stq, 16)
                k_stack(NA - 1, 1)
                for g in range(GROUPS):
                    sp.wait_ge(mt_done, 1 + b * GROUPS + g + 1)
                    for h in range(2):
                        sp.dma_start(
                            qstack[SROWS + h:SROWS + h + 1, GP * g:GP * (g + 1), :, :].rearrange(
                                "p a e q -> p (a e q)").rearrange("p (u q) -> p u q", q=P).bitcast(F32),
                            mT[UNITS * h:UNITS * (h + 1), :]).then_inc(mcp, 16)

                sp.wait_ge(score_done, 1 + b * STEPS + STEPS - NT)
                sp.wait_ge(maxmm_done, 1 + b * GROUPS * NMAX + GROUPS * NMAX)
                sp.dma_start(xg[:], x_v[b, :, :, 0, :]).then_inc(xgld, 16)
                sp.wait_ge(ones_done, 1 + b * 3 + 3)
                for n in range(NC):
                    c = ORDER[n]
                    if n >= 2:
                        sp.wait_ge(sumy_done, 1 + b * 2 * NC + 2 * (n - 1))
                    sp.dma_start(xrow[n % 2][:].rearrange("p (t j) d -> p t j d", t=2),
                                 x_v[b, :, :, 2 * c:2 * c + 2, :]).then_inc(fld[n % 2], 16)
                    if n == 0:
                        for i in range(XB):
                            sp.wait_ge(x1st[i], 1 + b * 16 * X1S[i] + 16 * X1S[i])
                    else:
                        sp.wait_ge(turn_done, 1 + b * 2 * NC + TURNS[("t2", n - 1)] + 1)
                    if n == NC - 1:
                        sp.wait_ge(x1gst, 1 + b * 16 + 16)
                    sp.dma_start(x1in[:].rearrange("p (t j) d -> p t j d", t=2),
                                 x1_d[b, :, :, 2 * c:2 * c + 2, :]).then_inc(fld[n % 2], 16)
                    if n == 0:
                        sp.dma_start(bst[:].bitcast(F32), bst_d).then_inc(bstl, 16)
                        sp.dma_start(rows2[:, 0, :], rows_bc(b2)).then_inc(rld, 16)
                        sp.dma_start(rows2[:, 1, :], rows_bc(wo_b)).then_inc(rld, 16)
                    if n == 1:
                        sp.wait_ge(x1g_done, 1 + b * NQ + NQ)
                        sp.dma_start(x1_d[b, :, :, 0, :], xg[:]).then_inc(x1gst, 16)
                for c in range(XB):
                    sp.dma_start(xin[c][:], x_v[(b + 1) % B, :, :, c, :]).then_inc(xld[c], 16)
                for n in range(NC):
                    c = ORDER[n]
                    sp.wait_ge(norm_done, 1 + b * NLN * CT + CT * (LN[("ln4", n)] + 1))
                    sp.dma_start(o_v[b, :, :, 2 * c:2 * c + 2, :],
                                 srow[n % 2][:].rearrange("p (t j) d -> p t j d", t=2)).then_inc(ost[n % 2], 16)
            for i in range(2):
                sp.wait_ge(ost[i], 1 + B * 32)
            for i in range(XB):
                sp.wait_ge(x1st[i], 1 + B * 16 * X1S[i])
                sp.wait_ge(xld[i], 1 + B * 16 * XLD[i] + 16)
            sp.wait_ge(x1gst, 1 + B * 16)

        @block.gpsimd
        def _(pool):
            nc.gpsimd.memset(ident[:], 0.0).then_inc(p_ident, 1)
            nc.gpsimd.memset(vals[:], 1.0).then_inc(p_const, 1)
            nc.gpsimd.memset(mhalf[:], -0.5).then_inc(p_const, 1)
            for e in range(E):
                nc.gpsimd.memset(rank[:, e:e + 1], float(E - e)).then_inc(p_const, 1)
            pool.wait_ge(p_ident, 1)
            nc.gpsimd.affine_select(out=ident[:], in_=ident[:], compare_op=ALU.not_equal, fill=1.0, base=0,
                                    pattern=[[-1, P]], channel_multiplier=1).then_inc(p_ident, 1)
            for s in [rstd_done, arstd_done, ones_done, xc_done, res_done, resb_done, x3w_done, gl_done, xgc_done, ql_done]:
                pool.sem_inc(s, 1)

            def rsqrt_input(b, c):
                pool.wait_ge(avare_done, 1 + b * NA + c + 1)
                nc.gpsimd.tensor_tensor(arstd[:, c % 2, :], avare[:, c % 2, :], mhalf[:, 0:AT],
                                        ALU.pow).then_inc(arstd_done, 1)

            pool.wait_ge(p_const, 2 + E)
            for c in range(3):
                rsqrt_input(0, c)
            pool.wait_ge(d_setup, D_SETUP)
            written = nc.alloc_register(pool.engine)
            nc.gpsimd.reg_mov(written, 1)
            with pool.Fori(0, B) as b:
                def rsqrt(k):
                    pool.wait_ge(vare_done, 1 + b * NLN + k + 1)
                    nc.gpsimd.tensor_tensor(rstd[:], vare[:], mhalf[:], ALU.pow).then_inc(rstd_done, 1)

                for c in range(NA):
                    if c:
                        pool.wait_ge(anorm_done, 1 + b * NA * AT + AT * (c + 1))
                        nc.gpsimd.tensor_tensor(xin[c % XB][:], xin[c % XB][:],
                                                crow[:, None, :].to_broadcast([P, AT, D]), ALU.add).then_inc(xc_done, 1)
                    if c and c + 2 < NA:
                        rsqrt_input(b, c + 2)
                    if c == 0:
                        pool.wait_ge(bstw, 16)
                        for m in range(KT):
                            pool.wait_ge(qh_done, 1 + b * KT + m + 1)
                            nc.gpsimd.tensor_tensor(qstage[m][:, 1, :], qf[m][:].rearrange("p e q -> p (e q)"),
                                                    qstage[m][:, 0, :], ALU.subtract).then_inc(ql_done, 1)
                for i in range(2):
                    pool.wait_ge(ost[i], 1 + b * 32)
                pool.wait_ge(pe_setup, len(SG))
                pool.wait_ge(bstw, 16)
                pool.wait_ge(xc_done, 1 + b * (NA - 1) + NA - 1)
                nc.gpsimd.reg_add(written, written, 3)
                nc.gpsimd.memset(kstack[SROWS:MROWS, 4:8, :].bitcast(F32), 1.0).then_inc(ones_done, 1)
                nc.gpsimd.memset(kstack[SROWS:MROWS, 0:4, 0:T - AW].bitcast(F32), 1.0).then_inc(ones_done, 1)
                pool.wait_ge(stw[1], 1 + b * 8 * NA + 8 * NA)
                ones = vals[SROWS:MROWS, None, NT * H * VW:NT * H * VW + 1].to_broadcast([MROWS - SROWS, 4, AW])
                nc.gpsimd.tensor_tensor(kstack[SROWS:MROWS, 0:4, T - AW:T], ones, ones, ALU.mult).then_inc(ones_done, 1)
                pool.wait_ge(ones_done, pool.snap(written, min_val=4))

                for what, n in FFN_STEPS:
                    if what in ("ln2a", "ln3a", "ln4a"):
                        rsqrt(LN[(what[:3], n)])
                    if what == "nexta":
                        rsqrt_input(b + 1, n)
                    t, i = n // CT, n % CT
                    if what == "xg":
                        pool.wait_ge(xgld, 1 + b * 16 + 16)
                        nc.gpsimd.tensor_tensor(xg[:], xg[:], crow[:, None, :].to_broadcast([P, NQ, D]),
                                                ALU.add).then_inc(xgc_done, 1)
                    if what == "res":
                        if i == 0:
                            pool.wait_ge(fld[t % 2], 1 + b * 64 + 32 * (t // 2 + 1))
                        nc.gpsimd.tensor_tensor(xrow[t % 2][:, i, :], xrow[t % 2][:, i, :], x1in[:, i, :],
                                                ALU.add).then_inc(res_done, 1)
                    if what == "resb":
                        pool.wait_ge(res_done, 1 + b * NT + n + 1)
                        if n == 0:
                            pool.wait_ge(rld, 1 + b * 32 + 32)
                        nc.gpsimd.tensor_tensor(xrow[t % 2][:, i, :], xrow[t % 2][:, i, :], rows2[:, 0, :],
                                                ALU.add).then_inc(resb_done, 1)
                    if what == "x3w":
                        if i == 0:
                            pool.wait_ge(turn_done, 1 + b * 2 * NC + TURNS[("t3", t)] + 1)
                        nc.gpsimd.tensor_tensor(srow[t % 2][:, i, :], srow[t % 2][:, i, :], rows2[:, 1, :],
                                                ALU.add).then_inc(x3w_done, 1)
                    if what == "up" and n in GELU:
                        k = GELU[n]
                        pool.wait_ge(gh_done, 1 + b * NC * FT + k + 1)
                        nc.gpsimd.tensor_tensor(hid[n % RING][1][:], gel[k % 2][:], hid[n % RING][0][:],
                                                ALU.subtract).then_inc(gl_done, 1)

        @block.scalar
        def _(act):
            for s in [tah_done, kh_done, vcp_done, mt_done, exp_done, oth_done, turnh_done, gelu_done, rh_done,
                      ust_done, qf_done]:
                act.sem_inc(s, 1)

            def turned_high(b, c):
                act.wait_ge(ta_done, 1 + b * NA + c + 1)
                if c >= 2:
                    act.wait_ge(vmm_done, 1 + b * NA + c - 1)
                elif c == 0:
                    act.wait_ge(oproj_done, 1 + b)
                    act.wait_ge(x1gst, 1 + b * 16)
                nc.scalar.activation(xt[c % 2][0][:].rearrange("p k n -> p (k n)"), ps[:, input_bank(c), :],
                                     ACT.Copy).then_inc(tah_done, 1)

            for c in range(2):
                turned_high(0, c)
            for k, (what, i) in enumerate(SG):
                act.wait_ge(pe_setup, k + 1)
                bank = ps[:, k % 8, :]
                if what == "wout":
                    nc.scalar.activation(wof[:].rearrange("p k d -> p (k d)"), bank, ACT.Copy).then_inc(a_setup, 1)
                    act.wait_ge(a_setup, 1)
                    nc.scalar.activation(wo[0][:].rearrange("p k d -> p (k d)"), bank, ACT.Copy).then_inc(a_setup, 1)
                elif what == "qk":
                    act.wait_ge(wload[3], 16 * 5)
                    nc.scalar.activation(wa[0][:, i, 0:512], bank, ACT.Copy, scale=cols[:, G1 + i:G1 + i + 1]
                                         ).then_inc(a_setup, 1)
                elif what == "vo":
                    nc.scalar.activation(wa[0][:, i, 512:1024], bank, ACT.Copy, scale=cols[:, G1 + i:G1 + i + 1]
                                         ).then_inc(a_setup, 1)
                elif what in ("upM", "upF"):
                    kt, half = i // 2, i % 2
                    s = cols[:, G2 + kt:G2 + kt + 1] if what == "upM" else 1.0
                    nc.scalar.activation(wup[what[2]][0][:, kt, 512 * half:512 * half + 512], bank, ACT.Copy,
                                         scale=s).then_inc(a_setup, 1)
                elif what in ("dnM", "dnF"):
                    nc.scalar.activation(wdn[what[2]][0][:, 2 * i:2 * i + 2, :].rearrange("p k d -> p (k d)"), bank,
                                         ACT.Copy).then_inc(a_setup, 1)
                elif what == "ga":
                    act.wait_ge(p_const, 2 + E)
                    nc.scalar.activation(ga[:, :, 0:E + ER], ps[:, k % 8, 0:2 * (E + ER)].rearrange(
                        "p (k n) -> p k n", k=KT), ACT.Copy).then_inc(a_setup, 1)
                elif what == "bst":
                    nc.scalar.activation(bsts[:, 512 * i:512 * i + 512], ps[0:UROWS, k % 8, :], ACT.Copy
                                         ).then_inc(a_setup, 1)

            with act.Fori(0, B) as b:
                for c in range(NA):
                    act.wait_ge(kmm_done, 1 + b * NA + c + 1)
                    act.wait_ge(stw[c % 2], 1 + b * 8 * NA + 16 * (c // 2))
                    if c == 1:
                        for i in range(2):
                            act.wait_ge(ost[i], 1 + b * 32)
                        act.wait_ge(bstw, 16)
                    for m in range(KT):
                        nc.scalar.activation(kstage[c % 2][:, m, :], ps[:, c % 2, AW * m:AW * (m + 1)],
                                             ACT.Identity, bias=cols[:, BIN + KT + m:BIN + KT + m + 1]).then_inc(kh_done, 1)
                    if 1 <= c < NA - 1:
                        turned_high(b, c + 1)
                    act.wait_ge(vmm_done, 1 + b * NA + c + 1)
                    if c == 0:
                        act.wait_ge(av_done, 1 + b * STEPS)
                        act.wait_ge(p_const, 2 + E)
                    v0 = 2 + 2 * (c % 2)
                    nc.scalar.activation(
                        vals[:, AT * c * H * VW:AT * (c + 1) * H * VW].rearrange("p (h v) -> p h v", v=VW)[:, :, 0:HD],
                        ps[:, v0:v0 + 2, 0:D].rearrange("p t (h v) -> p t h v", v=HD), ACT.Copy).then_inc(vcp_done, 1)
                    if c == 0:
                        act.wait_ge(qmm_done, 1 + b + 1)
                        act.wait_ge(bstw, 16)
                        for m in range(KT):
                            for e in range(2):
                                nc.scalar.activation(
                                    qf[m][:, e, :], ps[:, 4 + m, 0:QW], ACT.Identity,
                                    scale=cols[:, MASK + e:MASK + e + 1],
                                    bias=cols[:, QB + 2 * m + e:QB + 2 * m + e + 1]).then_inc(qf_done, 1)

                def turn_max(g):
                    act.wait_ge(mturn_done, 1 + b * GROUPS + g + 1)
                    act.wait_ge(mcp, 1 + b * 32 * GROUPS + 32 * g)
                    nc.scalar.activation(mT[:], ps[0:2 * UNITS, 7, 0:P], ACT.Copy).then_inc(mt_done, 1)

                def ffn_step(what, n):
                    if what in ("t2", "t3"):
                        k = TURNS[(what, n)]
                        blk = BLOCK_OF[("M" if what == "t2" else "F", n)]
                        act.wait_ge(turn_done, 1 + b * 2 * NC + k + 1)
                        if blk >= 2:
                            act.wait_ge(up_done, 1 + b * ITEMS + 8 * (blk - 1))
                        nc.scalar.activation(turned[blk % 2][0][:], ps[:, turn_banks(what, n), :], ACT.Copy).then_inc(turnh_done, 1)
                    elif what == "nextt":
                        turned_high(b + 1, n)
                    elif what == "olow":
                        act.wait_ge(ott_done, 1 + b + 1)
                        nc.scalar.activation(ot[0][:].rearrange("p k q -> p (k q)"), ps[:, 7, :],
                                             ACT.Copy).then_inc(oth_done, 1)
                    elif what == "pick":
                        act.wait_ge(pickt_done, 1 + b * NC + n + 1)
                        if n:
                            act.wait_ge(up_done, 1 + b * ITEMS + 8 * (BLOCK_OF[("F", n - 1)] + 1))
                        nc.scalar.activation(ust[:], ps[0:UROWS, 6, :], ACT.Copy).then_inc(ust_done, 1)
                    elif what == "up":
                        act.wait_ge(up_done, 1 + b * ITEMS + n + 1)
                        if n in GELU:
                            k, f = GELU[n], n % FT
                            if k >= 2:
                                act.wait_ge(gl_done, 1 + b * NC * FT + k - 1)
                            nc.scalar.activation(gel[k % 2][:], ps[:, n % 2, :], ACT.Gelu,
                                                 bias=cols[:, B1C + f:B1C + f + 1]).then_inc(gelu_done, 1)
                        else:
                            if n >= RING:
                                act.wait_ge(down_done, 1 + b * ITEMS + n - RING + 1)
                            nc.scalar.activation(hid[n % RING][0][:], ps[:, n % 2, :], ACT.Relu).then_inc(rh_done, 1)

                turn_max(0)
                for i in range(XB):
                    act.wait_ge(x1st[i], 1 + b * 16 * X1S[i] + 16 * X1S[i])
                for s in range(STEPS):
                    act.wait_ge(score_done, 1 + b * STEPS + s + 1)
                    if s >= 2:
                        act.wait_ge(av_done, 1 + b * STEPS + s - 1)
                    nc.scalar.activation(prob[s % 2][:].rearrange("p h q -> p (h q)"),
                                         ps[:, 2 * (s % 2):2 * (s % 2) + 2, :].rearrange("p a n -> p (a n)"),
                                         ACT.Exp).then_inc(exp_done, 1)
                    if s % NT == TURN_MAX and s // NT + 1 < GROUPS:
                        turn_max(s // NT + 1)
                    if s == STEPS - NT + HEAD_TURN:
                        ffn_step("t2", 0)
                for step in FFN_STEPS[len(HEAD):]:
                    ffn_step(*step)

        @block.vector
        def _(dve):
            for s in [stat_done, aggr_done, vare_done, norm_done, astat_done, aaggr_done, avare_done, anorm_done,
                      tal_done, kl_done, x1_done, qh_done, maxr_done, negm_done, negs_done, oraw_done,
                      rsum_done, otok_done, otl_done, x1g_done, turnl_done, gh_done, rl_done, sumy_done, sumz_done,
                      gatec_done, pick_done]:
                dve.sem_inc(s, 1)

            aggregated = nc.alloc_register(dve.engine)
            nc.vector.reg_mov(aggregated, 1)
            aaggregated = nc.alloc_register(dve.engine)
            nc.vector.reg_mov(aaggregated, 1)

            def input_a(b, c):
                i = c % 2
                dve.wait_ge(xld[c % XB], 1 + b * 16 * XLD[c % XB] + 16 * (c // XB + 1))
                for t in range(AT):
                    nc.vector.bn_stats(astats[:, i, t, :], xin[c % XB][:, t, :]).then_inc(astat_done, 1)
                dve.wait_ge(astat_done, 1 + b * NA * AT + AT * (c + 1))
                nc.vector.reg_add(aaggregated, aaggregated, AT)
                for t in range(AT):
                    nc.vector.bn_aggr(amv[:, i, t, :], astats[:, i, t, :]).then_inc(aaggr_done, 1)
                dve.wait_ge(aaggr_done, dve.snap(aaggregated, min_val=AT + 1))
                nc.vector.tensor_scalar(avare[:, i, :], amv[:, i, :, 1], EPS, None, ALU.add).then_inc(avare_done, 1)

            def input_b(b, c):
                i = c % 2
                dve.wait_ge(arstd_done, 1 + b * NA + c + 1)
                dve.wait_ge(ta_done, 1 + b * NA + c)
                for t in range(AT):
                    nc.vector.tensor_scalar(xn[:, t, :], xin[c % XB][:, t, :], amv[:, i, t, 0:1], arstd[:, i, t:t + 1],
                                            ALU.subtract, ALU.mult).then_inc(anorm_done, 1)

            def turned_low(b, c):
                dve.wait_ge(tah_done, 1 + b * NA + c + 1)
                nc.vector.tensor_tensor(xt[c % 2][1][:].rearrange("p k n -> p (k n)"), ps[:, input_bank(c), :],
                                        xt[c % 2][0][:].rearrange("p k n -> p (k n)"), ALU.subtract).then_inc(tal_done, 1)

            for c in range(3):
                input_a(0, c)
                input_b(0, c)
            for c in range(2):
                turned_low(0, c)

            chain = [0]

            def link(ins, hold=True):
                chain[0] += 1
                ins.then_inc(d_setup, 1)
                if hold:
                    dve.wait_ge(d_setup, chain[0])

            dve.wait_ge(wload[0], 16)
            dve.wait_ge(wload[2], 64)
            dve.wait_ge(wload[3], 80)
            for m in range(6):
                link(nc.vector.tensor_tensor_reduce(out=junk[:], in0=nwin[:, m, :], in1=lnb[:, 0, :], scale=1.0, scalar=0.0,
                                                    op0=ALU.mult, op1=ALU.add, accum_out=cols[:, BINS + m:BINS + m + 1]))
            link(nc.vector.tensor_tensor(cols[:, BIN:BIN + 6], cols[:, BIN:BIN + 6], cols[:, BINS:BINS + 6], ALU.add))
            dve.wait_ge(p_const, 2 + E)
            for k in range(KT):
                link(nc.vector.tensor_scalar(cvb[:, k, :], vals[:, 0:P], cols[:, BIN + 4 + k:BIN + 5 + k], None, ALU.mult))
            assert chain[0] == CVB
            dve.wait_ge(p_ident, 2)
            for e in range(2):
                link(nc.vector.tensor_reduce(cols[:, MASK + e:MASK + e + 1],
                                             ident[:].rearrange("p (a e d) -> p e a d", e=2, d=HD)[:, e],
                                             AX.XY, ALU.add))
            link(nc.vector.tensor_scalar(cols[:, MASK:MASK + 2], cols[:, MASK:MASK + 2], float(HD) ** -0.5, None, ALU.mult))
            for m in range(KT):
                link(nc.vector.tensor_scalar(cols[:, QB + 2 * m:QB + 2 * m + 2], cols[:, MASK:MASK + 2],
                                             cols[:, BIN + m:BIN + m + 1], None, ALU.mult))
            dve.wait_ge(wload[4], 16)
            for m in range(FT):
                link(nc.vector.tensor_tensor_reduce(out=junk[:], in0=nw1[:, m, :], in1=lnb[:, 1, :], scale=1.0, scalar=0.0,
                                                    op0=ALU.mult, op1=ALU.add, accum_out=cols[:, B1S + m:B1S + m + 1]))
            link(nc.vector.tensor_tensor(cols[:, B1C:B1C + FT], cols[:, B1C:B1C + FT], cols[:, B1S:B1S + FT], ALU.add))
            assert chain[0] == BIASES
            n_act = 0
            for k, (what, i) in enumerate(SG[:-2]):
                dve.wait_ge(pe_setup, k + 1)
                n_act += {"wout": 2, "crow": 0}.get(what, 1)
                dve.wait_ge(a_setup, max(n_act, 1))
                bank = ps[:, k % 8, :]
                if what == "crow":
                    link(nc.vector.tensor_tensor(crow[:], ps[:, k % 8, 0:D], boutr[:], ALU.add), False)
                elif what == "wout":
                    link(nc.vector.tensor_tensor(wo[1][:].rearrange("p k d -> p (k d)"), bank,
                                                 wo[0][:].rearrange("p k d -> p (k d)"), ALU.subtract), False)
                elif what in ("qk", "vo"):
                    o = 0 if what == "qk" else 512
                    link(nc.vector.scalar_tensor_tensor(out=wa[1][:, i, o:o + 512], in0=bank, scalar=cols[:, G1 + i:G1 + i + 1],
                                                        in1=wa[0][:, i, o:o + 512], op0=ALU.mult, op1=ALU.subtract), False)
                elif what == "upM":
                    kt, o = i // 2, 512 * (i % 2)
                    link(nc.vector.scalar_tensor_tensor(out=wup["M"][1][:, kt, o:o + 512], in0=bank,
                                                        scalar=cols[:, G2 + kt:G2 + kt + 1], in1=wup["M"][0][:, kt, o:o + 512],
                                                        op0=ALU.mult, op1=ALU.subtract), False)
                elif what == "upF":
                    kt, o = i // 2, 512 * (i % 2)
                    link(nc.vector.tensor_tensor(wup["F"][1][:, kt, o:o + 512], bank, wup["F"][0][:, kt, o:o + 512],
                                                 ALU.subtract), False)
                elif what in ("dnM", "dnF"):
                    w = wdn[what[2]]
                    link(nc.vector.tensor_tensor(w[1][:, 2 * i:2 * i + 2, :].rearrange("p k d -> p (k d)"), bank,
                                                 w[0][:, 2 * i:2 * i + 2, :].rearrange("p k d -> p (k d)"), ALU.subtract), False)
                elif what == "ga":
                    link(nc.vector.tensor_tensor(
                        ga[:, :, E + ER:GW], ps[:, k % 8, 0:GW].rearrange("p (k n) -> p k n", k=KT),
                        ga[:, :, 0:E + ER], ALU.subtract), False)
            dve.wait_ge(wload[9], 16 * E)
            src = nlb[:].rearrange("p m e r -> p m (e r)")
            link(nc.vector.tensor_copy(lbs[:, :, 0:ER].bitcast(F32R), src))
            link(nc.vector.tensor_copy(lbs[:, :, ER:2 * ER], lbs[:, :, 0:ER]))
            link(nc.vector.tensor_tensor(lbs[:, :, 2 * ER:3 * ER].bitcast(F32R), src, lbs[:, :, 0:ER], ALU.subtract))
            link(nc.vector.tensor_copy(lbs[:, :, 3 * ER].bitcast(F32R), wibc[:]))
            link(nc.vector.tensor_tensor(lbs[:, :, 3 * ER + 1].bitcast(F32R), wibc[:], lbs[:, :, 3 * ER], ALU.subtract))
            assert chain[0] == D_SETUP, chain[0]

            with dve.Fori(0, B) as b:
                def ln_a(k, rows):
                    for i in range(CT):
                        nc.vector.bn_stats(stats[:, i, :], rows[:, i, :]).then_inc(stat_done, 1)
                    dve.wait_ge(stat_done, 1 + b * NLN * CT + CT * (k + 1))
                    dve.wait_ge(norm_done, 1 + b * NLN * CT + CT * k)
                    nc.vector.reg_add(aggregated, aggregated, CT)
                    for i in range(CT):
                        nc.vector.bn_aggr(mv[:, i, :], stats[:, i, :]).then_inc(aggr_done, 1)
                    dve.wait_ge(aggr_done, dve.snap(aggregated, min_val=CT + 1))
                    nc.vector.tensor_scalar(vare[:], mv[:, :, 1], EPS, None, ALU.add).then_inc(vare_done, 1)

                def ln_b(k, dst, rows):
                    dve.wait_ge(rstd_done, 1 + b * NLN + k + 1)
                    for i in range(CT):
                        nc.vector.tensor_scalar(dst[:, i, :], rows[:, i, :], mv[:, i, 0:1], rstd[:, i:i + 1],
                                                ALU.subtract, ALU.mult).then_inc(norm_done, 1)

                def row_max(u):
                    if u is None:
                        return
                    g, n = max_unit(u)[:2]
                    dve.wait_ge(maxmm_done, 1 + b * GROUPS * NMAX + u + 1)
                    if n == 0 and g >= 2:
                        dve.wait_ge(negm_done, 1 + b * GROUPS + g - 1)
                    nc.vector.tensor_reduce(mx[:, g % 2, n:n + 1], ps[:, max_bank(u), :], AX.X, ALU.max).then_inc(maxr_done, 1)
                    if n == NMAX - 1:
                        dve.wait_ge(maxr_done, 1 + b * GROUPS * NMAX + u + 1)
                        if g:
                            dve.wait_ge(negs_done, 1 + b * 2 * GROUPS + 2 * g)
                        nc.vector.tensor_reduce(negm[:], mx[:, g % 2, :].rearrange("p (k u) -> p u k", k=KQ), AX.X, ALU.max,
                                                negate=True).then_inc(negm_done, 1)
                        dve.wait_ge(negm_done, 1 + b * GROUPS + g + 1)
                        dve.wait_ge(mturn_done, 1 + b * GROUPS + g)
                        nc.vector.tensor_copy(negs[:, 0:UNITS].bitcast(F32R), negm[:]).then_inc(negs_done, 1)
                        dve.wait_ge(negs_done, 1 + b * 2 * GROUPS + 2 * g + 1)
                        nc.vector.tensor_tensor(negs[:, UNITS:].bitcast(F32R), negm[:], negs[:, 0:UNITS],
                                                ALU.subtract).then_inc(negs_done, 1)

                for c in range(NA):
                    for m in range(KT):
                        dve.wait_ge(kh_done, 1 + b * NA * KT + KT * (c + 1))
                        nc.vector.scalar_tensor_tensor(
                            out=kstage[c % 2][:, KT + m, :], in0=ps[:, c % 2, AW * m:AW * (m + 1)],
                            scalar=cols[:, BIN + KT + m:BIN + KT + m + 1], in1=kstage[c % 2][:, m, :],
                            op0=ALU.add, op1=ALU.subtract).then_inc(kl_done, 1)
                    row_max(early(c, 0))
                    if 1 <= c < NA - 1:
                        turned_low(b, c + 1)
                    if c and c + 2 < NA:
                        input_a(b, c + 2)
                    row_max(early(c, 1))
                    if c and c + 2 < NA:
                        input_b(b, c + 2)
                    row_max(early(c, 2))
                    if c:
                        if 1 < c and c + XB < NA:
                            dve.wait_ge(x1st[c - 1], 1 + b * 16 * X1S[c - 1] + 16)
                        dve.wait_ge(xc_done, 1 + b * (NA - 1) + c)
                        dve.wait_ge(vcp_done, 1 + b * NA + c + 1)
                        v0 = 2 + 2 * (c % 2)
                        nc.vector.tensor_tensor((x1o if c + XB < NA else xin[c % XB])[:], xin[c % XB][:], ps[:, v0:v0 + 2, D:2 * D],
                                                ALU.add).then_inc(x1_done, 1)
                    if c == 0:
                        dve.wait_ge(bstw, 16)
                        for m in range(KT):
                            dve.wait_ge(qf_done, 1 + b * 2 * KT + 2 * (m + 1))
                            nc.vector.tensor_copy(qstage[m][:, 0, :], qf[m][:].rearrange("p e q -> p (e q)")
                                                  ).then_inc(qh_done, 1)
                    row_max(early(c, 3))

                def out_raw(g):
                    dve.wait_ge(av_done, 1 + b * STEPS + NT * (g + 1))
                    dve.wait_ge(oturn_done, 1 + b * GROUPS + g)
                    nc.vector.tensor_copy(oraw[:], ps[:, 6, 0:QW]).then_inc(oraw_done, 1)

                def out_norm(g):
                    dve.wait_ge(oturn_done, 1 + b * GROUPS + g + 1)
                    if g:
                        dve.wait_ge(otok_done, 1 + b * GROUPS * NQ + NQ * g)
                    turned_o = ps[:, 7, 0:NQ * P].rearrange("p (t h v) -> p t h v", t=NQ, h=4)
                    nc.vector.reciprocal(rsum[:], turned_o[:, :, :, HD]).then_inc(rsum_done, 1)
                    dve.wait_ge(rsum_done, 1 + b * GROUPS + g + 1)
                    for t in range(NQ):
                        nc.vector.tensor_tensor(
                            otok[:, t, 4 * HD * g:4 * HD * (g + 1)].rearrange("p (h v) -> p h v", h=4),
                            turned_o[:, t, :, 0:HD], rsum[:, t, :, None].to_broadcast([P, 4, HD]),
                            ALU.mult).then_inc(otok_done, 1)

                def ffn_step(what, n):
                    if what == "ln2a":
                        dve.wait_ge(fld[n % 2], 1 + b * 64 + 32 * (n // 2 + 1))
                        ln_a(LN[("ln2", n)], x1in)
                    elif what == "ln2b":
                        dve.wait_ge(res_done, 1 + b * NT + CT * (n + 1))
                        ln_b(LN[("ln2", n)], x1in, x1in)
                    elif what == "onorm":
                        out_norm(GROUPS - 1)
                    elif what == "olow":
                        dve.wait_ge(oth_done, 1 + b + 1)
                        nc.vector.tensor_tensor(ot[1][:].rearrange("p k q -> p (k q)"), ps[:, 7, :],
                                                ot[0][:].rearrange("p k q -> p (k q)"), ALU.subtract).then_inc(otl_done, 1)
                    elif what == "oadd":
                        dve.wait_ge(oproj_done, 1 + b + 1)
                        dve.wait_ge(xgc_done, 1 + b + 1)
                        for t in range(NQ):
                            nc.vector.tensor_tensor(xg[:, t, :], xg[:, t, :], ps[:, 6, D * t:D * t + D],
                                                    ALU.add).then_inc(x1g_done, 1)
                    elif what == "nexta":
                        input_a(b + 1, n)
                    elif what == "nextb":
                        input_b(b + 1, n)
                    elif what == "nextt":
                        turned_low(b + 1, n)
                    elif what == "ln3a":
                        dve.wait_ge(sumy_done, 1 + b * 2 * NC + 2 * (n + 1))
                        ln_a(LN[("ln3", n)], srow[n % 2])
                    elif what == "ln3b":
                        ln_b(LN[("ln3", n)], srow[n % 2], srow[n % 2])
                    elif what == "ln4a":
                        dve.wait_ge(sumz_done, 1 + b * 2 * NC + 2 * (n + 1))
                        ln_a(LN[("ln4", n)], srow[n % 2])
                    elif what == "ln4b":
                        ln_b(LN[("ln4", n)], srow[n % 2], srow[n % 2])
                    elif what in ("t2", "t3"):
                        k = TURNS[(what, n)]
                        blk = BLOCK_OF[("M" if what == "t2" else "F", n)]
                        dve.wait_ge(turnh_done, 1 + b * 2 * NC + k + 1)
                        nc.vector.tensor_tensor(turned[blk % 2][1][:], ps[:, turn_banks(what, n), :], turned[blk % 2][0][:],
                                                ALU.subtract).then_inc(turnl_done, 1)
                    elif what == "sumy":
                        dve.wait_ge(down_done, 1 + b * ITEMS + 8 * (BLOCK_OF[("M", n)] + 1))
                        dve.wait_ge(resb_done, 1 + b * NT + CT * (n + 1))
                        if n >= 2:
                            dve.wait_ge(ost[n % 2], 1 + b * 32 + 16)
                        for h in range(2):
                            nc.vector.tensor_tensor(
                                srow[n % 2][:, 2 * h:2 * h + 2, :].rearrange("p t d -> p (t d)"),
                                xrow[n % 2][:, 2 * h:2 * h + 2, :].rearrange("p t d -> p (t d)"), ps[:, 2 + h, :],
                                ALU.add).then_inc(sumy_done, 1)
                    elif what == "sumz":
                        dve.wait_ge(down_done, 1 + b * ITEMS + 8 * (BLOCK_OF[("F", n)] + 1))
                        dve.wait_ge(x3w_done, 1 + b * NT + CT * (n + 1))
                        for h in range(2):
                            rows = srow[n % 2][:, 2 * h:2 * h + 2, :].rearrange("p t d -> p (t d)")
                            nc.vector.tensor_tensor(rows, rows, ps[:, 4 + h, :], ALU.add).then_inc(sumz_done, 1)
                    elif what == "gate":
                        dve.wait_ge(gate_done, 1 + b * NC + n + 1)
                        nc.vector.tensor_copy(gcopy[:].rearrange("p (a t) g -> p a t g", a=2),
                                              ps[:, 6:8, :].rearrange("p a (t g) -> p a t g", t=2)[:, :, :, 0:GW]
                                              ).then_inc(gatec_done, 1)
                        dve.wait_ge(gatec_done, 1 + b * NC + n + 1)
                        steps = [1 + b * NPICK * NC + NPICK * n]

                        def then(ins, steps=steps):
                            ins.then_inc(pick_done, 1)
                            steps[0] = steps[0] + 1
                            dve.wait_ge(pick_done, steps[0])

                        then(nc.vector.tensor_tensor(uall[:], gcopy[:, :, 0:E + ER], gcopy[:, :, E + ER:GW], ALU.add))
                        logits = uall[:, :, 0:E]
                        then(nc.vector.tensor_tensor(logits, logits, gateb[:, None, :].to_broadcast([P, CT, E]), ALU.add))
                        then(nc.vector.tensor_reduce(pickm[:], logits, AX.X, ALU.max))
                        top_of = pickm[:, :, None].to_broadcast([P, CT, E])
                        then(nc.vector.tensor_tensor(picke[:], logits, top_of, ALU.is_equal))
                        then(nc.vector.tensor_tensor(picke[:], picke[:], rank[:, None, :].to_broadcast([P, CT, E]), ALU.mult))
                        then(nc.vector.tensor_reduce(pickm[:], picke[:], AX.X, ALU.max))
                        then(nc.vector.tensor_tensor(picke[:], picke[:], top_of, ALU.is_equal))
                        u4 = uall[:, :, E:].rearrange("p t (e r) -> p t e r", r=R)
                        then(nc.vector.tensor_tensor(u4, u4, picke[:, :, :, None].to_broadcast([P, CT, E, R]), ALU.mult))
                        u2 = uall[:, :, E:]
                        if n:
                            dve.wait_ge(pickt_done, 1 + b * NC + n)
                        then(nc.vector.tensor_copy(us[:, :, 0:ER].bitcast(F32R), u2))
                        then(nc.vector.tensor_tensor(us[:, :, ER:2 * ER].bitcast(F32R), u2, us[:, :, 0:ER], ALU.subtract))
                        then(nc.vector.tensor_copy(us[:, :, 2 * ER:3 * ER], us[:, :, 0:ER]))
                        then(nc.vector.memset(us[:, :, 3 * ER:], 1.0))
                    elif what == "up":
                        if n >= RING:
                            dve.wait_ge(down_done, 1 + b * ITEMS + n - RING + 1)
                        if n in GELU:
                            k = GELU[n]
                            dve.wait_ge(gelu_done, 1 + b * NC * FT + k + 1)
                            nc.vector.tensor_copy(hid[n % RING][0][:], gel[k % 2][:]).then_inc(gh_done, 1)
                        else:
                            dve.wait_ge(rh_done, 1 + b * NC * FT + RELU[n] + 1)
                            nc.vector.scalar_tensor_tensor(out=hid[n % RING][1][:], in0=ps[:, n % 2, :], scalar=0.0,
                                                           in1=hid[n % RING][0][:], op0=ALU.max, op1=ALU.subtract
                                                           ).then_inc(rl_done, 1)

                for u in range(EARLY, LEAD):
                    row_max(u)
                u = LEAD
                for s in range(STEPS):
                    for _ in range(2):
                        if u < GROUPS * NMAX:
                            row_max(u)
                            u += 1
                    g, k = s // NT, s % NT
                    if g and k == OUT_TURN:
                        out_norm(g - 1)
                    if s == STEPS - NT + HEAD_LN:
                        ffn_step("ln2a", 0)
                        ffn_step("ln2b", 0)
                    if s == STEPS - NT + HEAD_TURN:
                        ffn_step("t2", 0)
                    if k == NT - 1:
                        out_raw(g)
                for step in FFN_STEPS[len(HEAD):]:
                    ffn_step(*step)

        @block.tensor
        def _(pe):
            mm = nc.tensor.matmul

            def three(o, l, r, start, stop, part=None):
                mm(o, l[0], r[0], start=start, stop=False, skip_group_check=True)
                mm(o, l[0], r[1], start=False, stop=False, skip_group_check=True)
                return mm(o, l[1], r[0], start=False, stop=stop, skip_group_check=True)

            for s in [ta_done, kmm_done, vmm_done, qmm_done, maxmm_done, mturn_done, score_done, av_done,
                      oturn_done, ott_done, oproj_done, turn_done, up_done, down_done, gate_done, pickt_done]:
                pe.sem_inc(s, 1)

            def turn_input(b, c):
                pe.wait_ge(anorm_done, 1 + b * NA * AT + AT * (c + 1))
                if c >= 2:
                    pe.wait_ge(tal_done, 1 + b * NA + c)
                for k in range(KT):
                    for i in range(AT):
                        last = nc.tensor.transpose(ps[:, input_bank(c), AW * k + P * i:AW * k + P * i + P],
                                                   xn[:, i, P * k:P * k + P], ident[:])
                last.then_inc(ta_done, 1)

            pe.wait_ge(p_ident, 2)
            for c in range(2):
                turn_input(0, c)
            n_a = n_d = 0
            freed = []
            for k, (what, i) in enumerate(SG):
                if k == input_bank(0):
                    pe.wait_ge(tal_done, 1 + 2)
                if k >= 8:
                    pe.wait_ge(a_setup, freed[k - 8][0])
                    pe.wait_ge(d_setup, BIASES + freed[k - 8][1])
                n_a += {"wout": 2, "crow": 0}.get(what, 1)
                n_d += what != "bst"
                freed.append((n_a, n_d))
                o = ps[:, k % 8, :]

                def turn(col, src, rows=P, n=P):
                    return nc.tensor.transpose(o[0:n, col:col + rows], src, ident[0:rows, 0:rows])

                if what == "wout":
                    pe.wait_ge(wload[1], 16)
                    for f in range(KT):
                        for m in range(KT):
                            last = turn(D * f + P * m, nwout[:, m, P * f:P * f + P])
                elif what == "qk":
                    pe.wait_ge(wload[0], 16)
                    for m in range(4):
                        last = turn(P * m, nwin[:, m, P * i:P * i + P])
                elif what == "vo":
                    pe.wait_ge(a_setup, 1)
                    for m in range(2):
                        turn(P * m, nwin[:, 4 + m, P * i:P * i + P])
                    for m in range(2):
                        last = mm(o[:, D:2 * D], nwin[:, 4 + m, P * i:P * i + P], wof[:, m, :], start=m == 0, stop=m == 1)
                elif what == "crow":
                    pe.wait_ge(d_setup, CVB)
                    for m in range(KT):
                        last = mm(o[:, 0:D], cvb[:, m, :], wof[:, m, :], start=m == 0, stop=m == 1)
                elif what in ("upM", "upF"):
                    pe.wait_ge(wload[4 if what == "upM" else 6], 16)
                    w = nw1 if what == "upM" else nwi
                    kt, half = i // 2, i % 2
                    for m in range(4):
                        last = turn(P * m, w[:, 4 * half + m, P * kt:P * kt + P])
                elif what in ("dnM", "dnF"):
                    pe.wait_ge(wload[5 if what == "dnM" else 7], 16)
                    w = nw2 if what == "dnM" else nwo
                    for f in range(2):
                        for m in range(2):
                            last = turn(D * f + P * m, w[:, m, P * (2 * i + f):P * (2 * i + f) + P])
                elif what == "ga":
                    pe.wait_ge(wload[8], 32)
                    for m in range(KT):
                        last = turn((E + ER) * m, nga[:, P * m:P * m + P], rows=E + ER)
                elif what == "bst":
                    pe.wait_ge(d_setup, D_SETUP)
                    for m in range(4):
                        last = turn(P * m, lbs[:, 4 * i + m, :], n=UROWS)
                last.then_inc(pe_setup, 1)
            pe.wait_ge(a_setup, A_SETUP)
            pe.wait_ge(d_setup, D_SETUP)

            with pe.Fori(0, B) as b:
                def score_max(u):
                    g, n, pair, e, t, piece = max_unit(u)
                    if n == 0 and g % 2 == 0:
                        pe.wait_ge(qcp[g // 2], 1 + b * 48 + 48)
                    if g == 0 and n % UNITS == 0:
                        pe.wait_ge(kcp[piece], 1 + b * KCP[piece] + KCP[piece])
                    if u == EARLY:
                        pe.wait_ge(x1_done, 1 + b * (NA - 1) + NA - 1)
                        pe.wait_ge(vcp_done, 1 + b * NA + NA)
                    elif 0 < u < EARLY:
                        pe.wait_ge(maxr_done, 1 + b * GROUPS * NMAX + u)
                    elif u >= EARLY + 2:
                        pe.wait_ge(maxr_done, 1 + b * GROUPS * NMAX + u - 1)
                    mm(ps[:, max_bank(u), :], qstack[0:SROWS, pair, e, P * t:P * t + P],
                       kstack[0:SROWS, pair, 512 * piece:512 * piece + 512], start=True, stop=True).then_inc(maxmm_done, 1)

                for c in range(NA):
                    t = xt[c % 2]
                    pe.wait_ge(tal_done, 1 + b * NA + c + 1)
                    if c >= 2:
                        pe.wait_ge(kl_done, 1 + b * NA * KT + KT * (c - 1))
                    elif c == 0:
                        pe.wait_ge(rl_done, 1 + b * NC * FT)
                    for m in range(KT):
                        for k in range(KT):
                            last = three(ps[:, c % 2, AW * m:AW * (m + 1)], [w[:, k, D + P * m:D + P * m + P] for w in wa],
                                         [h[:, k, :] for h in t], m == 0 and k == 0, k == KT - 1)
                    last.then_inc(kmm_done, 1)
                    if 1 <= c < NA - 1:
                        turn_input(b, c + 1)
                    if c == 0:
                        pe.wait_ge(sumz_done, 1 + b * 2 * NC)
                        for m in range(KT):
                            for k in range(KT):
                                last = three(ps[:, 4 + m, 0:QW], [w[:, k, P * m:P * m + P] for w in wa],
                                             [h[:, k, :] for h in t], k == 0, k == KT - 1)
                        last.then_inc(qmm_done, 1)
                    v0 = 2 + 2 * (c % 2)
                    if c >= 2:
                        pe.wait_ge(vcp_done, 1 + b * NA + c - 1)
                        pe.wait_ge(x1_done, 1 + b * (NA - 1) + c - 2)
                    elif c == 1:
                        pe.wait_ge(qf_done, 1 + b * 2 * KT + 2 * KT)
                    n = 2 * D if c else D
                    for i in range(AT):
                        if early(c, i) is not None:
                            score_max(early(c, i))
                        for k in range(KT):
                            last = three(ps[:, v0 + i, 0:n], [h[:, k, P * i:P * i + P] for h in t],
                                         [w[:, k, 2 * D:2 * D + n] for w in wa], k == 0, k == KT - 1)
                    last.then_inc(vmm_done, 1)
                    if early(c, 2) is not None:
                        score_max(early(c, 2))
                    if early(c, 3) is not None:
                        score_max(early(c, 3))

                def turn_max(g):
                    pe.wait_ge(negs_done, 1 + b * 2 * GROUPS + 2 * g + 2)
                    if g >= 2:
                        pe.wait_ge(otok_done, 1 + b * GROUPS * NQ + NQ * (g - 1))
                    nc.tensor.transpose(ps[0:2 * UNITS, 7, 0:P], negs[:], ident[:]).then_inc(mturn_done, 1)

                def scores(s):
                    g, k = s // NT, s % NT
                    if k == 0:
                        pe.wait_ge(mcp, 1 + b * 32 * GROUPS + 32 * (g + 1))
                    if s >= 2:
                        pe.wait_ge(exp_done, 1 + b * STEPS + s - 1)
                    for i in range(GP):
                        last = mm(ps[:, 2 * (s % 2) + i, :], kstack[:, GP * g + i, P * k:P * k + P],
                                  qstack[:, GP * g + i, :, :].rearrange("p e q -> p (e q)"), start=True, stop=True)
                    last.then_inc(score_done, 1)

                def attend(s, heads):
                    g, k = s // NT, s % NT
                    pe.wait_ge(exp_done, 1 + b * STEPS + s + 1)
                    if k == 0 and g and heads[0] == 0:
                        pe.wait_ge(oraw_done, 1 + b * GROUPS + g)
                    for h in heads:
                        v = (k * H + 4 * g + h) * VW
                        last = mm(ps[32 * h:32 * h + 32, 6, 0:QW], vals[:, v:v + 32], prob[s % 2][:, h, :],
                                  start=k == 0, stop=k == NT - 1)
                    if heads[-1] == 3:
                        last.then_inc(av_done, 1)

                def turn_out(g):
                    pe.wait_ge(oraw_done, 1 + b * GROUPS + g + 1)
                    pe.wait_ge(mt_done, 1 + b * GROUPS + min(g + 2, GROUPS) if g + 1 < GROUPS else b * GROUPS + GROUPS)
                    for t in range(NQ):
                        last = nc.tensor.transpose(ps[:, 7, P * t:P * t + P], oraw[:, P * t:P * t + P], ident[:])
                    last.then_inc(oturn_done, 1)

                def spare_free(step):
                    k = SPARE[step]
                    if k == 0:
                        pe.wait_ge(oraw_done, 1 + b * GROUPS + GROUPS)
                        pe.wait_ge(otok_done, 1 + b * GROUPS * NQ + NQ * (GROUPS - 1))
                        return
                    (what, n), = [s for s, i in SPARE.items() if i == k - 1]
                    if what in ("t2", "t3"):
                        pe.wait_ge(turnl_done, 1 + b * 2 * NC + TURNS[(what, n)] + 1)
                    elif what == "gate":
                        pe.wait_ge(gatec_done, 1 + b * NC + n + 1)
                    elif what == "oturn":
                        pe.wait_ge(otok_done, 1 + b * GROUPS * NQ + NQ * GROUPS)
                    elif what == "oproj":
                        pe.wait_ge(x1g_done, 1 + b * NQ + NQ)
                    else:
                        pe.wait_ge(ust_done, 1 + b * NC + n + 1)

                def ffn_step(what, n):
                    if what in ("t2", "t3"):
                        if (what, n) not in HEAD:
                            spare_free((what, n))
                        else:
                            pe.wait_ge(maxr_done, 1 + b * GROUPS * NMAX + GROUPS * NMAX)
                        pe.wait_ge(norm_done, 1 + b * NLN * CT + CT * (LN[("ln2" if what == "t2" else "ln3", n)] + 1))
                        rows = x1in if what == "t2" else srow[n % 2]
                        for k in range(KT):
                            for i in range(CT):
                                last = nc.tensor.transpose(ps[:, turn_banks(what, n).start + k, P * i:P * i + P], rows[:, i, P * k:P * k + P], ident[:])
                        last.then_inc(turn_done, 1)
                    elif what == "nextt":
                        if n == 0:
                            pe.wait_ge(ust_done, 1 + b * NC + NC)
                        turn_input(b + 1, n)
                    elif what == "oturn":
                        spare_free((what, n))
                        turn_out(GROUPS - 1)
                    elif what == "oturned":
                        pe.wait_ge(otok_done, 1 + b * GROUPS * NQ + GROUPS * NQ)
                        for k in range(KT):
                            for t in range(NQ):
                                last = nc.tensor.transpose(ps[:, 7, QW * k + P * t:QW * k + P * t + P],
                                                           otok[:, t, P * k:P * k + P], ident[:])
                        last.then_inc(ott_done, 1)
                    elif what == "oproj":
                        spare_free((what, n))
                        pe.wait_ge(oth_done, 1 + b + 1)
                        pe.wait_ge(otl_done, 1 + b + 1)
                        for t in range(NQ):
                            for k in range(KT):
                                last = three(ps[:, 6, D * t:D * t + D], [o[:, k, P * t:P * t + P] for o in ot],
                                             [w[:, k, :] for w in wo], t == 0 and k == 0, k == KT - 1)
                        last.then_inc(oproj_done, 1)
                    elif what == "gate":
                        spare_free((what, n))
                        t = turned[BLOCK_OF[("F", n)] % 2]
                        for i in range(CT):
                            for k in range(KT):
                                for h in range(2):
                                    last = mm(ps[:, 6 + i // 2, 256 * (i % 2):256 * (i % 2) + GW],
                                              t[h][:, k, P * i:P * i + P], ga[:, k, :],
                                              start=i % 2 == 0 and k == 0 and h == 0, stop=k == KT - 1 and h == 1,
                                              skip_group_check=True)
                        last.then_inc(gate_done, 1)
                    elif what == "pick":
                        spare_free((what, n))
                        pe.wait_ge(pick_done, 1 + b * NPICK * NC + NPICK * (n + 1))
                        for i in range(CT):
                            last = nc.tensor.transpose(ps[0:UROWS, 6, P * i:P * i + P], us[:, i, :], ident[:])
                        last.then_inc(pickt_done, 1)
                    elif what == "up":
                        blk, f = n // FT, n % FT
                        w, ch = BLOCKS[blk]
                        if f == 0:
                            k = TURNS[("t2" if w == "M" else "t3", ch)]
                            pe.wait_ge(turnh_done, 1 + b * 2 * NC + k + 1)
                            pe.wait_ge(turnl_done, 1 + b * 2 * NC + k + 1)
                        if n >= 2:
                            if n - 2 in GELU:
                                pe.wait_ge(gelu_done, 1 + b * NC * FT + GELU[n - 2] + 1)
                            else:
                                pe.wait_ge(rl_done, 1 + b * NC * FT + RELU[n - 2] + 1)
                        for k in range(KT):
                            last = three(ps[:, n % 2, :], [t[:, k, P * f:P * f + P] for t in wup[w]],
                                         [t[:, k, :] for t in turned[blk % 2]], k == 0, w == "M" and k == KT - 1)
                        if w == "F":
                            if f == 0:
                                pe.wait_ge(ust_done, 1 + b * NC + ch + 1)
                                pe.wait_ge(bstl, 1 + b * 16 + 16)
                            last = mm(ps[:, n % 2, :], bst[:, P * f:P * f + P], ust[:], start=False, stop=True,
                                      skip_group_check=True)
                        last.then_inc(up_done, 1)
                    elif what == "down":
                        blk, f = n // FT, n % FT
                        w, ch = BLOCKS[blk]
                        if n in GELU:
                            pe.wait_ge(gl_done, 1 + b * NC * FT + GELU[n] + 1)
                        else:
                            pe.wait_ge(rl_done, 1 + b * NC * FT + RELU[n] + 1)
                        if f == 0 and ch:
                            pe.wait_ge(sumy_done if w == "M" else sumz_done, 1 + b * 2 * NC + 2 * ch)
                        for i in range(CT):
                            bank = (2 if w == "M" else 4) + i // 2
                            last = three(ps[:, bank, D * (i % 2):D * (i % 2) + D],
                                         [t[:, P * i:P * i + P] for t in hid[n % RING]],
                                         [t[:, f, :] for t in wdn[w]], f == 0 and i % 2 == 0, f == FT - 1)
                        last.then_inc(down_done, 1)

                for u in range(EARLY, NMAX):
                    score_max(u)
                turn_max(0)
                for u in range(NMAX, LEAD):
                    score_max(u)
                pe.wait_ge(ones_done, 1 + b * 3 + 3)
                scores(0)
                scores(1)
                u = LEAD
                for s in range(STEPS):
                    g, k = s // NT, s % NT
                    if k == TURN_MAX and g + 1 < GROUPS:
                        turn_max(g + 1)
                    if g and k == OUT_TURN:
                        turn_out(g - 1)
                    if s == STEPS - NT + HEAD_TURN:
                        ffn_step("t2", 0)
                    if u < GROUPS * NMAX:
                        score_max(u)
                        u += 1
                    attend(s, range(4))
                    if u < GROUPS * NMAX:
                        score_max(u)
                        u += 1
                    if s + 2 < STEPS:
                        scores(s + 2)

                for step in FFN_STEPS[len(HEAD):]:
                    ffn_step(*step)



XLD = [len(range(i, NA, XB)) for i in range(XB)]
KCP = [96] * KQ
X1S = [XLD[0] - 1] + XLD[1:]
TURN_MAX = 12
OUT_TURN = 3
NPICK = 12
CVB = 9
BIASES = CVB + 5 + 9
D_SETUP = BIASES + 23 + 5
A_SETUP = 25


_INS = ["L0_attn_x", "L0_attn_w_in", "L0_attn_b_in", "L0_attn_w_out", "L0_attn_b_out", "L0_attn_w1", "L0_attn_b1",
        "L0_attn_w2", "L0_attn_b2", "L0_attn_ln1_g", "L0_attn_ln1_b", "L0_attn_ln2_g", "L0_attn_ln2_b",
        "L0_ffn_gate_W", "L0_ffn_gate_b", "L0_ffn_wi_W", "L0_ffn_wi_b", "L0_ffn_wo_W", "L0_ffn_wo_b",
        "L0_ffn_lora_A", "L0_ffn_lora_B"]


def kernel(**inputs):
    import numpy as _np
    import concourse.bacc as _bacc
    from concourse.bass_utils import run_bass_kernel_spmd as _run

    nc = _bacc.Bacc("TRN2", target_bir_lowering=False, num_devices=1)
    arrays, args = {}, []
    for name in _INS:
        a = _np.ascontiguousarray(inputs[name])
        arrays[f"in_{name}"] = a
        args.append(nc.dram_tensor(f"in_{name}", a.shape, mybir.dt.from_np(a.dtype), kind="ExternalInput").ap())
    args.append(nc.dram_tensor("out_0", (B, T, D), F32, kind="ExternalOutput").ap())
    attention_ffn_kernel(nc, *args)
    r = _run(nc, [arrays], core_ids=[0])
    return r.results[0]["out_0"]
```
